# Optimizing a Trainium2 kernel written in Bass

```python
import numpy as np
import jax
import jax.numpy as jnp

def _softmax(x, axis=-1):
    return jax.nn.softmax(x, axis=axis)

def _gelu(x):
    return jax.nn.gelu(x, approximate=True)

def _silu(x):
    return jax.nn.silu(x)

def _sigmoid(x):
    return jax.nn.sigmoid(x)

def _layernorm(x, axis=-1, eps=1e-05):
    m = jnp.mean(x, axis=axis, keepdims=True)
    v = jnp.var(x, axis=axis, keepdims=True)
    return (x - m) / jnp.sqrt(v + eps)

def _scatter_add(tgt, idx, src, axis=0):
    return tgt.at[idx].add(src)

def _segment_sum(src, seg, n):
    return jax.ops.segment_sum(src, seg, n)
kernel_name = 'mk_perceiver_d2_seqx_r4_46788a'

def setup_inputs(seed: int=0):
    np.random.seed(seed)
    _w = jnp.asarray

    def _rec_inputs():
        import jax
        import jax.numpy as jnp
        _rk = jax.random.key(seed)
        x = -0.0005207 + 1.001 * jax.random.normal(jax.random.fold_in(_rk, 1), (1, 256, 1024), jnp.float32)
        _lenS = 256 - jax.random.randint(jax.random.fold_in(_rk, 7), (1,), 0, max(1, 256 // 4) + 1, jnp.int32)
        _lenS2 = 4096 - jax.random.randint(jax.random.fold_in(_rk, 8), (1,), 0, max(1, 4096 // 4) + 1, jnp.int32)
        _ctx_4096P = jax.random.normal(jax.random.fold_in(_rk, 11), (1, 16, 1024), jnp.float32)
        _ctx_4096c = jax.random.dirichlet(jax.random.fold_in(_rk, 511), 0.3 * jnp.ones((16,), jnp.float32), (1, 4096))
        _ctx_4096t = jnp.einsum('bsk,bkd->bsd', _ctx_4096c, _ctx_4096P)
        _ctx_4096t = _ctx_4096t * jax.lax.rsqrt(jnp.mean(jnp.square(_ctx_4096t)) + 1e-12) * 0.953939
        ctx_4096 = -0.00010331 + 0.999899 * (_ctx_4096t + 0.3 * jax.random.normal(jax.random.fold_in(_rk, 611), (1, 4096, 1024), jnp.float32))
        return (x, ctx_4096)
    x, ctx_4096 = _rec_inputs()

    def _L0_xattn_setup():
        import jax, jax.numpy as jnp
        import numpy as np
        B, Q, D = (8, 64, 1024)
        CTX = 1024
        H, KV, HD = (16, 4, 96)
        G = H // KV
        key = jax.random.key(seed)
        ks = jax.random.split(key, 6)
        s = 0.02
        return {'latents': jax.random.normal(ks[0], (B, Q, D), jnp.float32), 'context': jax.random.normal(ks[1], (B, CTX, D), jnp.float32), 'Wq': jax.random.normal(ks[2], (H * HD, D), jnp.float32) * s, 'Wk': jax.random.normal(ks[3], (KV * HD, D), jnp.float32) * s, 'Wv': jax.random.normal(ks[4], (KV * HD, D), jnp.float32) * s, 'Wo': jax.random.normal(ks[5], (D, H * HD), jnp.float32) * s}
    _L0_xattn_all = _L0_xattn_setup()
    _L0_xattn_in = {k: v for k, v in _L0_xattn_all.items() if k in ('Wq', 'Wk', 'Wv', 'Wo')}
    del _L0_xattn_all

    def _L0_attn_setup():
        import jax, jax.numpy as jnp
        import numpy as np
        B, SEQ, EMBED, HEADS = (1, 1024, 1024, 16)
        HEAD_DIM = EMBED // HEADS
        ROT = 64
        MASKED_BIAS = -1000000000.0

        def _rotate_every_two(x):
            x1 = x[..., ::2]
            x2 = x[..., 1::2]
            return jnp.stack((-x2, x1), axis=-1).reshape(x.shape)

        def _apply_rope(x, sin, cos):
            sin = jnp.repeat(sin, 2, axis=-1)[None, :, None, :]
            cos = jnp.repeat(cos, 2, axis=-1)[None, :, None, :]
            return x * cos + _rotate_every_two(x) * sin
        key = jax.random.key(seed)
        ks = jax.random.split(key, 5)
        s = 0.02
        return {'hidden_states': jax.random.normal(ks[0], (B, SEQ, EMBED), jnp.float32), 'w_q': jax.random.normal(ks[1], (EMBED, EMBED), jnp.float32) * s, 'w_k': jax.random.normal(ks[2], (EMBED, EMBED), jnp.float32) * s, 'w_v': jax.random.normal(ks[3], (EMBED, EMBED), jnp.float32) * s, 'w_out': jax.random.normal(ks[4], (EMBED, EMBED), jnp.float32) * s}
    _L0_attn_all = _L0_attn_setup()
    _L0_attn_in = {k: v for k, v in _L0_attn_all.items() if k in ('w_q', 'w_k', 'w_v', 'w_out')}
    del _L0_attn_all

    def _L0_ffn_setup():
        import jax, jax.numpy as jnp
        import numpy as np
        R = 16
        LORA_ALPHA = 16
        SCALING = LORA_ALPHA / R
        key = jax.random.key(seed)
        kx, kr, ka = jax.random.split(key, 3)
        B, S, D, DO, E = (4, 512, 1024, 1024, 8)
        x = jax.random.normal(kx, (B, S, D), dtype=jnp.float32)
        bound_r = 1.0 / np.sqrt(D)
        route_w = jax.random.uniform(kr, (E, D), jnp.float32, -bound_r, bound_r)
        bound_a = 1.0 / np.sqrt(D)
        A = jax.random.uniform(ka, (E, R, D), jnp.float32, -bound_a, bound_a)
        kb = jax.random.fold_in(key, 7)
        Bw = jax.random.normal(kb, (E, DO, R), dtype=jnp.float32) * 0.02
        return {'x': x, 'route_w': route_w, 'A': A, 'Bw': Bw}
    _L0_ffn_all = _L0_ffn_setup()
    _L0_ffn_in = {k: v for k, v in _L0_ffn_all.items() if k in ('route_w', 'A', 'Bw')}
    del _L0_ffn_all

    def _L1_xattn_setup():
        import jax, jax.numpy as jnp
        import numpy as np
        DIM = 1024
        NUM_HEADS = 32
        NUM_KV_HEADS = 8
        HEAD_DIM = DIM // NUM_HEADS
        KV_DIM = DIM // (NUM_HEADS // NUM_KV_HEADS)
        B, S = (1, 512)
        key = jax.random.key(seed)
        ks = jax.random.split(key, 7)
        w_scale = DIM ** (-0.5)
        return {'query': jax.random.normal(ks[0], (B, S, DIM), jnp.float32), 'key': jax.random.normal(ks[1], (B, S, DIM), jnp.float32), 'value': jax.random.normal(ks[2], (B, S, DIM), jnp.float32), 'Wq': jax.random.normal(ks[3], (DIM, DIM), jnp.float32) * w_scale, 'Wk': jax.random.normal(ks[4], (DIM, KV_DIM), jnp.float32) * w_scale, 'Wv': jax.random.normal(ks[5], (DIM, KV_DIM), jnp.float32) * w_scale, 'Wo': jax.random.normal(ks[6], (DIM, DIM), jnp.float32) * w_scale}
    _L1_xattn_all = _L1_xattn_setup()
    _L1_xattn_in = {k: v for k, v in _L1_xattn_all.items() if k in ('Wq', 'Wk', 'Wv', 'Wo')}
    del _L1_xattn_all

    def _L1_attn_setup():
        import jax, jax.numpy as jnp
        import numpy as np
        B, S, D_IN = (2, 512, 1024)
        D_OUT, N_HEADS, N_KV = (1024, 32, 8)
        HEAD_DIM = D_OUT // N_HEADS
        GROUP = N_HEADS // N_KV
        CTX = 1024
        ROPE_BASE = 10000.0

        def precompute_rope(head_dim, theta_base, context_length):
            inv_freq = 1.0 / theta_base ** (jnp.arange(0, head_dim, 2, dtype=jnp.float32) / head_dim)
            pos = jnp.arange(context_length, dtype=jnp.float32)
            angles = pos[:, None] * inv_freq[None, :]
            angles = jnp.concatenate([angles, angles], axis=1)
            return (jnp.cos(angles), jnp.sin(angles))

        def compute_rope(x, cos, sin):
            s, hd = (x.shape[2], x.shape[3])
            x1, x2 = (x[..., :hd // 2], x[..., hd // 2:])
            rotated = jnp.concatenate([-x2, x1], axis=-1)
            c = cos[:s][None, None]
            si = sin[:s][None, None]
            return x * c + rotated * si
        key = jax.random.key(seed)
        kx, kq, kk, kv, ko = jax.random.split(key, 5)
        scale = 0.02
        x = jax.random.normal(kx, (B, S, D_IN), dtype=jnp.float32)
        Wq = jax.random.normal(kq, (D_IN, D_OUT), dtype=jnp.float32) * scale
        Wk = jax.random.normal(kk, (D_IN, N_KV * HEAD_DIM), dtype=jnp.float32) * scale
        Wv = jax.random.normal(kv, (D_IN, N_KV * HEAD_DIM), dtype=jnp.float32) * scale
        Wo = jax.random.normal(ko, (D_OUT, D_OUT), dtype=jnp.float32) * scale
        cos, sin = precompute_rope(HEAD_DIM, ROPE_BASE, CTX)
        return {'x': x, 'Wq': Wq, 'Wk': Wk, 'Wv': Wv, 'Wo': Wo, 'cos': cos, 'sin': sin}
    _L1_attn_all = _L1_attn_setup()
    _L1_attn_in = {k: v for k, v in _L1_attn_all.items() if k in ('Wq', 'Wk', 'Wv', 'Wo', 'cos', 'sin')}
    del _L1_attn_all

    def _L1_ffn_setup():
        import jax, jax.numpy as jnp
        import numpy as np
        EPS = 1e-06
        QMAX = 127.0

        def _quant_act(x):
            s = jnp.max(jnp.abs(x), axis=-1, keepdims=True) / QMAX
            s = jnp.maximum(s, 1e-08)
            q = jnp.clip(jnp.round(x / s), -QMAX, QMAX)
            return (q, s)

        def _quant_w(W):
            ws = jnp.max(jnp.abs(W), axis=1, keepdims=True) / QMAX
            ws = jnp.maximum(ws, 1e-08)
            Wq = jnp.clip(jnp.round(W / ws), -QMAX, QMAX)
            return (Wq, ws)
        key = jax.random.key(seed)
        k1, k2, k3, k4, k5 = jax.random.split(key, 5)
        B, S, D, I = (4, 512, 1024, 2752)
        return {'hidden_states': jax.random.normal(k1, (B, S, D), dtype=jnp.float32), 'rmsnorm_weight': jax.random.uniform(k2, (D,), dtype=jnp.float32), 'Wg': jax.random.normal(k3, (I, D), dtype=jnp.float32) * 0.02, 'Wu': jax.random.normal(k4, (I, D), dtype=jnp.float32) * 0.02, 'Wd': jax.random.normal(k5, (D, I), dtype=jnp.float32) * 0.02}
    _L1_ffn_all = _L1_ffn_setup()
    _L1_ffn_in = {k: v for k, v in _L1_ffn_all.items() if k in ('rmsnorm_weight', 'Wg', 'Wu', 'Wd')}
    del _L1_ffn_all
    return {'x': x, 'ctx_4096': ctx_4096, 'L0_xattn_Wq': _L0_xattn_in['Wq'], 'L0_xattn_Wk': _L0_xattn_in['Wk'], 'L0_xattn_Wv': _L0_xattn_in['Wv'], 'L0_xattn_Wo': _L0_xattn_in['Wo'], 'L0_attn_w_q': _L0_attn_in['w_q'], 'L0_attn_w_k': _L0_attn_in['w_k'], 'L0_attn_w_v': _L0_attn_in['w_v'], 'L0_attn_w_out': _L0_attn_in['w_out'], 'L0_ffn_route_w': _L0_ffn_in['route_w'], 'L0_ffn_A': _L0_ffn_in['A'], 'L0_ffn_Bw': _L0_ffn_in['Bw'], 'L1_xattn_Wq': _L1_xattn_in['Wq'], 'L1_xattn_Wk': _L1_xattn_in['Wk'], 'L1_xattn_Wv': _L1_xattn_in['Wv'], 'L1_xattn_Wo': _L1_xattn_in['Wo'], 'L1_attn_Wq': _L1_attn_in['Wq'], 'L1_attn_Wk': _L1_attn_in['Wk'], 'L1_attn_Wv': _L1_attn_in['Wv'], 'L1_attn_Wo': _L1_attn_in['Wo'], 'L1_attn_cos': _L1_attn_in['cos'], 'L1_attn_sin': _L1_attn_in['sin'], 'L1_ffn_rmsnorm_weight': _L1_ffn_in['rmsnorm_weight'], 'L1_ffn_Wg': _L1_ffn_in['Wg'], 'L1_ffn_Wu': _L1_ffn_in['Wu'], 'L1_ffn_Wd': _L1_ffn_in['Wd']}

def reference(x, ctx_4096, L0_xattn_Wq, L0_xattn_Wk, L0_xattn_Wv, L0_xattn_Wo, L0_attn_w_q, L0_attn_w_k, L0_attn_w_v, L0_attn_w_out, L0_ffn_route_w, L0_ffn_A, L0_ffn_Bw, L1_xattn_Wq, L1_xattn_Wk, L1_xattn_Wv, L1_xattn_Wo, L1_attn_Wq, L1_attn_Wk, L1_attn_Wv, L1_attn_Wo, L1_attn_cos, L1_attn_sin, L1_ffn_rmsnorm_weight, L1_ffn_Wg, L1_ffn_Wu, L1_ffn_Wd):
    import jax
    import jax.numpy as jnp

    def _L0_xattn_ref(latents, context, Wq, Wk, Wv, Wo):
        import jax, jax.numpy as jnp
        import numpy as np
        B, Q, D = (8, 64, 1024)
        CTX = 1024
        H, KV, HD = (16, 4, 96)
        G = H // KV
        b, q_len, _ = latents.shape
        hidden = jnp.concatenate([context, latents], axis=1)
        s_len = hidden.shape[1]
        q = (latents @ Wq.T).reshape(b, q_len, H, HD)
        k = (hidden @ Wk.T).reshape(b, s_len, KV, HD)
        v = (hidden @ Wv.T).reshape(b, s_len, KV, HD)
        q = q.transpose(0, 2, 1, 3).reshape(b, KV, G, q_len, HD)
        k = k.transpose(0, 2, 1, 3)
        v = v.transpose(0, 2, 1, 3)
        scale = 1.0 / jnp.sqrt(jnp.asarray(HD, q.dtype))
        scores = jnp.einsum('bkgqd,bksd->bkgqs', q, k) * scale
        attn = jax.nn.softmax(scores.astype(jnp.float32), axis=-1).astype(q.dtype)
        out = jnp.einsum('bkgqs,bksd->bkgqd', attn, v)
        out = out.reshape(b, H, q_len, HD).transpose(0, 2, 1, 3).reshape(b, q_len, H * HD)
        return out @ Wo.T

    def _L0_attn_ref(hidden_states, w_q, w_k, w_v, w_out):
        import jax, jax.numpy as jnp
        import numpy as np
        B, SEQ, EMBED, HEADS = (1, 1024, 1024, 16)
        HEAD_DIM = EMBED // HEADS
        ROT = 64
        MASKED_BIAS = -1000000000.0

        def _rotate_every_two(x):
            x1 = x[..., ::2]
            x2 = x[..., 1::2]
            return jnp.stack((-x2, x1), axis=-1).reshape(x.shape)

        def _apply_rope(x, sin, cos):
            sin = jnp.repeat(sin, 2, axis=-1)[None, :, None, :]
            cos = jnp.repeat(cos, 2, axis=-1)[None, :, None, :]
            return x * cos + _rotate_every_two(x) * sin
        Bt, S, E = hidden_states.shape
        q = (hidden_states @ w_q.T).reshape(Bt, S, HEADS, HEAD_DIM)
        k = (hidden_states @ w_k.T).reshape(Bt, S, HEADS, HEAD_DIM)
        v = (hidden_states @ w_v.T).reshape(Bt, S, HEADS, HEAD_DIM)
        inv_freq = 1.0 / 10000.0 ** (jnp.arange(0, ROT, 2, dtype=jnp.float32) / ROT)
        sinusoid = jnp.arange(S, dtype=jnp.float32)[:, None] * inv_freq[None, :]
        sin, cos = (jnp.sin(sinusoid), jnp.cos(sinusoid))
        q = jnp.concatenate([_apply_rope(q[..., :ROT], sin, cos), q[..., ROT:]], axis=-1)
        k = jnp.concatenate([_apply_rope(k[..., :ROT], sin, cos), k[..., ROT:]], axis=-1)
        q = q.transpose(0, 2, 1, 3).astype(jnp.float32)
        k = k.transpose(0, 2, 1, 3).astype(jnp.float32)
        v = v.transpose(0, 2, 1, 3)
        scores = jnp.einsum('bhqd,bhkd->bhqk', q, k)
        causal = jnp.tril(jnp.ones((S, S), dtype=bool))[None, None]
        scores = jnp.where(causal, scores, MASKED_BIAS)
        scores = scores / jnp.sqrt(jnp.float32(HEAD_DIM))
        attn = jax.nn.softmax(scores, axis=-1).astype(v.dtype)
        out = jnp.einsum('bhqk,bhkd->bhqd', attn, v)
        out = out.transpose(0, 2, 1, 3).reshape(Bt, S, E)
        return out @ w_out.T

    def _L0_ffn_ref(x, route_w, A, Bw):
        import jax, jax.numpy as jnp
        import numpy as np
        R = 16
        LORA_ALPHA = 16
        SCALING = LORA_ALPHA / R
        logits = jnp.einsum('bsd,ed->bse', x, route_w)
        topk_v, topk_idx = jax.lax.top_k(logits, 1)
        E = logits.shape[-1]
        route_weight = jax.nn.one_hot(topk_idx[..., 0], E, dtype=logits.dtype) * topk_v
        h = jnp.einsum('bsd,erd->bser', x, A)
        wh = route_weight[..., None] * h
        out = jnp.einsum('bser,eor->bso', wh, Bw) * SCALING
        return out

    def _L1_xattn_ref(query, key, value, Wq, Wk, Wv, Wo):
        import jax, jax.numpy as jnp
        import numpy as np
        DIM = 1024
        NUM_HEADS = 32
        NUM_KV_HEADS = 8
        HEAD_DIM = DIM // NUM_HEADS
        KV_DIM = DIM // (NUM_HEADS // NUM_KV_HEADS)
        B, S = (1, 512)
        b, sq, _ = query.shape
        _, sk, _ = key.shape
        rep = NUM_HEADS // NUM_KV_HEADS
        q = (query @ Wq).reshape(b, sq, NUM_HEADS, HEAD_DIM).transpose(0, 2, 1, 3)
        k = (key @ Wk).reshape(b, sk, NUM_KV_HEADS, HEAD_DIM).transpose(0, 2, 1, 3)
        v = (value @ Wv).reshape(b, sk, NUM_KV_HEADS, HEAD_DIM).transpose(0, 2, 1, 3)
        k = jnp.repeat(k, rep, axis=1)
        v = jnp.repeat(v, rep, axis=1)
        scale = HEAD_DIM ** (-0.5)
        scores = jnp.einsum('bhqd,bhkd->bhqk', q, k) * scale
        probs = jax.nn.softmax(scores, axis=-1)
        out = jnp.einsum('bhqk,bhkd->bhqd', probs, v)
        out = out.transpose(0, 2, 1, 3).reshape(b, sq, DIM)
        return out @ Wo

    def _L1_attn_ref(x, Wq, Wk, Wv, Wo, cos, sin):
        import jax, jax.numpy as jnp
        import numpy as np
        B, S, D_IN = (2, 512, 1024)
        D_OUT, N_HEADS, N_KV = (1024, 32, 8)
        HEAD_DIM = D_OUT // N_HEADS
        GROUP = N_HEADS // N_KV
        CTX = 1024
        ROPE_BASE = 10000.0

        def precompute_rope(head_dim, theta_base, context_length):
            inv_freq = 1.0 / theta_base ** (jnp.arange(0, head_dim, 2, dtype=jnp.float32) / head_dim)
            pos = jnp.arange(context_length, dtype=jnp.float32)
            angles = pos[:, None] * inv_freq[None, :]
            angles = jnp.concatenate([angles, angles], axis=1)
            return (jnp.cos(angles), jnp.sin(angles))

        def compute_rope(x, cos, sin):
            s, hd = (x.shape[2], x.shape[3])
            x1, x2 = (x[..., :hd // 2], x[..., hd // 2:])
            rotated = jnp.concatenate([-x2, x1], axis=-1)
            c = cos[:s][None, None]
            si = sin[:s][None, None]
            return x * c + rotated * si
        b, s, _ = x.shape
        q = (x @ Wq).reshape(b, s, N_HEADS, HEAD_DIM).transpose(0, 2, 1, 3)
        k = (x @ Wk).reshape(b, s, N_KV, HEAD_DIM).transpose(0, 2, 1, 3)
        v = (x @ Wv).reshape(b, s, N_KV, HEAD_DIM).transpose(0, 2, 1, 3)
        q = compute_rope(q, cos, sin)
        k = compute_rope(k, cos, sin)
        k = jnp.repeat(k, GROUP, axis=1)
        v = jnp.repeat(v, GROUP, axis=1)
        scores = jnp.einsum('bhqd,bhkd->bhqk', q, k) / jnp.sqrt(jnp.float32(HEAD_DIM))
        causal = jnp.tril(jnp.ones((s, s), dtype=bool))
        scores = jnp.where(causal[None, None], scores, -jnp.inf)
        weights = jax.nn.softmax(scores, axis=-1)
        ctx = jnp.einsum('bhqk,bhkd->bhqd', weights, v)
        ctx = ctx.transpose(0, 2, 1, 3).reshape(b, s, D_OUT)
        return ctx @ Wo

    def _L1_ffn_ref(hidden_states, rmsnorm_weight, Wg, Wu, Wd):
        import jax, jax.numpy as jnp
        import numpy as np
        EPS = 1e-06
        QMAX = 127.0

        def _quant_act(x):
            s = jnp.max(jnp.abs(x), axis=-1, keepdims=True) / QMAX
            s = jnp.maximum(s, 1e-08)
            q = jnp.clip(jnp.round(x / s), -QMAX, QMAX)
            return (q, s)

        def _quant_w(W):
            ws = jnp.max(jnp.abs(W), axis=1, keepdims=True) / QMAX
            ws = jnp.maximum(ws, 1e-08)
            Wq = jnp.clip(jnp.round(W / ws), -QMAX, QMAX)
            return (Wq, ws)
        B, S, D = hidden_states.shape
        x = hidden_states.reshape(B * S, D)
        x = x * jax.lax.rsqrt(jnp.mean(x * x, axis=-1, keepdims=True) + EPS)
        x = x * rmsnorm_weight
        q, s = _quant_act(x)
        Wgq, wsg = _quant_w(Wg)
        Wuq, wsu = _quant_w(Wu)
        gate = jnp.einsum('td,id->ti', q, Wgq) * s * wsg.T
        up = jnp.einsum('td,id->ti', q, Wuq) * s * wsu.T
        h = jax.nn.silu(gate) * up
        q2, s2 = _quant_act(h)
        Wdq, wsd = _quant_w(Wd)
        out = jnp.einsum('ti,di->td', q2, Wdq) * s2 * wsd.T
        return out.reshape(B, S, D)
    x = x + _L0_xattn_ref(_layernorm(x, axis=-1), ctx_4096, L0_xattn_Wq, L0_xattn_Wk, L0_xattn_Wv, L0_xattn_Wo)
    x = x + _L0_attn_ref(_layernorm(x, axis=-1), L0_attn_w_q, L0_attn_w_k, L0_attn_w_v, L0_attn_w_out)
    x = x + _L0_ffn_ref(_layernorm(x, axis=-1), L0_ffn_route_w, L0_ffn_A, L0_ffn_Bw)
    x = x + _L1_xattn_ref(_layernorm(x, axis=-1), ctx_4096, ctx_4096, L1_xattn_Wq, L1_xattn_Wk, L1_xattn_Wv, L1_xattn_Wo)
    x = x + _L1_attn_ref(_layernorm(x, axis=-1), L1_attn_Wq, L1_attn_Wk, L1_attn_Wv, L1_attn_Wo, L1_attn_cos, L1_attn_sin)
    x = x + _L1_ffn_ref(_layernorm(x, axis=-1), L1_ffn_rmsnorm_weight, L1_ffn_Wg, L1_ffn_Wu, L1_ffn_Wd)
    return x

_drawn_inputs = setup_inputs


def setup_inputs(seed=0):
    import zlib

    import numpy as np

    out = dict(_drawn_inputs(seed))
    spreads = {}
    factors = {'L1_attn_Wq': 3.477, 'L1_attn_Wk': 3.549, 'L1_attn_cos': 5.052, 'L1_attn_sin': 5.079}
    for name, (base, spread) in spreads.items():
        noise = np.random.default_rng([zlib.crc32(name.encode()), seed]).standard_normal(out[name].shape)
        drawn = base * np.exp(spread * noise) if base else spread * noise
        out[name] = jnp.asarray(drawn.astype(out[name].dtype))
    for name, factor in factors.items():
        out[name] = (out[name] * factor).astype(out[name].dtype)
    return out
```

```python
from contextlib import ExitStack

import numpy as np

import concourse.bass as bass
from concourse import mybir

F32 = mybir.dt.float32
F32R = mybir.dt.float32r
BF16 = mybir.dt.bfloat16
ALU = mybir.AluOpType
ACT = mybir.ActivationFunctionType
AX_X = mybir.AxisListType.X

P = 128
BANK = 512
ROUND = 12582912.0
QMAX = 127.0


class Signal:

    def __init__(self, semaphore):
        self.semaphore, self.value = semaphore, 0

    def after(self, instruction, step=1):
        instruction.then_inc(self.semaphore, step)
        self.value += step
        return (self, self.value)


class Feed:

    def __init__(self, queue, wait, buffers, signals, pieces, first=()):
        self.queue, self.wait, self.buffers, self.signals = queue, wait, buffers, signals
        self.pieces, self.loaded, self.taken = pieces, [], 0
        for _ in range(min(len(buffers), len(pieces))):
            self.load(first)

    def load(self, events):
        n = len(self.loaded)
        if n == len(self.pieces):
            return
        slot = n % len(self.buffers)
        self.wait(self.queue, *events)
        for destination, source in self.pieces[n](self.buffers[slot]):
            event = self.signals[slot].after(self.queue.dma_start(destination, source), 16)
        self.loaded.append(event)

    def take(self):
        n = self.taken
        self.taken += 1
        return self.buffers[n % len(self.buffers)], self.loaded[n]

    def release(self, *events):
        self.load(events)


def build(nc, a, out, stop=99):
    T = 256
    D = 1024
    CTX = 4096
    TT, KT = T // P, D // P
    waited = {}

    with ExitStack() as ctx:
        def signal(name):
            return Signal(ctx.enter_context(nc.semaphore(name)))

        def wait(engine, *events):
            for event in events:
                if event is None:
                    continue
                s, value = event
                if waited.get((id(engine), id(s)), 0) < value:
                    engine.wait_ge(s.semaphore, value)
                    waited[(id(engine), id(s))] = value

        pe, act, dve, pool, sp = nc.tensor, nc.scalar, nc.vector, nc.gpsimd, nc.sync
        pe_done, act_done, dve_done, pool_done = (signal(f"{n}_done") for n in ("pe", "act", "dve", "pool"))
        PE, ACTE, DVE, POOL = pe_done.after, act_done.after, dve_done.after, pool_done.after

        def so_far(engine_done):
            return (engine_done, engine_done.value)

        def sb(stack, name, shape, dtype=F32):
            return stack.enter_context(nc.sbuf_tensor(name, shape, dtype))

        psum = ctx.enter_context(nc.psum_tensor("psum", [P, 8, BANK], F32))
        bank_read = [None] * 8
        const_in, x_in, small_dma = signal("const_in"), signal("x_in"), signal("small_dma")
        panel_in = [signal(f"panel_in{i}") for i in range(3)]

        x = sb(ctx, "x", [P, TT, D])
        ident = sb(ctx, "ident", [P, P])
        stats = sb(ctx, "stats", [P, TT, 2, 6])
        moments = sb(ctx, "moments", [P, TT, 2])
        tiny = sb(ctx, "tiny", [P, 8, TT])
        FF = 2752
        FT = -(-FF // P)
        NQ = 2 * FT + KT
        w_scale = sb(ctx, "w_scale", [P, NQ])
        w_inverse = sb(ctx, "w_inverse", [P, NQ])
        w_top = sb(ctx, "w_top", [P, NQ])
        ident_b = sb(ctx, "ident_b", [P, P], BF16)
        scales_set = POOL(pool.memset(w_scale[:], 1.0))
        x_in.after(sp.dma_start(x[:], a["x"].rearrange("a (t p) d -> p (a t) d", p=P)), 16)
        const_ready = const_in.after(sp.dma_start(ident[:], a["ident"]), 16)
        wait(act, const_ready)
        ident_ready = ACTE(act.activation(ident_b[:], ident[:], ACT.Copy))
        x_ready = (x_in, 16)

        def inverse_root(variance, eps, ready):
            v, sd, r, w = (tiny[:, i, :] for i in range(4))
            wait(dve, ready)
            e = DVE(dve.tensor_scalar(v, variance, 1.0, eps, ALU.mult, ALU.add))
            wait(act, e)
            e = ACTE(act.activation(sd, v, ACT.Sqrt))
            wait(dve, e)
            wait(dve, DVE(dve.reciprocal(r, sd)))
            wait(dve, DVE(dve.tensor_tensor(w, v, r, ALU.mult)))
            wait(dve, DVE(dve.tensor_tensor(w, w, r, ALU.mult)))
            wait(dve, DVE(dve.tensor_scalar(w, w, -0.5, 1.5, ALU.mult, ALU.add)))
            return r, DVE(dve.tensor_tensor(r, r, w, ALU.mult))

        def layernorm(xn, free=()):
            wait(dve, x_ready, *free)
            for t in range(TT):
                for h in range(2):
                    e = DVE(dve.bn_stats(stats[:, t, h, :], x[:, t, h * 512:h * 512 + 512]))
            wait(dve, e)
            for t in range(TT):
                e = DVE(dve.bn_aggr(moments[:, t, :], stats[:, t].rearrange("p h s -> p (h s)")))
            r, e = inverse_root(moments[:, :, 1], 1e-5, e)
            wait(dve, e)
            for t in range(TT):
                e = DVE(dve.tensor_scalar(xn[:, t, :], x[:, t, :], moments[:, t, 0:1], r[:, t:t + 1],
                                          ALU.subtract, ALU.mult))
            return e

        def turn(src, dst, ready, banks, cols=D, free=()):
            done = []
            wait(pe, ready, const_ready)
            for i in range(cols // P // 2):
                b = banks[i % len(banks)]
                wait(pe, bank_read[b])
                for j in range(2):
                    for t in range(TT):
                        k = 2 * i + j
                        c = (j * TT + t) * P
                        e = PE(pe.transpose(psum[:, b, c:c + P], src[:, t, k * P:k * P + P], ident[:]))
                copy = psum[:, b, :].rearrange("p (j n) -> p j n", j=2)
                if i % 2:
                    wait(dve, e, *free)
                    bank_read[b] = DVE(dve.tensor_copy(dst[:, 2 * i:2 * i + 2, :], copy))
                else:
                    wait(act, e, *free)
                    bank_read[b] = ACTE(act.activation(dst[:, 2 * i:2 * i + 2, :], copy, ACT.Copy))
                done.append(bank_read[b])
            return done

        def linear(stationary, ready, panels, halves, banks, consume, width=BANK):
            wait(pe, *ready)
            for n in range(halves):
                own = [banks[(TT * n + t) % len(banks)] for t in range(TT)]
                wait(pe, *(bank_read[b] for b in own))
                k = 0
                while k < len(stationary):
                    w, arrived = panels.take()
                    wait(pe, arrived)
                    for r in range(w.rows):
                        for t in range(TT):
                            mm = pe.matmul(psum[:, own[t], 0:width], stationary[k][:, t * P:t * P + P],
                                           w.ap(r, width), start=k == 0, stop=k == len(stationary) - 1)
                        k += 1
                    e = PE(mm)
                    panels.release(e)
                for t in range(TT):
                    bank_read[own[t]] = consume(n, t, psum[:, own[t], 0:width], e)

        def add_to_x(n, t, product, event):
            nonlocal x_ready
            wait(dve, event)
            block = x[:, t, n * BANK:(n + 1) * BANK]
            x_ready = DVE(dve.tensor_tensor(block, product, block, ALU.add))
            return x_ready

        def invert_row(rows, result, turned, few, ready):
            n = rows.shape[-1]
            wait(dve, ready)
            read = DVE(dve.transpose(turned, rows))
            wait(dve, read)
            wait(dve, DVE(dve.reciprocal(few, turned.rearrange("p (b j) -> p b j", j=32)[:, :, 0])))
            return read, DVE(dve.transpose(result, few.unsqueeze(2).broadcast_to([32, n // 32, 32])))

        H0, KV0, HD0 = 16, 4, 96
        G0 = H0 // KV0
        KV1, HD1 = 8, 32
        G1 = 4
        S0 = CTX + T
        CH = 256
        NCH = S0 // CH
        VW = P
        NS0 = S0 // P
        V1W = KV1 // 2 * 3 * HD1

        def scratch(name, shape, dtype):
            return nc.dram_tensor(name, shape, dtype, kind="Internal").ap()

        k0_high = scratch("k0_high", [KV0, HD0, S0], F32)
        k0_low = scratch("k0_low", [KV0, HD0, S0], F32)
        k1_high = scratch("k1_high", [KV1 * HD1, CTX], F32)
        k1_low = scratch("k1_low", [KV1 * HD1, CTX], F32)
        v0_dram = scratch("v0_dram", [KV0, P, NS0, VW], F32)
        v1_dram = scratch("v1_dram", [P, CTX // P, V1W], F32)

        attn0 = ExitStack()
        q_high = sb(attn0, "q_high", [HD0 + 1, H0 * T], F32R)
        q_low = sb(attn0, "q_low", [HD0 + 1, H0 * T], F32R)
        top0 = sb(attn0, "top0", [P, KV0 * G0 * TT, NCH])
        neg_top0 = sb(attn0, "neg_top0", [P, KV0 * G0 * TT])
        top_high = sb(attn0, "top_high", [32, P], F32R)
        top_low = sb(attn0, "top_low", [32, P], F32R)

        kv_spilled = []
        with ExitStack() as phase:
            xnT = sb(phase, "xnT_ab", [P, KT, T])
            w_high = sb(phase, "w_high", [P, KT, 1280], F32R)
            w_low = sb(phase, "w_low", [P, KT, 1280], F32R)
            c_high = [sb(phase, f"c_high{i}", [P, KT, CH], F32R) for i in range(2)]
            c_low = [sb(phase, f"c_low{i}", [P, KT, CH], F32R) for i in range(2)]
            staged = [sb(phase, f"staged{i}", [P, 1280]) for i in range(3)]
            k_out = [[sb(phase, f"k_out{i}{p}", [P, 2, CH], F32R) for p in "hl"] for i in range(3)]
            v0_out = [sb(phase, f"v0_out{i}", [P, KV0, VW]) for i in range(2)]
            v1_out = [sb(phase, f"v1_out{i}", [P, V1W]) for i in range(2)]
            stage_in = [signal(f"stage_in{i}") for i in range(3)]
            k_sent = [signal(f"k_sent{i}") for i in range(3)]
            v0_sent = [signal(f"v0_sent{i}") for i in range(2)]
            v1_sent = [signal(f"v1_sent{i}") for i in range(2)]

            for v in v0_out:
                POOL(pool.memset(v[:, :, HD0:VW], 1.0))
            for v in v1_out:
                ones_set = POOL(pool.memset(v[:], 1.0))

            def q_piece(h):
                return lambda s: [(s[:, 0:KT * HD0], a["wq0"][h])]

            def w_piece(k):
                return lambda s: [(s[:], a["wkv"][k])]

            def c_piece(c, half):
                return lambda s: [(s[:, 0:4 * CH], a["ctxT"][c, :, half * 4 * CH:(half + 1) * 4 * CH])]

            order = []
            for i in range(KT):
                order += [q_piece(2 * i), q_piece(2 * i + 1), w_piece(i)]
            for c in range(CTX // CH):
                order += [c_piece(c, 0), c_piece(c, 1)]
            stage = Feed(sp, wait, staged, stage_in, order)

            with ExitStack() as early:
                xn = sb(early, "xn_ab", [P, TT, D])
                normed = layernorm(xn)
                turned = turn(xn, xnT, normed, [0, 1, 2, 3])
            queries = []
            for h in range(H0):
                b = 4 + h % 4
                w, arrived = stage.take()
                wait(pe, arrived, bank_read[b], *turned)
                for k in range(KT):
                    mm = pe.matmul(psum[0:HD0, b, 0:T], w[:, k * HD0:(k + 1) * HD0], xnT[:, k, :],
                                   start=k == 0, stop=k == KT - 1)
                e = PE(mm)
                stage.release(e)
                cols = slice(h * T, (h + 1) * T)
                wait(act, e)
                e_high = ACTE(act.activation(q_high[0:HD0, cols], psum[0:HD0, b, 0:T], ACT.Copy))
                wait(dve, e_high)
                bank_read[b] = DVE(dve.tensor_tensor(q_low[0:HD0, cols], psum[0:HD0, b, 0:T],
                                                     q_high[0:HD0, cols].bitcast(F32), ALU.subtract))
                queries.append(bank_read[b])
                if h % 2:
                    i = h // 2
                    w, arrived = stage.take()
                    wait(act, arrived)
                    e = ACTE(act.activation(w_high[:, i, :], w[:], ACT.Copy))
                    wait(dve, e)
                    weights_split = DVE(dve.tensor_tensor(w_low[:, i, :], w[:],
                                                          w_high[:, i, :].bitcast(F32), ALU.subtract))
                    stage.release(weights_split)

            chunk_read = [None] * NCH

            def split_chunk(c):
                high, low = c_high[c % 2], c_low[c % 2]
                free = chunk_read[c - 2] if c >= 2 else None
                for half in range(2):
                    ks = slice(4 * half, 4 * half + 4)
                    if c < CTX // CH:
                        s, arrived = stage.take()
                        src = s[:, 0:4 * CH].rearrange("p (k n) -> p k n", k=4)
                    else:
                        src, arrived = xnT[:, ks, :], None
                    wait(act, arrived, free)
                    e = ACTE(act.activation(high[:, ks, :], src, ACT.Copy))
                    wait(dve, e, free)
                    e = DVE(dve.tensor_tensor(low[:, ks, :], src, high[:, ks, :].bitcast(F32), ALU.subtract))
                    if c < CTX // CH:
                        stage.release(e)
                return e

            bank_turn = 0

            def next_bank():
                nonlocal bank_turn
                bank_turn += 1
                return (bank_turn - 1) % 8

            k_slot = v_slot = 0
            k_slot_free = [()] * 3
            split = [split_chunk(0)]
            for c in range(NCH):
                latents = c == NCH - 1
                if not latents:
                    split.append(split_chunk(c + 1))
                high, low = c_high[c % 2], c_low[c % 2]
                at = slice(c * CH, (c + 1) * CH)
                wait(pe, split[c], weights_split)
                pending = []

                def take_maxima(jobs):
                    for pair, slot, e_high in jobs:
                        wait(pe, e_high, *queries)
                        for j in range(2):
                            head = 2 * pair + j
                            for g in range(0, G0 * TT, 2):
                                b = next_bank()
                                wait(pe, bank_read[b])
                                for i in range(2):
                                    q0 = head * G0 * T + (g + i) * P
                                    mm = pe.matmul(psum[:, b, i * CH:(i + 1) * CH],
                                                   q_high[0:HD0, q0:q0 + P],
                                                   k_out[slot][0][0:HD0, j, :], start=True, stop=True)
                                e = PE(mm)
                                wait(dve, e)
                                r0 = head * G0 * TT + g
                                bank_read[b] = DVE(dve.tensor_reduce(
                                    top0[:, r0:r0 + 2, c], psum[:, b, :].rearrange("p (i n) -> p i n", i=2),
                                    AX_X, ALU.max))
                        k_slot_free[slot] = k_slot_free[slot] + (e,)

                for pair in range(2 if latents else 3):
                    tiles = (0, 1) if pair < 2 else (0,)
                    m = HD0 if latents else P
                    b = next_bank()
                    wait(pe, bank_read[b])
                    for j in tiles:
                        col = (2 * pair + j) * P
                        for k in range(KT):
                            o = psum[0:m, b, j * CH:(j + 1) * CH]
                            pe.matmul(o, w_high[:, k, col:col + m], high[:, k, :], start=k == 0, stop=False)
                            pe.matmul(o, w_high[:, k, col:col + m], low[:, k, :], start=False, stop=False)
                            mm = pe.matmul(o, w_low[:, k, col:col + m], high[:, k, :], start=False,
                                           stop=k == KT - 1)
                    e = PE(mm)
                    slot = k_slot % 3
                    k_slot += 1
                    n = len(tiles)
                    src = psum[0:m, b, 0:n * CH].rearrange("p (j n) -> p j n", j=n)
                    kh, kl = (k_out[slot][i][0:m, 0:n, :] for i in range(2))
                    wait(act, e, *k_slot_free[slot])
                    e_high = ACTE(act.activation(kh, src, ACT.Copy))
                    wait(dve, e_high, *k_slot_free[slot])
                    bank_read[b] = DVE(dve.tensor_tensor(kl, src, kh.bitcast(F32), ALU.subtract))
                    wait(sp, bank_read[b])
                    for part, k0d, k1d in ((0, k0_high, k1_high), (1, k0_low, k1_low)):
                        o = k_out[slot][part][:].bitcast(F32)
                        if pair < 2:
                            e = k_sent[slot].after(sp.dma_start(
                                k0d[2 * pair:2 * pair + 2, :, at].rearrange("h d n -> d h n"), o[0:HD0, :, :]), 16)
                            if not latents:
                                e = k_sent[slot].after(sp.dma_start(
                                    k1d[2 * pair * HD1:(2 * pair + 2) * HD1, at].rearrange(
                                        "(h d) n -> d h n", d=HD1), o[HD0:P, :, :]), 16)
                        else:
                            e = k_sent[slot].after(sp.dma_start(k1d[P:2 * P, at], o[:, 0, :]), 16)
                    k_slot_free[slot] = (e,)
                    if pending:
                        take_maxima(pending)
                        pending = []
                    if pair < 2:
                        pending = [(pair, slot, e_high)]
                take_maxima(pending)

                for s in range(CH // P):
                    ts = slice(s * P, (s + 1) * P)
                    b0, b1 = next_bank(), next_bank()
                    wait(pe, bank_read[b0], bank_read[b1])
                    outs = [(psum[:, b0, 0:KV0 * HD0], slice(640, 1024))]
                    if not latents:
                        outs.append((psum[:, b1, 0:KV1 * HD1], slice(1024, 1280)))
                    for k in range(KT):
                        for tokens, weights in ((high, w_high), (high, w_low), (low, w_high)):
                            for o, cols in outs:
                                mm = pe.matmul(o, tokens[:, k, ts], weights[:, k, cols],
                                               start=k == 0 and tokens is high and weights is w_high,
                                               stop=k == KT - 1 and tokens is low)
                    e = PE(mm)
                    if s == CH // P - 1:
                        chunk_read[c] = e
                    slot = v_slot % 2
                    v_slot += 1
                    row = c * (CH // P) + s
                    wait(act, e, ones_set, (v0_sent[slot], v0_sent[slot].value))
                    bank_read[b0] = ACTE(act.activation(
                        v0_out[slot][:, :, 0:HD0], outs[0][0].rearrange("p (h d) -> p h d", h=KV0), ACT.Copy))
                    wait(sp, bank_read[b0])
                    v0_sent[slot].after(sp.dma_start(v0_dram[:, :, row, :].rearrange("h p d -> p h d"),
                                                     v0_out[slot][:]), 16)
                    if not latents:
                        wait(dve, e, ones_set, (v1_sent[slot], v1_sent[slot].value))
                        bank_read[b1] = DVE(dve.tensor_copy(
                            v1_out[slot][:].rearrange("p (q b d) -> p q b d", b=3, d=HD1)[:, :, 0:3:2, :],
                            outs[1][0].rearrange("p (q b d) -> p q b d", b=2, d=HD1)))
                        wait(sp, bank_read[b1])
                        v1_sent[slot].after(sp.dma_start(v1_dram[:, row, :], v1_out[slot][:]), 16)
            kv_spilled = [(s, s.value) for s in (*k_sent, *v0_sent, *v1_sent)]

            wait(dve, bank_read[(bank_turn - 1) % 8], *bank_read)
            e = DVE(dve.tensor_reduce(neg_top0[:], top0[:], AX_X, ALU.max, negate=True))
            b = next_bank()
            wait(pe, e, bank_read[b])
            e = PE(pe.transpose(psum[0:32, b, 0:P], neg_top0[:], ident[:]))
            wait(act, e)
            e = ACTE(act.activation(top_high[:], psum[0:32, b, 0:P], ACT.Copy))
            wait(dve, e)
            bank_read[b] = DVE(dve.tensor_tensor(top_low[:], psum[0:32, b, 0:P], top_high[:].bitcast(F32),
                                                 ALU.subtract))
            wait(sp, bank_read[b], e)
            for q, top in ((q_high, top_high), (q_low, top_low)):
                tops_placed = small_dma.after(sp.dma_start(
                    q[HD0:HD0 + 1, :].bitcast(F32).rearrange("o (r n) -> o r n", n=P), top[:].bitcast(F32)), 16)
            last_of_b = [so_far(pe_done), so_far(act_done), so_far(dve_done), *kv_spilled]

        q_dram = scratch("q_dram", [2 * FT, P, KT * P], BF16)
        qd_dram = scratch("qd_dram", [KT, P, FT * P], BF16)
        ws_dram = scratch("ws_dram", [NQ, P], F32)
        q_spilled = [signal(f"q_spilled{i}") for i in range(2)]
        wf_in = [signal(f"wf_in{i}") for i in range(2)]

        class Quantiser:

            def __init__(self, stack, banks):
                self.rows = [sb(stack, f"wf_rows{i}", [P, FF]) for i in range(2)]
                self.ints = [sb(stack, f"wf_ints{i}", [P, FF], BF16) for i in range(2)]
                self.turned = [sb(stack, f"wf_turned{i}", [P, FT * P], BF16) for i in range(2)]
                self.turned_read, self.ints_read = [None] * 2, [None] * 2
                self.banks, self.n, self.rounded = banks, 0, {}

            def start(self, first):
                pieces = [self.piece(n) for n in range(NQ)]
                self.feed = Feed(sp, wait, self.rows, wf_in, pieces, first)

            def shape(self, n):
                if n < 2 * FT:
                    i = n % FT
                    return n // FT, i, min(P, FF - i * P), D
                return 2, n - 2 * FT, P, FF

            def piece(self, n):
                which, i, rows, cols = self.shape(n)
                return lambda tile: [(tile[0:rows, 0:cols], a[f"ffn_w{which}"][i * P:i * P + rows, :])]

            def quantise(self, n):
                _, _, rows, cols = self.shape(n)
                w, arrived = self.feed.take()
                w = w[0:rows, 0:cols]
                top, scale, inv = (z[0:rows, n:n + 1] for z in (w_top, w_scale, w_inverse))
                wait(dve, arrived, scales_set)
                wait(dve, DVE(dve.tensor_reduce(top, w, AX_X, ALU.max, apply_absolute_value=True)))
                wait(dve, DVE(dve.tensor_scalar(scale, top, 1.0 / QMAX, 1e-8, ALU.mult, ALU.max)))
                e = DVE(dve.reciprocal(inv, scale))
                wait(pool, e, so_far(pool_done))
                e = POOL(pool.tensor_scalar(w, w, inv, ROUND, ALU.mult, ALU.add))
                wait(act, e, self.ints_read[n % 2])
                self.rounded[n] = ACTE(act.activation(self.ints[n % 2][0:rows, 0:cols], w, ACT.Copy, bias=-ROUND))
                self.feed.release(self.rounded[n])

            def turn(self, n, engine):
                which, i, rows, cols = self.shape(n)
                ints, out_tile = self.ints[n % 2], self.turned[n % 2]
                blocks = -(-cols // P)
                wait(pe, self.rounded[n], ident_ready, const_ready)
                for b0 in range(0, blocks, 8):
                    b = self.banks[(b0 // 8 + n) % 2]
                    some = range(b0, min(b0 + 8, blocks))
                    bank = psum[:, b, :].bitcast(BF16).rearrange("p (k n) -> p k n", n=P)
                    wait(pe, bank_read[b])
                    for k in some:
                        width = min(P, cols - k * P)
                        e = PE(pe.transpose(bank[0:width, k - b0, 0:rows], ints[0:rows, k * P:k * P + width],
                                            ident_b[0:rows, 0:rows]))
                    full = [k for k in some if cols - k * P >= P]
                    jobs = [(P, full[0], len(full))] if full else []
                    if len(full) < len(some):
                        jobs.append((cols % P, some[-1], 1))
                    for height, k0, count in jobs:
                        dst = out_tile[0:height, k0 * P:(k0 + count) * P].rearrange("p (k n) -> p k n", n=P)[:, :, 0:rows]
                        src = bank[0:height, k0 - b0:k0 - b0 + count, 0:rows]
                        if engine is act:
                            wait(act, e, self.turned_read[n % 2])
                            done = ACTE(act.activation(dst, src, ACT.Copy))
                        else:
                            wait(dve, e, self.turned_read[n % 2])
                            done = DVE(dve.tensor_copy(dst, src))
                    bank_read[b] = done
                self.ints_read[n % 2] = e
                wait(sp, done)
                if which < 2:
                    pairs = [(q_dram[n], out_tile[:, 0:KT * P])] if rows == P else [
                        (q_dram[n].rearrange("p (k n) -> p k n", n=P)[:, :, 0:rows],
                         out_tile[:, 0:KT * P].rearrange("p (k n) -> p k n", n=P)[:, :, 0:rows])]
                else:
                    whole = FF // P * P
                    pairs = [(qd_dram[i, :, 0:whole], out_tile[:, 0:whole]),
                             (qd_dram[i, 0:FF - whole, whole:], out_tile[0:FF - whole, whole:])]
                for destination, source in pairs:
                    self.turned_read[n % 2] = q_spilled[n % 2].after(sp.dma_start(destination, source), 16)

            def step(self):
                if self.n < NQ:
                    self.quantise(self.n)
                if 0 < self.n <= NQ:
                    self.turn(self.n - 1, dve)
                self.n += 1

        panel_stack = ExitStack()
        panel_tiles = [panel_stack.enter_context(nc.sbuf_tensor(f"panel{i}", [P, KT * BANK], F32, side="right"))
                       for i in range(3)]
        class Panel:

            def __init__(self, tile, rows, k=P):
                self.tile, self.rows, self.k = tile, rows, k

            def ap(self, r, width):
                return self.tile[0:self.k, r * width:(r + 1) * width]

        class Panels:

            def __init__(self, feed, shapes):
                self.feed, self.shapes, self.n = feed, shapes, 0

            def take(self):
                tile, arrived = self.feed.take()
                rows, k = self.shapes[self.n]
                self.n += 1
                return Panel(tile, rows, k), arrived

            def release(self, *events):
                self.feed.release(*events)

        plan = []

        def panel(source, rows, width, k=P):
            plan.append((source, rows, width, k))

        for half in range(2):
            for part in range(2):
                panel(a["wo0"][half, part], 8, BANK, HD0)
        for name in ("wq_a", "wk_a", "wv_a", "wo_a"):
            for half in range(2):
                panel(a[name][half], KT, BANK)
        panel(a["route"], KT, 136)
        panel(a["lora_b"], 2, BANK)
        for name in ("wq1", "wo1", "wq_b"):
            for half in range(2):
                panel(a[name][half], KT, BANK)
        panel(a["wkv_b"], KT, BANK)
        for half in range(2):
            panel(a["wo_b"][half], KT, BANK)

        def panel_piece(source, rows, width, k):
            return lambda tile: [(tile[0:k, 0:rows * width], source)]

        panels = Panels(Feed(sp, wait, panel_tiles, panel_in, [panel_piece(*p) for p in plan], first=last_of_b),
                        [(rows, k) for _, rows, _, k in plan])

        weighted = sb(attn0, "weighted0", [HD0, H0, T])
        with ExitStack() as phase:
            SC = 512
            key_high = [sb(phase, f"key_high{i}", [HD0 + 1, SC], F32R) for i in range(4)]
            key_low = [sb(phase, f"key_low{i}", [HD0, SC], F32R) for i in range(4)]
            value = [sb(phase, f"value{i}", [P, SC // P, VW]) for i in range(4)]
            probs = [sb(phase, f"probs{i}", [P, G0 * T]) for i in range(3)]
            raw = sb(phase, "raw0", [HD0, G0 * T])
            sums = sb(phase, "sums0", [32, G0 * T])
            few = sb(phase, "few0", [32, G0 * T // 32])
            inverse = sb(phase, "inverse0", [HD0, G0 * T])
            kv_in = [signal(f"kv_in{i}") for i in range(4)]
            quantiser = Quantiser(phase, (6, 7))
            wait(pool, *last_of_b)
            for k in key_high:
                wait(pool, so_far(pool_done))
                ones_set = POOL(pool.memset(k[HD0:HD0 + 1, :].bitcast(F32), 1.0))

            def kv_piece(kv, first):
                n = min(SC, S0 - first)

                def dmas(slot):
                    high, low, v = slot
                    return [(high[0:HD0, 0:n].bitcast(F32), k0_high[kv, :, first:first + n]),
                            (low[:, 0:n].bitcast(F32), k0_low[kv, :, first:first + n]),
                            (v[:, 0:n // P, :], v0_dram[kv, :, first // P:(first + n) // P, :])]
                return dmas

            pieces = [kv_piece(kv, first) for kv in range(KV0) for first in range(0, S0, SC)]
            feed = Feed(sp, wait, list(zip(key_high, key_low, value)), kv_in, pieces,
                        first=last_of_b)
            quantiser.start(last_of_b)
            steps = [(kv, s) for kv in range(KV0) for s in range(NS0)]
            exp_done, pv_done, held = {}, {}, {}
            scale = float(1.0 / np.sqrt(np.float32(HD0)))

            def scores(n):
                kv, s = steps[n]
                if s % (SC // P) == 0:
                    held["now"] = feed.take()
                (high, low, v), arrived = held["now"]
                held[n] = v
                wait(pe, arrived, tops_placed, ones_set)
                at = slice(s % 4 * P, s % 4 * P + P)
                for half in range(2):
                    b = 2 * (n % 2) + half
                    wait(pe, bank_read[b])
                    q = slice(kv * G0 * T + half * BANK, kv * G0 * T + (half + 1) * BANK)
                    pe.matmul(psum[:, b, :], high[:, at], q_high[:, q], start=True, stop=False)
                    pe.matmul(psum[:, b, :], high[:, at], q_low[:, q], start=False, stop=False)
                    mm = pe.matmul(psum[:, b, :], low[:, at], q_high[0:HD0, q], start=False, stop=True)
                e = PE(mm)
                wait(act, e, pv_done.get(n - 3))
                exp_done[n] = ACTE(act.activation(
                    probs[n % 3][:], psum[:, 2 * (n % 2):2 * (n % 2) + 2, :].rearrange("p b n -> p (b n)"),
                    ACT.Exp, scale=scale))
                bank_read[2 * (n % 2)] = bank_read[2 * (n % 2) + 1] = exp_done[n]

            def weigh(n):
                kv, s = steps[n]
                wait(pe, exp_done[n])
                for half in range(2):
                    wait(pe, bank_read[4 + half])
                    halves_done[half] = PE(pe.matmul(psum[:, 4 + half, :], held[n][:, s % 4, :],
                                                     probs[n % 3][:, half * BANK:(half + 1) * BANK],
                                                     start=s == 0, stop=s == NS0 - 1))
                pv_done[n] = halves_done[1]
                if s % 4 == 3 or s == NS0 - 1:
                    feed.release(pv_done[n])
                if s == NS0 - 1:
                    for half in range(2):
                        cols = slice(half * BANK, (half + 1) * BANK)
                        wait(act, halves_done[half], normalised[0])
                        e_raw = ACTE(act.activation(raw[:, cols], psum[0:HD0, 4 + half, :], ACT.Copy))
                        read, inverted = invert_row(psum[HD0:P, 4 + half, :], inverse[0:32, cols], sums[:, cols],
                                                    few[:, half * 16:(half + 1) * 16], e_raw)
                        bank_read[4 + half] = read
                    wait(dve, inverted)
                    for row in (32, 64):
                        e = DVE(dve.tensor_copy(inverse[row:row + 32, :], inverse[0:32, :]))
                    wait(dve, e)
                    o = weighted[:, kv * G0:(kv + 1) * G0, :].rearrange("d g n -> d (g n)")
                    normalised[0] = DVE(dve.tensor_tensor(o, raw[:], inverse[:], ALU.mult))

            normalised, halves_done = [None], [None, None]
            scores(0)
            for n in range(len(steps)):
                if n + 1 < len(steps):
                    scores(n + 1)
                weigh(n)
                if n % 2 == 1:
                    quantiser.step()
            while quantiser.n <= NQ:
                quantiser.step()
            attended = normalised[0]
            last_of_c = [attended, pv_done[len(steps) - 1], *quantiser.turned_read, *quantiser.ints_read]
            q_all_spilled = [(s, s.value) for s in q_spilled]

        linear([weighted[:, h, :] for h in range(H0)], [attended], panels, 2, [0, 1, 2, 3], add_to_x)
        attn0.close()
        done = [x_ready, *last_of_c, so_far(pe_done), so_far(act_done)]
        out_done = signal("out_done")

        def finish():
            wait(sp, x_ready)
            e = out_done.after(sp.dma_start(out.rearrange("a (t p) d -> p (a t) d", p=P), x[:]), 16)
            wait(sp, e)

        if stop <= 1:
            return finish()

        class Causal:

            def __init__(self, name, heads, kv_heads, hd, scale, interleaved):
                self.name, self.heads, self.kv_heads, self.hd = name, heads, kv_heads, hd
                self.scale, self.interleaved = scale, interleaved

            def run(self, cos_dram, sin_dram, free):
                heads, kv_heads, hd = self.heads, self.kv_heads, self.hd
                per = P // hd
                KW = kv_heads * hd
                n_ = self.name
                with ExitStack() as phase:
                    xn = sb(phase, f"xn_{n_}", [P, TT, D])
                    xnT = sb(phase, f"xnT_{n_}", [P, KT, T])
                    q_rot = sb(phase, f"q_rot_{n_}", [P, TT, D])
                    k_rot = sb(phase, f"k_rot_{n_}", [P, TT, KW])
                    v = sb(phase, f"v_{n_}", [P, TT, KW])
                    qz = sb(phase, f"qz_{n_}", [P, heads, T])
                    kT = sb(phase, f"kT_{n_}", [P, KW // P, T])
                    cos = sb(phase, f"cos_{n_}", [P, TT, hd])
                    sin = sb(phase, f"sin_{n_}", [P, TT, hd])
                    mask = sb(phase, f"mask_{n_}", [P, 3 * P])
                    part = [sb(phase, f"part{i}_{n_}", [P, BANK]) for i in range(2)]
                    masked = [sb(phase, f"masked{i}_{n_}", [P, 3 * P]) for i in range(4)]
                    probs = [sb(phase, f"probs{i}_{n_}", [P, 3 * P]) for i in range(4)]
                    probsT = [sb(phase, f"probsT{i}_{n_}", [P, 3 * P]) for i in range(4)]
                    small = sb(phase, f"small_{n_}", [P, 4, 3, TT])
                    oT = sb(phase, f"oT_{n_}", [P, KT, T])
                    wait(sp, *free)
                    for dst, src in ((cos, cos_dram), (sin, sin_dram), (mask, a["mask"])):
                        tables_ready = const_in.after(sp.dma_start(dst[:], src), 16)
                    wait(pool, so_far(pool_done), *free)
                    zeroed = POOL(pool.memset(qz[:], 0.0))
                    normed = layernorm(xn, free)
                    turned = turn(xn, xnT, normed, [4, 5, 6, 7])

                    def halves(ap):
                        if self.interleaved:
                            v4 = ap.rearrange("p b (i two) -> p b i two", two=2)
                            return v4[:, :, :, 0], v4[:, :, :, 1]
                        return ap[:, :, 0:hd // 2], ap[:, :, hd // 2:hd]

                    part_free = None

                    def rotate(dst, src, t, event):
                        nonlocal part_free
                        cols = src.shape[-1]
                        nb = cols // hd
                        blocks = lambda ap: ap.rearrange("p (b d) -> p b d", d=hd)
                        table = lambda z: z[:, t, :].unsqueeze(1).broadcast_to([P, nb, hd])
                        one, two = (blocks(z[:, 0:cols]) for z in part)
                        src, dst = blocks(src), blocks(dst)
                        wait(dve, event, tables_ready, part_free)
                        DVE(dve.tensor_tensor(one, src, table(cos), ALU.mult))
                        (s1, s2), (n1, n2), (t1, t2) = halves(src), halves(table(sin)), halves(two)
                        DVE(dve.tensor_tensor(t1, s2, n1, ALU.mult))
                        read = DVE(dve.tensor_tensor(t2, s1, n2, ALU.mult))
                        wait(dve, read)
                        (o1, o2), (d1, d2) = halves(one), halves(dst)
                        DVE(dve.tensor_tensor(d1, o1, t1, ALU.subtract))
                        part_free = DVE(dve.tensor_tensor(d2, o2, t2, ALU.add))
                        return read

                    xnT_k = [xnT[:, k, :] for k in range(KT)]

                    def take_q(n, t, product, event):
                        return rotate(q_rot[:, t, n * BANK:(n + 1) * BANK], product, t, event)

                    def take_k(n, t, product, event):
                        return rotate(k_rot[:, t, n * BANK:(n + 1) * BANK], product, t, event)

                    def take_v(n, t, product, event):
                        wait(act, event)
                        return ACTE(act.activation(v[:, t, n * BANK:(n + 1) * BANK], product, ACT.Copy))

                    def take_kv(n, t, product, event):
                        wait(act, event)
                        wait(dve, ACTE(act.activation(v[:, t, :], product[:, KW:2 * KW], ACT.Copy)))
                        return rotate(k_rot[:, t, :], product[:, 0:KW], t, event)

                    linear(xnT_k, turned, panels, 2, [0, 1, 2, 3], take_q)
                    if KW == D:
                        linear(xnT_k, turned, panels, 2, [4, 5, 6, 7], take_k)
                        k_ready = part_free
                        linear(xnT_k, turned, panels, 2, [0, 1, 2, 3], take_v)
                    else:
                        linear(xnT_k, turned, panels, 1, [4, 5, 6, 7], take_kv)
                        k_ready = part_free
                    v_ready = so_far(act_done)
                    k_turned = turn(k_rot, kT, k_ready, [4, 5, 6, 7], KW)
                    wait(pe, k_ready, const_ready)
                    placed = []
                    for i in range(KT // 2):
                        b = i % 4
                        wait(pe, bank_read[b])
                        for j in range(2):
                            for t in range(TT):
                                k = 2 * i + j
                                c = (j * TT + t) * P
                                e = PE(pe.transpose(psum[:, b, c:c + P], q_rot[:, t, k * P:k * P + P], ident[:]))
                        for j in range(2):
                            for g in range(per):
                                head = (2 * i + j) * per + g
                                row = head * kv_heads // heads * hd % P
                                dst = qz[row:row + hd, head, :]
                                src = psum[g * hd:(g + 1) * hd, b, j * T:(j + 1) * T]
                                if i % 2:
                                    wait(dve, e, zeroed)
                                    done = DVE(dve.tensor_copy(dst, src))
                                else:
                                    wait(act, e, zeroed)
                                    done = ACTE(act.activation(dst, src, ACT.Copy))
                        bank_read[b] = done
                        placed.append(done)

                    scored, exps, norms, turns = {}, {}, {}, {}

                    def scores(h):
                        b, s = h % 2, h % 4
                        block = h * kv_heads // heads * hd // P
                        wait(pe, bank_read[b], *placed, *k_turned)
                        pe.matmul(psum[:, b, 0:P], qz[:, h, 0:P], kT[:, block, 0:P], start=True, stop=True)
                        e = PE(pe.matmul(psum[:, b, P:3 * P], qz[:, h, P:T], kT[:, block, :], start=True, stop=True))
                        scored[h] = e

                    def soften(h):
                        b, s = h % 2, h % 4
                        top, total = small[:, s, 0, :], small[:, s, 1, :]
                        wait(dve, scored[h], exps.get(h - 4))
                        e = DVE(dve.scalar_tensor_tensor(out=masked[s][:], in0=psum[:, b, 0:3 * P], scalar=self.scale,
                                                         in1=mask[:], op0=ALU.mult, op1=ALU.add))
                        bank_read[b] = e
                        wait(dve, e)
                        spans = (slice(0, P), slice(P, 3 * P))
                        for t in range(TT):
                            e = DVE(dve.tensor_reduce(top[:, t:t + 1], masked[s][:, spans[t]], AX_X, ALU.max,
                                                      negate=True))
                        wait(act, e, turns.get(h - 4))
                        for t in range(TT):
                            e = ACTE(act.activation(probs[s][:, spans[t]], masked[s][:, spans[t]], ACT.Exp,
                                                    bias=top[:, t:t + 1], accum_out=total[:, t:t + 1]))
                        exps[h] = e

                    def normalise(h):
                        s = h % 4
                        total, inv = small[:, s, 1, :], small[:, s, 2, :]
                        wait(dve, exps[h])
                        wait(dve, DVE(dve.reciprocal(inv, total)))
                        for t, span in enumerate((slice(0, P), slice(P, 3 * P))):
                            e = DVE(dve.tensor_scalar(probs[s][:, span], probs[s][:, span], inv[:, t:t + 1], None,
                                                      ALU.mult))
                        norms[h] = e

                    weighed = {}

                    def turn_probs(h):
                        b, s = 2 + h % 2, h % 4
                        wait(pe, norms[h], bank_read[b])
                        for i in range(3):
                            e = PE(pe.transpose(psum[:, b, i * P:(i + 1) * P], probs[s][:, i * P:(i + 1) * P],
                                                ident[:]))
                        turns[h] = e
                        wait(act, e, weighed.get(h - 4))
                        bank_read[b] = ACTE(act.activation(probsT[s][:], psum[:, b, 0:3 * P], ACT.Copy))

                    def weigh(h):
                        s, chunk = h % 4, h // per
                        b = 4 + chunk % 2
                        row = h % per * hd
                        j = h * kv_heads // heads
                        wait(pe, bank_read[2 + h % 2], bank_read[b], v_ready)
                        pe.matmul(psum[row:row + hd, b, 0:T], v[:, 0, j * hd:(j + 1) * hd], probsT[s][:, 0:T],
                                  start=True, stop=False, skip_group_check=True)
                        e = PE(pe.matmul(psum[row:row + hd, b, P:T], v[:, 1, j * hd:(j + 1) * hd],
                                         probsT[s][:, T:3 * P], start=False, stop=True, skip_group_check=True))
                        weighed[h] = e
                        if h % per == per - 1:
                            wait(act, e)
                            bank_read[b] = ACTE(act.activation(oT[:, chunk, :], psum[:, b, 0:T], ACT.Copy))

                    for i in range(heads + 3):
                        if i < heads:
                            scores(i)
                        if 0 <= i - 2 < heads:
                            normalise(i - 2)
                        if i < heads:
                            soften(i)
                        if 0 <= i - 2 < heads:
                            turn_probs(i - 2)
                        if i >= 3:
                            weigh(i - 3)
                    linear([oT[:, k, :] for k in range(KT)], [bank_read[4], bank_read[5]], panels, 2,
                           [0, 1, 2, 3], add_to_x)
                return [x_ready, so_far(pe_done), so_far(act_done)]

        attend_d = Causal("d", 16, 16, 64, 0.125, True)
        done = attend_d.run(a["cos_a"], a["sin_a"], done)
        if stop <= 2:
            return finish()

        E_, R = 8, 16
        with ExitStack() as phase:
            xn = sb(phase, "xn_e", [P, TT, D])
            xnT = sb(phase, "xnT_e", [P, KT, T])
            rank = sb(phase, "rank", [P, E_])
            chosen = sb(phase, "chosen", [P, TT, 2, E_])
            best = sb(phase, "best", [P, TT, 2])
            hidden = sb(phase, "hidden_e", [P, TT, E_ * R])
            hiddenT = sb(phase, "hiddenT_e", [P, T])
            wait(sp, *done)
            rank_ready = const_in.after(sp.dma_start(rank[:], a["rank"]), 16)
            normed = layernorm(xn, done)
            turned = turn(xn, xnT, normed, [4, 5, 6, 7])
            routed = []

            def route(n, t, product, event):
                top, first = best[:, t, 0:1], best[:, t, 1:2]
                ranks, weights = chosen[:, t, 0, :], chosen[:, t, 1, :]
                wait(dve, event, rank_ready)
                wait(dve, DVE(dve.tensor_reduce(top, product[:, 0:E_], AX_X, ALU.max)))
                wait(dve, DVE(dve.scalar_tensor_tensor(out=ranks, in0=product[:, 0:E_], scalar=top, in1=rank[:],
                                                       op0=ALU.is_equal, op1=ALU.mult)))
                wait(dve, DVE(dve.tensor_reduce(first, ranks, AX_X, ALU.max)))
                wait(dve, DVE(dve.tensor_scalar(weights, ranks, first, top, ALU.is_equal, ALU.mult)))
                e = DVE(dve.tensor_tensor(hidden[:, t, :].rearrange("p (e r) -> p e r", r=R),
                                          product[:, E_:E_ + E_ * R].rearrange("p (e r) -> p e r", r=R),
                                          weights.unsqueeze(2).broadcast_to([P, E_, R]), ALU.mult))
                routed.append(e)
                return e

            linear([xnT[:, k, :] for k in range(KT)], turned, panels, 1, [0, 1], route, width=E_ + E_ * R)
            wait(pe, *routed, bank_read[2])
            for t in range(TT):
                e = PE(pe.transpose(psum[:, 2, t * P:(t + 1) * P], hidden[:, t, :], ident[:]))
            wait(act, e)
            bank_read[2] = ACTE(act.activation(hiddenT[:], psum[:, 2, 0:T], ACT.Copy))
            w, arrived = panels.take()
            wait(pe, bank_read[2], arrived)
            for n in range(2):
                for t in range(TT):
                    b = 4 + 2 * n + t
                    wait(pe, bank_read[b])
                    e = PE(pe.matmul(psum[:, b, :], hiddenT[:, t * P:(t + 1) * P], w.ap(n, BANK), start=True,
                                     stop=True))
                    bank_read[b] = add_to_x(n, t, psum[:, b, :], e)
            panels.release(e)
            done = [x_ready, so_far(pe_done), so_far(act_done)]
        if stop <= 3:
            return finish()

        H1 = KV1 * G1
        NS1 = CTX // P
        NC1 = CTX // BANK
        with ExitStack() as phase:
            q_rows = sb(phase, "q_rows", [3 * HD1 + 2, KV1, G1 * T], F32R)
            k_rows = [sb(phase, f"k_rows{i}", [3 * HD1 + 2, CTX], F32R) for i in range(2)]
            v_all = sb(phase, "v_all", [P, NS1, V1W])
            probs = [sb(phase, f"probs_f{i}", [P, G1 * T]) for i in range(4)]
            odd = sb(phase, "odd_f", [2 * HD1, G1 * T])
            inverse = sb(phase, "inverse_f", [2 * HD1, G1 * T])
            sums = sb(phase, "sums_f", [HD1, BANK])
            few = sb(phase, "few_f", [HD1, BANK // 32])
            top1 = sb(phase, "top1", [P, G1 * TT, NC1])
            neg_top1 = sb(phase, "neg_top1", [P, G1 * TT])
            t_high = sb(phase, "t_high", [G1 * TT, P], F32R)
            t_low = sb(phase, "t_low", [G1 * TT, P], F32R)
            oT = sb(phase, "oT_f", [P, KV1, T])
            k1_in = [signal(f"k1_in{i}") for i in range(2)]
            v1_in = signal("v1_in")
            top_in = signal("top_in")

            def k1_piece(kv):
                rows = slice(kv * HD1, (kv + 1) * HD1)
                return lambda k: [(k[0:HD1, :].bitcast(F32), k1_high[rows, :]),
                                  (k[HD1:2 * HD1, :].bitcast(F32), k1_high[rows, :]),
                                  (k[2 * HD1:3 * HD1, :].bitcast(F32), k1_low[rows, :])]

            wait(pool, *done)
            for k in k_rows:
                wait(pool, so_far(pool_done))
                ones_set = POOL(pool.memset(k[3 * HD1:3 * HD1 + 2, :].bitcast(F32), 1.0))
            keys = Feed(sp, wait, k_rows, k1_in, [k1_piece(kv) for kv in range(KV1)], first=[*done, *kv_spilled])
            v1_ready = v1_in.after(sp.dma_start(v_all[:], v1_dram), 16)

            xn_parts = [probs[0], probs[1]]
            wait(dve, x_ready, *done)
            for t in range(TT):
                for h in range(2):
                    e = DVE(dve.bn_stats(stats[:, t, h, :], x[:, t, h * 512:h * 512 + 512]))
            wait(dve, e)
            for t in range(TT):
                e = DVE(dve.bn_aggr(moments[:, t, :], stats[:, t].rearrange("p h s -> p (h s)")))
            r, e = inverse_root(moments[:, :, 1], 1e-5, e)
            wait(dve, e)
            for t in range(TT):
                e = DVE(dve.tensor_scalar(xn_parts[t][:], x[:, t, :], moments[:, t, 0:1], r[:, t:t + 1],
                                          ALU.subtract, ALU.mult))
            wait(pe, e)
            xnT_parts = [probs[2], probs[3]]
            turned = []
            for i in range(KT // 2):
                b = 4 + i
                wait(pe, bank_read[b])
                for j in range(2):
                    for t in range(TT):
                        c = (j * TT + t) * P
                        k = 2 * i + j
                        e = PE(pe.transpose(psum[:, b, c:c + P], xn_parts[t][:, k * P:(k + 1) * P], ident[:]))
                wait(act, e)
                bank_read[b] = ACTE(act.activation(xnT_parts[i // 2][:, i % 2 * 2 * T:(i % 2 + 1) * 2 * T],
                                                   psum[:, b, :], ACT.Copy))
            wait(pe, bank_read[7])
            max_jobs, q1_ready = {}, {}

            def maxima(kv, m):
                rows, chunk = divmod(m, NC1)
                k, arrived = max_jobs[kv]
                b = 6 + m % 2
                wait(pe, arrived, bank_read[b], q1_ready[kv])
                e = PE(pe.matmul(psum[:, b, :], q_rows[0:3 * HD1, kv, rows * P:(rows + 1) * P],
                                 k[0:3 * HD1, chunk * BANK:(chunk + 1) * BANK], start=True, stop=True))
                wait(dve, e)
                bank_read[b] = DVE(dve.tensor_reduce(top1[:, rows, chunk:chunk + 1], psum[:, b, :], AX_X, ALU.max))

            tops_read = {}

            def place_maxima(kv):
                wait(dve, bank_read[6], bank_read[7], tops_read.get("pe"))
                tops_read["dve"] = DVE(dve.tensor_reduce(neg_top1[:], top1[:], AX_X, ALU.max, negate=True))

            def place_rows(kv):
                wait(pe, tops_read["dve"], bank_read[6])
                e = PE(pe.transpose(psum[0:G1 * TT, 6, 0:P], neg_top1[:], ident[:]))
                tops_read["pe"] = e
                wait(act, e, tops_read.get("dma"))
                e = ACTE(act.activation(t_high[:], psum[0:G1 * TT, 6, 0:P], ACT.Copy))
                wait(dve, e, tops_read.get("dma"))
                bank_read[6] = DVE(dve.tensor_tensor(t_low[:], psum[0:G1 * TT, 6, 0:P], t_high[:].bitcast(F32),
                                                     ALU.subtract))
                wait(sp, e, bank_read[6])
                for r, top in ((0, t_high), (1, t_low)):
                    row = 3 * HD1 + r
                    e = top_in.after(sp.dma_start(
                        q_rows[row:row + 1, kv, :].bitcast(F32).rearrange("o (r n) -> o r n", n=P),
                        top[:].bitcast(F32)), 16)
                tops_read["dma"] = e
                return e

            max_jobs[0] = keys.take()
            beside = list(range(G1 * TT * NC1))
            for n in range(2):
                w, arrived = panels.take()
                wait(pe, arrived)
                for c in range(4):
                    b, kv = c, 4 * n + c
                    wait(pe, bank_read[b])
                    for k in range(KT):
                        if kv > 0 and beside:
                            maxima(0, beside.pop(0))
                        mm = pe.matmul(psum[:, b, 0:T], w.ap(k, BANK)[:, c * P:(c + 1) * P],
                                       xnT_parts[k // 4][:, k % 4 * T:(k % 4 + 1) * T], start=k == 0, stop=k == KT - 1)
                    e = PE(mm)
                    for g in range(G1):
                        src = psum[g * HD1:(g + 1) * HD1, b, 0:T]
                        cols = slice(g * T, (g + 1) * T)
                        wait(act, e)
                        high = q_rows[0:HD1, kv, cols]
                        ACTE(act.activation(high, src, ACT.Copy))
                        e_high = ACTE(act.activation(q_rows[2 * HD1:3 * HD1, kv, cols], src, ACT.Copy))
                        wait(dve, e_high)
                        bank_read[b] = DVE(dve.tensor_tensor(q_rows[HD1:2 * HD1, kv, cols], src,
                                                             high.bitcast(F32), ALU.subtract))
                    q1_ready[kv] = bank_read[b]
                panels.release(e)
            q1_read = e

            scale = float(HD1 ** -0.5)
            for m in beside:
                maxima(0, m)
            place_maxima(0)
            placed = {0: place_rows(0)}
            exp_done, pv_done = {}, {}
            tiles = [(kv, s) for kv in range(KV1) for s in range(NS1)]

            def scores1(n):
                kv, s = tiles[n]
                k, arrived = max_jobs[kv]
                wait(pe, arrived, placed[kv], q1_ready[kv], ones_set)
                for half in range(2):
                    b = 2 * (n % 2) + half
                    wait(pe, bank_read[b])
                    e = PE(pe.matmul(psum[:, b, :], k[:, s * P:(s + 1) * P],
                                     q_rows[:, kv, half * BANK:(half + 1) * BANK], start=True, stop=True))
                wait(act, e, pv_done.get(n - 4), q1_read)
                exp_done[n] = ACTE(act.activation(
                    probs[n % 4][:], psum[:, 2 * (n % 2):2 * (n % 2) + 2, :].rearrange("p b n -> p (b n)"),
                    ACT.Exp, scale=scale))
                bank_read[2 * (n % 2)] = bank_read[2 * (n % 2) + 1] = exp_done[n]

            weighed_kv = [None, None]

            def weigh1(n, half):
                kv, s = tiles[n]
                wait(pe, exp_done[n], exp_done[n + 1], bank_read[4], bank_read[5], v1_ready, ones_set)
                for i in range(2):
                    col = kv // 2 * 3 * HD1 + kv % 2 * HD1
                    mm = pe.matmul(psum[i * 64:(i + 1) * 64, 4 + half, :], v_all[:, s + i, col:col + 2 * HD1],
                                   probs[(n + i) % 4][:, half * BANK:(half + 1) * BANK],
                                   start=s == 0, stop=s == NS1 - 2)
                pv_done[n] = pv_done[n + 1] = e = PE(mm)
                if s == NS1 - 2:
                    cols = slice(half * BANK, (half + 1) * BANK)
                    vr = slice(kv % 2 * HD1, kv % 2 * HD1 + HD1)
                    sr = slice(HD1 - kv % 2 * HD1, 2 * HD1 - kv % 2 * HD1)
                    wait(act, e, weighed_kv[half])
                    e = ACTE(act.activation(odd[:, cols], psum[64:128, 4 + half, :], ACT.Copy))
                    wait(dve, e)
                    e = DVE(dve.tensor_tensor(odd[:, cols], psum[0:64, 4 + half, :], odd[:, cols], ALU.add))
                    bank_read[4 + half] = e
                    later.append((kv, half, cols, vr, sr, e))

            later = []

            def normalise1():
                kv, half, cols, vr, sr, e = later.pop(0)
                wait(dve, so_far(dve_done))
                _, e = invert_row(odd[sr, cols], inverse[vr, cols], sums[:], few[:], e)
                wait(dve, e)
                for g in (2 * half, 2 * half + 1):
                    c = slice(g * T, (g + 1) * T)
                    weighed_kv[half] = DVE(dve.tensor_tensor(oT[g * HD1:(g + 1) * HD1, kv, :], odd[vr, c],
                                                             inverse[vr, c], ALU.mult))

            scores1(0)
            scores1(1)
            jobs = G1 * TT * NC1
            first_pair, last_pair = 2, NS1 // 2 - 4
            count = last_pair - first_pair + 1
            for n in range(0, len(tiles), 2):
                kv, s = tiles[n]
                pair = s // 2
                ahead = kv + 1 < KV1
                if s == 0 and ahead:
                    max_jobs[kv + 1] = keys.take()
                beside = [m for m in range(jobs) if ahead and first_pair + m * count // jobs == pair]
                steps = [lambda n=n: scores1(n + 2), lambda n=n: scores1(n + 3)] if n + 2 < len(tiles) else []
                steps += [lambda n=n: weigh1(n, 0), lambda n=n: weigh1(n, 1)]
                for i, step in enumerate(steps):
                    for m in beside[i * len(beside) // 4:(i + 1) * len(beside) // 4]:
                        maxima(kv + 1, m)
                    step()
                    if i == 2 and ahead and pair == last_pair + 1:
                        placed[kv + 1] = place_rows(kv + 1)
                if ahead and pair == last_pair:
                    place_maxima(kv + 1)
                if later and s != NS1 - 2:
                    normalise1()
                if s == NS1 - 2:
                    keys.release(pv_done[n])
            while later:
                normalise1()
            linear([oT[:, kv, :] for kv in range(KV1)], weighed_kv, panels, 2, [0, 1, 2, 3], add_to_x)
            done = [x_ready, so_far(pe_done), so_far(act_done), so_far(dve_done)]
        if stop <= 4:
            return finish()

        attend_g = Causal("g", 32, 8, 32, float(1.0 / np.sqrt(np.float32(32.0))), False)
        done = attend_g.run(a["cos_b"], a["sin_b"], done)
        if stop <= 5:
            return finish()

        panel_stack.close()
        with ExitStack() as phase:
            xn = sb(phase, "xn_h", [P, TT, D])
            square = sb(phase, "square", [P, D])
            gain = sb(phase, "gain", [P, D])
            ints = sb(phase, "ints_h", [P, TT, D], BF16)
            intsT = sb(phase, "intsT_h", [P, KT, T], BF16)
            act_scale = sb(phase, "act_scale", [P, 8, TT])
            gate_up = [sb(phase, f"gate_up{i}", [P, 2, 4 * KT * P], BF16) for i in range(2)]
            down = sb(phase, "down", [P, KT, FT * P], BF16)
            ws_g = sb(phase, "ws_g", [P, FF])
            ws_u = sb(phase, "ws_u", [P, FF])
            ws_d = sb(phase, "ws_d", [P, D])
            ws_turned = sb(phase, "ws_turned", [NQ, P])
            g_part = [sb(phase, f"g_part{i}", [P, BANK]) for i in range(2)]
            s_part = [sb(phase, f"s_part{i}", [P, BANK]) for i in range(2)]
            u_part = [sb(phase, f"u_part{i}", [P, BANK]) for i in range(2)]
            hid = sb(phase, "hid", [P, TT, FF])
            gu_in = [signal(f"gu_in{i}") for i in range(2)]
            down_in, ws_sent, ws_in = signal("down_in"), signal("ws_sent"), signal("ws_in")
            wait(sp, *done)
            gain_ready = const_in.after(sp.dma_start(gain[:], a["rms_weight"].partition_broadcast(P)), 16)
            wait(pe, *done, bank_read[0])
            e = PE(pe.transpose(psum[0:NQ, 0, 0:P], w_scale[:], ident[:]))
            wait(act, e, *done)
            bank_read[0] = ACTE(act.activation(ws_turned[:], psum[0:NQ, 0, 0:P], ACT.Copy))
            wait(sp, bank_read[0])
            e = ws_sent.after(sp.dma_start(ws_dram, ws_turned[:]), 16)

            def chunk_piece(c):
                n = min(4, FT - 4 * c)

                def dmas(tile):
                    pairs = []
                    for which in range(2):
                        at = which * FT + 4 * c
                        whole = n if 4 * c + n < FT else n - 1
                        pairs.append((tile[:, which, 0:whole * KT * P].rearrange("p (i m) -> p i m", i=whole),
                                      q_dram[at:at + whole].rearrange("i p m -> p i m")))
                        if whole < n:
                            rest = FF % P
                            view = lambda z: z.rearrange("p (k n) -> p k n", n=P)[:, :, 0:rest]
                            pairs.append((view(tile[:, which, whole * KT * P:n * KT * P]), view(q_dram[at + whole])))
                    return pairs
                return dmas

            chunks = -(-FT // 4)
            order = [chunk_piece(c) for c in range(chunks)]
            ring = Feed(sp, wait, gate_up, gu_in, order, first=[*done, *q_all_spilled])
            wait(sp, e)
            flat = ws_dram.rearrange("r n -> (r n)")
            ws_in.after(sp.dma_start(ws_g[:], flat[0:FF].partition_broadcast(P)), 16)
            ws_in.after(sp.dma_start(ws_u[:], flat[FT * P:FT * P + FF].partition_broadcast(P)), 16)
            ws_ready = ws_in.after(sp.dma_start(ws_d[:], flat[2 * FT * P:NQ * P].partition_broadcast(P)), 16)
            whole = FF // P * P
            down_in.after(sp.dma_start(down[:, :, 0:whole], qd_dram[:, :, 0:whole].rearrange("k p m -> p k m")), 16)
            down_ready = down_in.after(sp.dma_start(
                down[0:FF - whole, :, whole:], qd_dram[:, 0:FF - whole, whole:].rearrange("k p m -> p k m")), 16)

            def quantise(values, result, t, slot, ready):
                top, sc, inv = (act_scale[:, slot + i, t:t + 1] for i in range(3))
                wait(dve, ready)
                wait(dve, DVE(dve.tensor_reduce(top, values, AX_X, ALU.max, apply_absolute_value=True)))
                wait(dve, DVE(dve.tensor_scalar(sc, top, 1.0 / QMAX, 1e-8, ALU.mult, ALU.max)))
                wait(dve, DVE(dve.reciprocal(inv, sc)))
                wait(dve, DVE(dve.tensor_scalar(values, values, inv, ROUND, ALU.mult, ALU.add)))
                return DVE(dve.tensor_scalar(result, values, ROUND, None, ALU.subtract))

            normed = layernorm(xn, done)
            mean_square = act_scale[:, 6, :]
            wait(act, normed)
            for t in range(TT):
                e = ACTE(act.activation(square[:], xn[:, t, :], ACT.Square, accum_out=mean_square[:, t:t + 1]))
                wait(act, e)
            wait(dve, e)
            e = DVE(dve.tensor_scalar(mean_square, mean_square, 1.0 / D, None, ALU.mult))
            r, e = inverse_root(mean_square, 1e-6, e)
            wait(dve, e, gain_ready)
            for t in range(TT):
                e = DVE(dve.scalar_tensor_tensor(out=xn[:, t, :], in0=xn[:, t, :], scalar=r[:, t:t + 1],
                                                 in1=gain[:], op0=ALU.mult, op1=ALU.mult))
                rounded = quantise(xn[:, t, :], ints[:, t, :], t, 0, e)
            wait(pe, rounded)
            for i in range(2):
                b = 1 + i
                wait(pe, bank_read[b])
                bank = psum[:, b, :].bitcast(BF16)
                for j in range(4):
                    for t in range(TT):
                        k = 4 * i + j
                        c = j * T + t * P
                        e = PE(pe.transpose(bank[:, c:c + P], ints[:, t, k * P:(k + 1) * P], ident_b[:]))
                wait(dve, e)
                bank_read[b] = DVE(dve.tensor_copy(intsT[:, 4 * i:4 * i + 4, :].rearrange("p k n -> p (k n)"), bank))
            ints_turned = [bank_read[1], bank_read[2]]

            job = 0
            silu_done, mixed = {}, {}
            for c in range(chunks):
                w, arrived = ring.take()
                n_tiles = min(4, FT - 4 * c)
                width = min(BANK, FF - c * BANK)
                wait(pe, arrived, *ints_turned)
                for t in range(TT):
                    bg, bu = 2 * (job % 4), 2 * (job % 4) + 1
                    wait(pe, bank_read[bg], bank_read[bu])
                    parts = [(0, width)] if width == BANK else [(i * P, min(P, width - i * P)) for i in range(n_tiles)]
                    for which, b in ((0, bg), (1, bu)):
                        grid = w[:, which, :].rearrange("p (i k n) -> p i k n", k=KT, n=P)
                        for first, count in parts:
                            for k in range(KT):
                                moving = grid[:, :, k, :] if width == BANK else grid[:, first // P, k, 0:count]
                                mm = pe.matmul(psum[:, b, first:first + count], intsT[:, k, t * P:(t + 1) * P],
                                               moving, start=k == 0, stop=k == KT - 1)
                    e = PE(mm)
                    at = slice(c * BANK, c * BANK + width)
                    i = job % 2
                    sc = act_scale[:, 1, t:t + 1]
                    wait(dve, e, ws_ready, mixed.get(job - 2))
                    e_g = DVE(dve.scalar_tensor_tensor(out=g_part[i][:, 0:width], in0=psum[:, bg, 0:width], scalar=sc,
                                                       in1=ws_g[:, at], op0=ALU.mult, op1=ALU.mult))
                    bank_read[bg] = e_g
                    wait(act, e_g, mixed.get(job - 2))
                    silu_done[job] = ACTE(act.activation(s_part[i][:, 0:width], g_part[i][:, 0:width], ACT.Silu))
                    e_u = DVE(dve.scalar_tensor_tensor(out=u_part[i][:, 0:width], in0=psum[:, bu, 0:width], scalar=sc,
                                                       in1=ws_u[:, at], op0=ALU.mult, op1=ALU.mult))
                    bank_read[bu] = e_u
                    wait(pool, silu_done[job], e_u, so_far(pool_done))
                    mixed[job] = POOL(pool.tensor_tensor(hid[:, t, at], s_part[i][:, 0:width], u_part[i][:, 0:width],
                                                         ALU.mult))
                    job += 1
                ring.release(e)
            chunks_read = e

            hid_i = [w[:, 0, 0:FF] for w in gate_up]
            out_T = [gate_up[t][:, 1, 0:FT * P] for t in range(TT)]
            for t in range(TT):
                wait(dve, chunks_read)
                rounded = quantise(hid[:, t, :], hid_i[t], t, 3, mixed[job - 1])
                wait(pe, rounded)
                for b0 in range(0, FT, 8):
                    b = b0 // 8 + 4 * t
                    some = range(b0, min(b0 + 8, FT))
                    bank = psum[:, b, :].bitcast(BF16).rearrange("p (k n) -> p k n", n=P)
                    wait(pe, bank_read[b])
                    for k in some:
                        rows = min(P, FF - k * P)
                        e = PE(pe.transpose(bank[0:rows, k - b0, :], hid_i[t][:, k * P:k * P + rows], ident_b[:]))
                    wait(act, e)
                    full = [k for k in some if FF - k * P >= P]
                    for height, k0, count in [(P, full[0], len(full))] + (
                            [(FF % P, some[-1], 1)] if len(full) < len(some) else []):
                        bank_read[b] = ACTE(act.activation(
                            out_T[t][0:height, k0 * P:(k0 + count) * P].rearrange("p (k n) -> p k n", n=P),
                            bank[0:height, k0 - b0:k0 - b0 + count, :], ACT.Copy))
                wait(pe, bank_read[b], down_ready)
                for n in range(2):
                    b = 3 + 4 * n
                    wait(pe, bank_read[b])
                    for k in range(FT):
                        rows = min(P, FF - k * P)
                        mm = pe.matmul(psum[:, b, :], out_T[t][0:rows, k * P:(k + 1) * P],
                                       down[0:rows, 4 * n:4 * n + 4, k * P:(k + 1) * P], start=k == 0, stop=k == FT - 1)
                    e = PE(mm)
                    wait(dve, e)
                    at = slice(n * BANK, (n + 1) * BANK)
                    e = DVE(dve.scalar_tensor_tensor(out=xn[:, t, at], in0=psum[:, b, :],
                                                     scalar=act_scale[:, 4, t:t + 1], in1=ws_d[:, at],
                                                     op0=ALU.mult, op1=ALU.mult))
                    bank_read[b] = e
                    wait(dve, e)
                    x_ready = DVE(dve.tensor_tensor(x[:, t, at], xn[:, t, at], x[:, t, at], ALU.add))
        return finish()


def program(nc, a, out, stop=99):
    build(nc, a, out, stop)


def layouts(i):
    c = np.ascontiguousarray
    P_, KT = 128, 8

    def tiled(w, width):
        k, n = w.shape
        return c(w.reshape(k // P_, P_, n // width, width).transpose(2, 1, 0, 3).reshape(n // width, P_, -1))

    a = {"x": i["x"], "ident": np.eye(P_, dtype=np.float32)}
    a["wq0"] = tiled(i["L0_xattn_Wq"].T, 96)
    k0, k1 = i["L0_xattn_Wk"].T.reshape(1024, 4, 96), i["L1_xattn_Wk"].reshape(1024, 8, 32)
    packed = np.concatenate([k0, k1[:, :4]], axis=2).reshape(1024, 512)
    wkv = np.concatenate([packed, k1[:, 4:].reshape(1024, 128), i["L0_xattn_Wv"].T, i["L1_xattn_Wv"]], axis=1)
    a["wkv"] = c(wkv.reshape(KT, P_, 1280))
    ctx = i["ctx_4096"][0].reshape(16, 256, KT, P_)
    a["ctxT"] = c(ctx.transpose(0, 3, 2, 1).reshape(16, P_, KT * 256))
    wo0 = i["L0_xattn_Wo"].T.reshape(2, 8, 96, 2, 512)
    a["wo0"] = c(wo0.transpose(3, 0, 2, 1, 4).reshape(2, 2, 96, 8 * 512))
    for name, w in (("wq_a", i["L0_attn_w_q"].T), ("wk_a", i["L0_attn_w_k"].T), ("wv_a", i["L0_attn_w_v"].T),
                    ("wo_a", i["L0_attn_w_out"].T), ("wq1", i["L1_xattn_Wq"]), ("wo1", i["L1_xattn_Wo"]),
                    ("wq_b", i["L1_attn_Wq"]), ("wo_b", i["L1_attn_Wo"])):
        a[name] = tiled(w, 512)
    a["wkv_b"] = tiled(np.concatenate([i["L1_attn_Wk"], i["L1_attn_Wv"]], axis=1), 512)[0]
    a["route"] = tiled(np.concatenate([i["L0_ffn_route_w"], i["L0_ffn_A"].reshape(128, 1024)], axis=0).T, 136)[0]
    f = np.float32
    freq = f(1.0) / f(10000.0) ** (np.arange(0, 64, 2, dtype=f) / f(64))
    angles = np.repeat(np.arange(256, dtype=f)[:, None] * freq[None, :], 2, axis=1).reshape(2, P_, 64)
    a["cos_a"], a["sin_a"] = (c(g(angles).transpose(1, 0, 2)) for g in (np.cos, np.sin))
    a["cos_b"], a["sin_b"] = (c(i[n][:256].reshape(2, P_, 32).transpose(1, 0, 2))
                              for n in ("L1_attn_cos", "L1_attn_sin"))
    q = np.arange(P_)[:, None]
    keys = np.arange(2 * P_)[None, :]
    a["mask"] = np.where(np.concatenate([keys[:, :P_] <= q, keys <= q + P_], axis=1), f(0), f(-1e30)).astype(f)
    a["rank"] = np.tile(np.arange(8, 0, -1, dtype=f), (P_, 1))
    a["rms_weight"] = i["L1_ffn_rmsnorm_weight"]
    a["ffn_w0"], a["ffn_w1"], a["ffn_w2"] = i["L1_ffn_Wg"], i["L1_ffn_Wu"], i["L1_ffn_Wd"]
    a["lora_b"] = c(i["L0_ffn_Bw"].transpose(0, 2, 1).reshape(128, 1024))
    return a


def kernel(**inputs):
    from concourse import bacc
    from concourse.bass_utils import run_bass_kernel_spmd

    arrays = {f"in_{n}_dram": np.ascontiguousarray(v)
              for n, v in layouts({n: np.asarray(v) for n, v in inputs.items()}).items()}
    nc = bacc.Bacc("TRN2", target_bir_lowering=False, num_devices=1)
    a = {n[3:-5]: nc.dram_tensor(n, v.shape, mybir.dt.from_np(v.dtype), kind="ExternalInput").ap()
         for n, v in arrays.items()}
    out = nc.dram_tensor("out_0_dram", (1, 256, 1024), F32, kind="ExternalOutput").ap()
    program(nc, a, out)
    result = run_bass_kernel_spmd(nc, [arrays], core_ids=[0])
    return result.results[0]["out_0_dram"]
```

```python
from contextlib import ExitStack

import numpy as np

import concourse.bass as bass
from concourse import mybir

F32 = mybir.dt.float32
F32R = mybir.dt.float32r
BF16 = mybir.dt.bfloat16
ALU = mybir.AluOpType
ACT = mybir.ActivationFunctionType
AX_X = mybir.AxisListType.X

P = 128
BANK = 512
ROUND = 12582912.0
QMAX = 127.0


class Signal:

    def __init__(self, semaphore):
        self.semaphore, self.value = semaphore, 0

    def after(self, instruction, step=1):
        instruction.then_inc(self.semaphore, step)
        self.value += step
        return (self, self.value)


class Feed:

    def __init__(self, queue, wait, buffers, signals, pieces, first=()):
        self.queue, self.wait, self.buffers, self.signals = queue, wait, buffers, signals
        self.pieces, self.loaded, self.taken = pieces, [], 0
        for _ in range(min(len(buffers), len(pieces))):
            self.load(first)

    def load(self, events):
        n = len(self.loaded)
        if n == len(self.pieces):
            return
        slot = n % len(self.buffers)
        self.wait(self.queue, *events)
        for destination, source in self.pieces[n](self.buffers[slot]):
            event = self.signals[slot].after(self.queue.dma_start(destination, source), 16)
        self.loaded.append(event)

    def take(self):
        n = self.taken
        self.taken += 1
        return self.buffers[n % len(self.buffers)], self.loaded[n]

    def release(self, *events):
        self.load(events)


def build(nc, a, out, stop=99):
    T = 256
    D = 1024
    CTX = 4096
    TT, KT = T // P, D // P
    waited = {}

    with ExitStack() as ctx:
        def signal(name):
            return Signal(ctx.enter_context(nc.semaphore(name)))

        def wait(engine, *events):
            for event in events:
                if event is None:
                    continue
                s, value = event
                if waited.get((id(engine), id(s)), 0) < value:
                    engine.wait_ge(s.semaphore, value)
                    waited[(id(engine), id(s))] = value

        pe, act, dve, pool, sp = nc.tensor, nc.scalar, nc.vector, nc.gpsimd, nc.sync
        pe_done, act_done, dve_done, pool_done = (signal(f"{n}_done") for n in ("pe", "act", "dve", "pool"))
        PE, ACTE, DVE, POOL = pe_done.after, act_done.after, dve_done.after, pool_done.after

        def so_far(engine_done):
            return (engine_done, engine_done.value)

        def sb(stack, name, shape, dtype=F32):
            return stack.enter_context(nc.sbuf_tensor(name, shape, dtype))

        psum = ctx.enter_context(nc.psum_tensor("psum", [P, 8, BANK], F32))
        bank_read = [None] * 8
        const_in, x_in, small_dma = signal("const_in"), signal("x_in"), signal("small_dma")
        panel_in = [signal(f"panel_in{i}") for i in range(3)]

        x = sb(ctx, "x", [P, TT, D])
        ident = sb(ctx, "ident", [P, P])
        stats = sb(ctx, "stats", [P, TT, 2, 6])
        moments = sb(ctx, "moments", [P, TT, 2])
        tiny = sb(ctx, "tiny", [P, 8, TT])
        FF = 2752
        FT = -(-FF // P)
        NQ = 2 * FT + KT
        w_scale = sb(ctx, "w_scale", [P, NQ])
        w_inverse = sb(ctx, "w_inverse", [P, NQ])
        w_top = sb(ctx, "w_top", [P, NQ])
        ident_b = sb(ctx, "ident_b", [P, P], BF16)
        scales_set = POOL(pool.memset(w_scale[:], 1.0))
        x_in.after(sp.dma_start(x[:], a["x"].rearrange("a (t p) d -> p (a t) d", p=P)), 16)
        const_ready = const_in.after(sp.dma_start(ident[:], a["ident"]), 16)
        wait(act, const_ready)
        ident_ready = ACTE(act.activation(ident_b[:], ident[:], ACT.Copy))
        x_ready = (x_in, 16)
        stats_ready = None

        def inverse_root(variance, eps, ready):
            v, sd, r, w = (tiny[:, i, :] for i in range(4))
            wait(dve, ready)
            e = DVE(dve.tensor_scalar(v, variance, 1.0, eps, ALU.mult, ALU.add))
            wait(act, e)
            e = ACTE(act.activation(sd, v, ACT.Sqrt))
            wait(dve, e)
            wait(dve, DVE(dve.reciprocal(r, sd)))
            wait(dve, DVE(dve.tensor_tensor(w, v, r, ALU.mult)))
            wait(dve, DVE(dve.tensor_tensor(w, w, r, ALU.mult)))
            wait(dve, DVE(dve.tensor_scalar(w, w, -0.5, 1.5, ALU.mult, ALU.add)))
            return r, DVE(dve.tensor_tensor(r, r, w, ALU.mult))

        def take_stats(t, h):
            return DVE(dve.bn_stats(stats[:, t, h, :], x[:, t, h * BANK:(h + 1) * BANK]))

        def layernorm(xn, free=()):
            wait(dve, stats_ready, *free)
            for t in range(TT):
                e = DVE(dve.bn_aggr(moments[:, t, :], stats[:, t].rearrange("p h s -> p (h s)")))
            r, e = inverse_root(moments[:, :, 1], 1e-5, e)
            wait(dve, e)
            for t in range(TT):
                e = DVE(dve.tensor_scalar(xn[:, t, :], x[:, t, :], moments[:, t, 0:1], r[:, t:t + 1],
                                          ALU.subtract, ALU.mult))
            return e

        def turn(src, dst, ready, banks, cols=D, free=()):
            done = []
            wait(pe, ready, const_ready)
            for i in range(cols // P // 2):
                b = banks[i % len(banks)]
                wait(pe, bank_read[b])
                for j in range(2):
                    for t in range(TT):
                        k = 2 * i + j
                        c = (j * TT + t) * P
                        e = PE(pe.transpose(psum[:, b, c:c + P], src[:, t, k * P:k * P + P], ident[:]))
                copy = psum[:, b, :].rearrange("p (j n) -> p j n", j=2)
                if i % 2:
                    wait(dve, e, *free)
                    bank_read[b] = DVE(dve.tensor_copy(dst[:, 2 * i:2 * i + 2, :], copy))
                else:
                    wait(act, e, *free)
                    bank_read[b] = ACTE(act.activation(dst[:, 2 * i:2 * i + 2, :], copy, ACT.Copy))
                done.append(bank_read[b])
            return done

        def halve(src, high, low, ready, free=(), low_free=()):
            wait(act, *ready, *free)
            e_high = ACTE(act.activation(high, src, ACT.Copy))
            wait(dve, e_high, *free, *low_free)
            return e_high, DVE(dve.tensor_tensor(low, src, high.bitcast(F32), ALU.subtract))

        def turn_split(src, high, low, ready, banks, free=()):
            wait(pe, ready, const_ready)
            for i in range(KT // 2):
                b = banks[i % len(banks)]
                wait(pe, bank_read[b])
                for j in range(2):
                    for t in range(TT):
                        k = 2 * i + j
                        c = (j * TT + t) * P
                        e = PE(pe.transpose(psum[:, b, c:c + P], src[:, t, k * P:k * P + P], ident[:]))
                bank = psum[:, b, :].rearrange("p (j n) -> p j n", j=2)
                _, bank_read[b] = halve(bank, high[:, 2 * i:2 * i + 2, :], low[:, 2 * i:2 * i + 2, :], [e], free)
            return [bank_read[b]]

        class Panel:

            def __init__(self, tile, rows, k=P):
                self.tile, self.rows, self.k = tile, rows, k

            def ap(self, r, width):
                return self.tile[0:self.k, r * width:(r + 1) * width]

        class Panels:

            def __init__(self, feed, shapes):
                self.feed, self.shapes, self.n = feed, shapes, 0

            def take(self):
                tile, arrived = self.feed.take()
                rows, k = self.shapes[self.n]
                self.n += 1
                return Panel(tile, rows, k), arrived

            def release(self, *events):
                self.feed.release(*events)

        class Splitter:
            UNIT = 2

            def __init__(self, tiles, panels, count):
                self.tiles, self.panels, self.left = tiles, panels, count
                self.ready, self.read, self.n, self.taken = [], [None] * len(tiles), 0, 0
                self.panel, self.row = None, 0
                for _ in tiles:
                    self.prepare()

            def prepare(self):
                if self.panel is None:
                    if not self.left:
                        return
                    self.left -= 1
                    (self.panel, self.arrived), self.row = self.panels.take(), 0
                k, at = self.panel.k, slice(self.row * BANK, (self.row + self.UNIT) * BANK)
                slot = self.n % len(self.tiles)
                high, low = (z[0:k, :] for z in self.tiles[slot])
                _, e = halve(self.panel.tile[0:k, at], high, low, [self.arrived], [self.read[slot]])
                self.ready.append((Panel(self.tiles[slot][0], self.UNIT, k), Panel(self.tiles[slot][1], self.UNIT, k), e))
                self.n += 1
                self.row += self.UNIT
                if self.row == self.panel.rows:
                    self.panels.release(e)
                    self.panel = None

            def take(self):
                return self.ready.pop(0)

            def release(self, event):
                self.read[self.taken % len(self.tiles)] = event
                self.taken += 1
                self.prepare()

        def linear_split(stationary, ready, splitter, halves, banks, consume, beside=None):
            wait(pe, *ready)
            for n in range(halves):
                own = [banks[(TT * n + t) % len(banks)] for t in range(TT)]
                wait(pe, *(bank_read[b] for b in own))
                k = 0
                while k < len(stationary):
                    w_high, w_low, arrived = splitter.take()
                    wait(pe, arrived)
                    for r in range(w_high.rows):
                        high, low = stationary[k]
                        for t in range(TT):
                            o, ts = psum[:, own[t], :], slice(t * P, (t + 1) * P)
                            pe.matmul(o, high[:, ts], w_high.ap(r, BANK), start=k == 0, stop=False)
                            pe.matmul(o, high[:, ts], w_low.ap(r, BANK), start=False, stop=False)
                            mm = pe.matmul(o, low[:, ts], w_high.ap(r, BANK), start=False,
                                           stop=k == len(stationary) - 1)
                        k += 1
                    e = PE(mm)
                    if k < len(stationary):
                        splitter.release(e)
                        if beside and k in (4, 8):
                            beside.pop(0)()
                for t in range(TT):
                    bank_read[own[t]] = consume(n, t, psum[:, own[t], :], e)
                splitter.release(e)
                if beside and len(stationary) == 8:
                    beside.pop(0)()

        def linear(stationary, ready, panels, halves, banks, consume, width=BANK):
            wait(pe, *ready)
            for n in range(halves):
                own = [banks[(TT * n + t) % len(banks)] for t in range(TT)]
                wait(pe, *(bank_read[b] for b in own))
                k = 0
                while k < len(stationary):
                    w, arrived = panels.take()
                    wait(pe, arrived)
                    for r in range(w.rows):
                        for t in range(TT):
                            mm = pe.matmul(psum[:, own[t], 0:width], stationary[k][:, t * P:t * P + P],
                                           w.ap(r, width), start=k == 0, stop=k == len(stationary) - 1)
                        k += 1
                    e = PE(mm)
                    panels.release(e)
                for t in range(TT):
                    bank_read[own[t]] = consume(n, t, psum[:, own[t], 0:width], e)

        def add_to_x(n, t, product, event):
            nonlocal x_ready, stats_ready
            wait(dve, event)
            block = x[:, t, n * BANK:(n + 1) * BANK]
            x_ready = DVE(dve.tensor_tensor(block, product, block, ALU.add))
            read = x_ready
            wait(dve, x_ready)
            stats_ready = take_stats(t, n)
            return read

        def invert_row(rows, result, turned, few, ready):
            n = rows.shape[-1]
            wait(dve, ready)
            read = DVE(dve.transpose(turned, rows))
            wait(dve, read)
            wait(dve, DVE(dve.reciprocal(few, turned.rearrange("p (b j) -> p b j", j=32)[:, :, 0])))
            return read, DVE(dve.transpose(result, few.unsqueeze(2).broadcast_to([32, n // 32, 32])))

        H0, KV0, HD0 = 16, 4, 96
        G0 = H0 // KV0
        KV1, HD1 = 8, 32
        G1 = 4
        S0 = CTX + T
        CH = 256
        NCH = S0 // CH
        VW = P
        NS0 = S0 // P
        V1W = KV1 // 2 * 3 * HD1

        def scratch(name, shape, dtype):
            return nc.dram_tensor(name, shape, dtype, kind="Internal").ap()

        k0_high = scratch("k0_high", [KV0, HD0, S0], F32)
        k0_low = scratch("k0_low", [KV0, HD0, S0], F32)
        k1_high = scratch("k1_high", [KV1 * HD1, CTX], F32)
        k1_low = scratch("k1_low", [KV1 * HD1, CTX], F32)
        v0_high = scratch("v0_high", [KV0, P, NS0, VW], F32)
        v0_low = scratch("v0_low", [KV0, P, NS0, VW], F32)
        v1_dram = scratch("v1_dram", [P, CTX // P, V1W], F32)

        attn0 = ExitStack()
        q_high = sb(attn0, "q_high", [HD0 + 1, H0 * T], F32R)
        q_low = sb(attn0, "q_low", [HD0 + 1, H0 * T], F32R)
        top0 = sb(attn0, "top0", [P, KV0 * G0 * TT, NCH])
        neg_top0 = sb(attn0, "neg_top0", [P, KV0 * G0 * TT])
        top_high = sb(attn0, "top_high", [32, P], F32R)
        top_low = sb(attn0, "top_low", [32, P], F32R)

        kv_spilled = []
        with ExitStack() as phase:
            xnT = sb(phase, "xnT_ab", [P, KT, T])
            w_high = sb(phase, "w_high", [P, KT, 1280], F32R)
            w_low = sb(phase, "w_low", [P, KT, 1280], F32R)
            staged = [sb(phase, f"staged{i}", [P, 1280]) for i in range(3)]
            k_out = [[sb(phase, f"k_out{i}{p}", [P, 2, CH], F32R) for p in "hl"] for i in range(3)]
            v0_out = [[sb(phase, f"v0_out{i}{p}", [P, KV0, VW], F32R) for p in "hl"] for i in range(2)]
            v1_out = [sb(phase, f"v1_out{i}", [P, V1W]) for i in range(2)]
            stage_in = [signal(f"stage_in{i}") for i in range(3)]
            k_sent = [signal(f"k_sent{i}") for i in range(3)]
            v0_sent = [signal(f"v0_sent{i}") for i in range(2)]
            v1_sent = [signal(f"v1_sent{i}") for i in range(2)]

            for high, low in v0_out:
                POOL(pool.memset(high[:, :, HD0:VW].bitcast(F32), 1.0))
                POOL(pool.memset(low[:, :, HD0:VW].bitcast(F32), 0.0))
            for v in v1_out:
                ones_set = POOL(pool.memset(v[:], 1.0))

            def q_piece(h):
                return lambda s: [(s[:, 0:KT * HD0], a["wq0"][h])]

            def w_piece(k):
                return lambda s: [(s[:], a["wkv"][k])]

            def c_piece(c, half):
                return lambda s: [(s[:, 0:4 * CH], a["ctxT"][c, :, half * 4 * CH:(half + 1) * 4 * CH])]

            order = []
            for i in range(KT):
                order += [q_piece(2 * i), q_piece(2 * i + 1), w_piece(i)]
            for c in range(CTX // CH):
                order += [c_piece(c, 0), c_piece(c, 1)]
            stage = Feed(sp, wait, staged, stage_in, order)

            with ExitStack() as early:
                xn = sb(early, "xn_ab", [P, TT, D])
                wait(dve, x_ready)
                for t in range(TT):
                    for h in range(2):
                        stats_ready = take_stats(t, h)
                normed = layernorm(xn)
                turned = turn(xn, xnT, normed, [0, 1, 2, 3])
            c_high = [sb(phase, f"c_high{i}", [P, KT, CH], F32R) for i in range(2)]
            c_low = [sb(phase, f"c_low{i}", [P, KT, CH], F32R) for i in range(2)]
            queries = []
            for h in range(H0):
                b = 4 + h % 4
                w, arrived = stage.take()
                wait(pe, arrived, bank_read[b], *turned)
                for k in range(KT):
                    mm = pe.matmul(psum[0:HD0, b, 0:T], w[:, k * HD0:(k + 1) * HD0], xnT[:, k, :],
                                   start=k == 0, stop=k == KT - 1)
                e = PE(mm)
                stage.release(e)
                cols = slice(h * T, (h + 1) * T)
                wait(act, e)
                e_high = ACTE(act.activation(q_high[0:HD0, cols], psum[0:HD0, b, 0:T], ACT.Copy))
                wait(dve, e_high)
                bank_read[b] = DVE(dve.tensor_tensor(q_low[0:HD0, cols], psum[0:HD0, b, 0:T],
                                                     q_high[0:HD0, cols].bitcast(F32), ALU.subtract))
                queries.append(bank_read[b])
                if h % 2:
                    i = h // 2
                    w, arrived = stage.take()
                    wait(act, arrived)
                    e = ACTE(act.activation(w_high[:, i, :], w[:], ACT.Copy))
                    wait(dve, e)
                    weights_split = DVE(dve.tensor_tensor(w_low[:, i, :], w[:],
                                                          w_high[:, i, :].bitcast(F32), ALU.subtract))
                    stage.release(weights_split)

            chunk_read = [None] * NCH

            def split_chunk(c):
                high, low = c_high[c % 2], c_low[c % 2]
                free = chunk_read[c - 2] if c >= 2 else None
                for half in range(2):
                    ks = slice(4 * half, 4 * half + 4)
                    if c < CTX // CH:
                        s, arrived = stage.take()
                        src = s[:, 0:4 * CH].rearrange("p (k n) -> p k n", k=4)
                    else:
                        src, arrived = xnT[:, ks, :], None
                    wait(act, arrived, free)
                    e = ACTE(act.activation(high[:, ks, :], src, ACT.Copy))
                    wait(dve, e, free)
                    e = DVE(dve.tensor_tensor(low[:, ks, :], src, high[:, ks, :].bitcast(F32), ALU.subtract))
                    if c < CTX // CH:
                        stage.release(e)
                return e

            bank_turn = 0

            def next_bank():
                nonlocal bank_turn
                bank_turn += 1
                return (bank_turn - 1) % 8

            k_slot = v_slot = 0
            k_slot_free = [()] * 3
            split = [split_chunk(0)]
            for c in range(NCH):
                latents = c == NCH - 1
                if not latents:
                    split.append(split_chunk(c + 1))
                high, low = c_high[c % 2], c_low[c % 2]
                at = slice(c * CH, (c + 1) * CH)
                wait(pe, split[c], weights_split)
                pending = []

                def take_maxima(jobs):
                    for pair, slot, e_high in jobs:
                        wait(pe, e_high, *queries)
                        for j in range(2):
                            head = 2 * pair + j
                            for g in range(0, G0 * TT, 2):
                                b = next_bank()
                                wait(pe, bank_read[b])
                                for i in range(2):
                                    q0 = head * G0 * T + (g + i) * P
                                    mm = pe.matmul(psum[:, b, i * CH:(i + 1) * CH],
                                                   q_high[0:HD0, q0:q0 + P],
                                                   k_out[slot][0][0:HD0, j, :], start=True, stop=True)
                                e = PE(mm)
                                wait(dve, e)
                                r0 = head * G0 * TT + g
                                bank_read[b] = DVE(dve.tensor_reduce(
                                    top0[:, r0:r0 + 2, c], psum[:, b, :].rearrange("p (i n) -> p i n", i=2),
                                    AX_X, ALU.max))
                        k_slot_free[slot] = k_slot_free[slot] + (e,)

                for pair in range(2 if latents else 3):
                    tiles = (0, 1) if pair < 2 else (0,)
                    m = HD0 if latents else P
                    b = next_bank()
                    wait(pe, bank_read[b])
                    for j in tiles:
                        col = (2 * pair + j) * P
                        for k in range(KT):
                            o = psum[0:m, b, j * CH:(j + 1) * CH]
                            pe.matmul(o, w_high[:, k, col:col + m], high[:, k, :], start=k == 0, stop=False)
                            pe.matmul(o, w_high[:, k, col:col + m], low[:, k, :], start=False, stop=False)
                            mm = pe.matmul(o, w_low[:, k, col:col + m], high[:, k, :], start=False,
                                           stop=k == KT - 1)
                    e = PE(mm)
                    slot = k_slot % 3
                    k_slot += 1
                    n = len(tiles)
                    src = psum[0:m, b, 0:n * CH].rearrange("p (j n) -> p j n", j=n)
                    kh, kl = (k_out[slot][i][0:m, 0:n, :] for i in range(2))
                    wait(act, e, *k_slot_free[slot])
                    e_high = ACTE(act.activation(kh, src, ACT.Copy))
                    wait(dve, e_high, *k_slot_free[slot])
                    bank_read[b] = DVE(dve.tensor_tensor(kl, src, kh.bitcast(F32), ALU.subtract))
                    wait(sp, bank_read[b])
                    for part, k0d, k1d in ((0, k0_high, k1_high), (1, k0_low, k1_low)):
                        o = k_out[slot][part][:].bitcast(F32)
                        if pair < 2:
                            e = k_sent[slot].after(sp.dma_start(
                                k0d[2 * pair:2 * pair + 2, :, at].rearrange("h d n -> d h n"), o[0:HD0, :, :]), 16)
                            if not latents:
                                e = k_sent[slot].after(sp.dma_start(
                                    k1d[2 * pair * HD1:(2 * pair + 2) * HD1, at].rearrange(
                                        "(h d) n -> d h n", d=HD1), o[HD0:P, :, :]), 16)
                        else:
                            e = k_sent[slot].after(sp.dma_start(k1d[P:2 * P, at], o[:, 0, :]), 16)
                    k_slot_free[slot] = (e,)
                    if pending:
                        take_maxima(pending)
                        pending = []
                    if pair < 2:
                        pending = [(pair, slot, e_high)]
                take_maxima(pending)

                for s in range(CH // P):
                    ts = slice(s * P, (s + 1) * P)
                    b0, b1 = next_bank(), next_bank()
                    wait(pe, bank_read[b0], bank_read[b1])
                    outs = [(psum[:, b0, 0:KV0 * HD0], slice(640, 1024))]
                    if not latents:
                        outs.append((psum[:, b1, 0:KV1 * HD1], slice(1024, 1280)))
                    for k in range(KT):
                        for tokens, weights in ((high, w_high), (high, w_low), (low, w_high)):
                            for o, cols in outs:
                                mm = pe.matmul(o, tokens[:, k, ts], weights[:, k, cols],
                                               start=k == 0 and tokens is high and weights is w_high,
                                               stop=k == KT - 1 and tokens is low)
                    e = PE(mm)
                    if s == CH // P - 1:
                        chunk_read[c] = e
                    slot = v_slot % 2
                    v_slot += 1
                    row = c * (CH // P) + s
                    _, bank_read[b0] = halve(
                        outs[0][0].rearrange("p (h d) -> p h d", h=KV0), v0_out[slot][0][:, :, 0:HD0],
                        v0_out[slot][1][:, :, 0:HD0], [e], [ones_set, so_far(v0_sent[slot])])
                    wait(sp, bank_read[b0])
                    for part, v0d in enumerate((v0_high, v0_low)):
                        v0_sent[slot].after(sp.dma_start(v0d[:, :, row, :].rearrange("h p d -> p h d"),
                                                         v0_out[slot][part][:].bitcast(F32)), 16)
                    if not latents:
                        wait(dve, e, ones_set, (v1_sent[slot], v1_sent[slot].value))
                        bank_read[b1] = DVE(dve.tensor_copy(
                            v1_out[slot][:].rearrange("p (q b d) -> p q b d", b=3, d=HD1)[:, :, 0:3:2, :],
                            outs[1][0].rearrange("p (q b d) -> p q b d", b=2, d=HD1)))
                        wait(sp, bank_read[b1])
                        v1_sent[slot].after(sp.dma_start(v1_dram[:, row, :], v1_out[slot][:]), 16)
            kv_spilled = [(s, s.value) for s in (*k_sent, *v0_sent, *v1_sent)]

            wait(dve, bank_read[(bank_turn - 1) % 8], *bank_read)
            e = DVE(dve.tensor_reduce(neg_top0[:], top0[:], AX_X, ALU.max, negate=True))
            b = next_bank()
            wait(pe, e, bank_read[b])
            e = PE(pe.transpose(psum[0:32, b, 0:P], neg_top0[:], ident[:]))
            wait(act, e)
            e = ACTE(act.activation(top_high[:], psum[0:32, b, 0:P], ACT.Copy))
            wait(dve, e)
            bank_read[b] = DVE(dve.tensor_tensor(top_low[:], psum[0:32, b, 0:P], top_high[:].bitcast(F32),
                                                 ALU.subtract))
            wait(sp, bank_read[b], e)
            for q, top in ((q_high, top_high), (q_low, top_low)):
                tops_placed = small_dma.after(sp.dma_start(
                    q[HD0:HD0 + 1, :].bitcast(F32).rearrange("o (r n) -> o r n", n=P), top[:].bitcast(F32)), 16)
            last_of_b = [so_far(pe_done), so_far(act_done), so_far(dve_done), *kv_spilled]

        q_dram = scratch("q_dram", [2 * FT, P, KT * P], BF16)
        qd_dram = scratch("qd_dram", [KT, P, FT * P], BF16)
        ws_dram = scratch("ws_dram", [NQ, P], F32)
        q_spilled = [signal(f"q_spilled{i}") for i in range(2)]
        wf_in = [signal(f"wf_in{i}") for i in range(2)]

        class Quantiser:

            def __init__(self, stack, banks):
                self.rows = [sb(stack, f"wf_rows{i}", [P, FF]) for i in range(2)]
                self.ints = [sb(stack, f"wf_ints{i}", [P, FF], BF16) for i in range(2)]
                self.turned = [sb(stack, f"wf_turned{i}", [P, FT * P], BF16) for i in range(2)]
                self.top_first = sb(stack, "top_first", [P, 1])
                self.turned_read, self.ints_read = [None] * 2, [None] * 2
                self.banks, self.n, self.rounded, self.shifted = banks, 0, {}, {}

            def start(self, first):
                pieces = [self.piece(n) for n in range(NQ)]
                self.feed = Feed(sp, wait, self.rows, wf_in, pieces, first)

            def shape(self, n):
                if n < 2 * FT:
                    i = n % FT
                    return n // FT, i, min(P, FF - i * P), D
                return 2, n - 2 * FT, P, FF

            def piece(self, n):
                which, i, rows, cols = self.shape(n)
                return lambda tile: [(tile[0:rows, 0:cols], a[f"ffn_w{which}"][i * P:i * P + rows, :])]

            def reduce_first(self, n):
                _, _, rows, cols = self.shape(n)
                self.first_part = cols // 3 * 2
                w, arrived = self.feed.take()
                wait(dve, arrived)
                self.taken = w, DVE(dve.tensor_reduce(self.top_first[:], w[:, 0:self.first_part], AX_X, ALU.max,
                                                      apply_absolute_value=True))

            def quantise(self, n):
                which, _, rows, cols = self.shape(n)
                top, scale, inv = (z[0:rows, n:n + 1] for z in (w_top, w_scale, w_inverse))
                if which == 2:
                    w, e = self.taken
                    wait(dve, DVE(dve.tensor_reduce(top, w[:, self.first_part:cols], AX_X, ALU.max,
                                                    apply_absolute_value=True)), e)
                    wait(dve, DVE(dve.tensor_tensor(top, top, self.top_first[:], ALU.max)))
                    w = w[:, 0:cols]
                else:
                    w, arrived = self.feed.take()
                    w = w[0:rows, 0:cols]
                    wait(dve, arrived, scales_set)
                    wait(dve, DVE(dve.tensor_reduce(top, w, AX_X, ALU.max, apply_absolute_value=True)))
                wait(dve, DVE(dve.tensor_scalar(scale, top, 1.0 / QMAX, 1e-8, ALU.mult, ALU.max)))
                e = DVE(dve.reciprocal(inv, scale))
                wait(pool, e, so_far(pool_done))
                self.shifted[n] = (w, POOL(pool.tensor_scalar(w, w, inv, ROUND, ALU.mult, ALU.add)))

            def settle(self, n):
                _, _, rows, cols = self.shape(n)
                w, e = self.shifted.pop(n)
                wait(pool, e, self.ints_read[n % 2])
                self.rounded[n] = POOL(pool.tensor_scalar(self.ints[n % 2][0:rows, 0:cols], w, -ROUND, 1.0,
                                                          ALU.add, ALU.mult))
                self.feed.release(self.rounded[n])

            def turn(self, n, engine):
                which, i, rows, cols = self.shape(n)
                ints, out_tile = self.ints[n % 2], self.turned[n % 2]
                blocks = -(-cols // P)
                wait(pe, self.rounded[n], ident_ready, const_ready)
                for b0 in range(0, blocks, 8):
                    b = self.banks[(b0 // 8 + n) % 2]
                    some = range(b0, min(b0 + 8, blocks))
                    bank = psum[:, b, :].bitcast(BF16).rearrange("p (k n) -> p k n", n=P)
                    wait(pe, bank_read[b])
                    for k in some:
                        width = min(P, cols - k * P)
                        e = PE(pe.transpose(bank[0:width, k - b0, 0:rows], ints[0:rows, k * P:k * P + width],
                                            ident_b[0:rows, 0:rows]))
                    full = [k for k in some if cols - k * P >= P]
                    jobs = [(P, full[0], len(full))] if full else []
                    if len(full) < len(some):
                        jobs.append((cols % P, some[-1], 1))
                    for height, k0, count in jobs:
                        dst = out_tile[0:height, k0 * P:(k0 + count) * P].rearrange("p (k n) -> p k n", n=P)[:, :, 0:rows]
                        src = bank[0:height, k0 - b0:k0 - b0 + count, 0:rows]
                        if engine is act:
                            wait(act, e, self.turned_read[n % 2])
                            done = ACTE(act.activation(dst, src, ACT.Copy))
                        else:
                            wait(dve, e, self.turned_read[n % 2])
                            done = DVE(dve.tensor_copy(dst, src))
                    bank_read[b] = done
                self.ints_read[n % 2] = e
                wait(sp, done)
                if which < 2:
                    pairs = [(q_dram[n], out_tile[:, 0:KT * P])] if rows == P else [
                        (q_dram[n].rearrange("p (k n) -> p k n", n=P)[:, :, 0:rows],
                         out_tile[:, 0:KT * P].rearrange("p (k n) -> p k n", n=P)[:, :, 0:rows])]
                else:
                    whole = FF // P * P
                    pairs = [(qd_dram[i, :, 0:whole], out_tile[:, 0:whole]),
                             (qd_dram[i, 0:FF - whole, whole:], out_tile[0:FF - whole, whole:])]
                for destination, source in pairs:
                    self.turned_read[n % 2] = q_spilled[n % 2].after(sp.dma_start(destination, source), 16)

            def turn_last(self):
                if 0 <= self.n - 2 < NQ:
                    self.turn(self.n - 2, dve)
                if 0 <= self.n - 1 < NQ:
                    self.settle(self.n - 1)

            def step(self, n):
                if self.finished():
                    return
                if self.n < 2 * FT:
                    if n % 2 == 1:
                        self.turn_last()
                        self.quantise(self.n)
                        self.n += 1
                elif n % 4 == 1:
                    self.turn_last()
                elif n % 4 == 2 and self.n < NQ:
                    self.reduce_first(self.n)
                elif n % 4 == 3:
                    if self.n < NQ:
                        self.quantise(self.n)
                    self.n += 1

            def finished(self):
                return self.n > NQ + 1

        panel_stack = ExitStack()
        panel_tiles = [panel_stack.enter_context(nc.sbuf_tensor(f"panel{i}", [P, KT // 2 * BANK], F32, side="right"))
                       for i in range(3)]
        plan = []

        def panel(source, rows, width, k=P):
            plan.append((source, rows, width, k))

        def halved(name, rows=KT, k=P):
            for half in range(2):
                for first in range(0, rows, 4):
                    panel(a[name][half, :, first * BANK:(first + 4) * BANK], 4, BANK, k)

        halved("wo0", H0, HD0)
        for name in ("wq_a", "wk_a", "wv_a", "wo_a"):
            halved(name)
        panel(a["route"], KT, 136)
        panel(a["lora_b"], 2, BANK)
        for name in ("wq1", "wo1", "wq_b"):
            halved(name)
        for first in (0, 4):
            panel(a["wkv_b"][:, first * BANK:(first + 4) * BANK], 4, BANK)
        halved("wo_b")

        def panel_piece(source, rows, width, k):
            return lambda tile: [(tile[0:k, 0:rows * width], source)]

        panels = Panels(Feed(sp, wait, panel_tiles, panel_in, [panel_piece(*p) for p in plan], first=last_of_b),
                        [(rows, k) for _, rows, _, k in plan])

        def split_tiles(stack, name, slots):
            return [[stack.enter_context(nc.sbuf_tensor(f"{name}{i}{part}", [P, Splitter.UNIT * BANK], F32R,
                                                        side="right")) for part in "hl"] for i in range(slots)]

        split_stack = ExitStack()
        with ExitStack() as phase:
            SC = 512
            key_high = [sb(phase, f"key_high{i}", [HD0 + 1, SC], F32R) for i in range(4)]
            key_low = [sb(phase, f"key_low{i}", [HD0, SC], F32R) for i in range(4)]
            value_high = [sb(phase, f"value_high{i}", [P, SC // P, VW], F32R) for i in range(4)]
            value_low = [sb(phase, f"value_low{i}", [P, SC // P, VW], F32R) for i in range(4)]
            probs = [sb(phase, f"probs{i}", [P, G0 * T]) for i in range(2)]
            probs_high = [sb(phase, f"probs_high{i}", [P, G0 * T], F32R) for i in range(3)]
            probs_low = [sb(phase, f"probs_low{i}", [P, G0 * T], F32R) for i in range(3)]
            raw = sb(phase, "raw0", [HD0, G0 * T])
            sums = sb(phase, "sums0", [32, G0 * T])
            few = sb(phase, "few0", [32, G0 * T // 32])
            inverse = sb(phase, "inverse0", [HD0, G0 * T])
            kv_in = [signal(f"kv_in{i}") for i in range(4)]
            quantiser_stack = ExitStack()
            quantiser = Quantiser(quantiser_stack, (6, 7))
            wait(pool, *last_of_b)
            for k in key_high:
                wait(pool, so_far(pool_done))
                ones_set = POOL(pool.memset(k[HD0:HD0 + 1, :].bitcast(F32), 1.0))

            def kv_piece(kv, first):
                n = min(SC, S0 - first)

                def dmas(slot):
                    high, low, v_high, v_low = slot
                    return [(high[0:HD0, 0:n].bitcast(F32), k0_high[kv, :, first:first + n]),
                            (low[:, 0:n].bitcast(F32), k0_low[kv, :, first:first + n]),
                            (v_high[:, 0:n // P, :].bitcast(F32), v0_high[kv, :, first // P:(first + n) // P, :]),
                            (v_low[:, 0:n // P, :].bitcast(F32), v0_low[kv, :, first // P:(first + n) // P, :])]
                return dmas

            pieces = [kv_piece(kv, first) for kv in range(KV0) for first in range(0, S0, SC)]
            feed = Feed(sp, wait, list(zip(key_high, key_low, value_high, value_low)), kv_in, pieces,
                        first=last_of_b)
            quantiser.start(last_of_b)
            steps = [(kv, s) for kv in range(KV0) for s in range(NS0)]
            low_done, pv_done, held = {}, {}, {}
            scale = float(1.0 / np.sqrt(np.float32(HD0)))

            def scores(n):
                kv, s = steps[n]
                if s % (SC // P) == 0:
                    held["now"] = feed.take()
                (high, low, *held[n]), arrived = held["now"]
                wait(pe, arrived, tops_placed, ones_set)
                at = slice(s % 4 * P, s % 4 * P + P)
                for half in range(2):
                    b = 2 * (n % 2) + half
                    wait(pe, bank_read[b])
                    q = slice(kv * G0 * T + half * BANK, kv * G0 * T + (half + 1) * BANK)
                    pe.matmul(psum[:, b, :], high[:, at], q_high[:, q], start=True, stop=False)
                    pe.matmul(psum[:, b, :], high[:, at], q_low[:, q], start=False, stop=False)
                    mm = pe.matmul(psum[:, b, :], low[:, at], q_high[0:HD0, q], start=False, stop=True)
                e = PE(mm)
                both = psum[:, 2 * (n % 2):2 * (n % 2) + 2, :].rearrange("p b n -> p (b n)")
                wait(act, e, pv_done.get(n - 3), low_done.get(n - 2))
                ACTE(act.activation(probs_high[n % 3][:], both, ACT.Exp, scale=scale))
                e = ACTE(act.activation(probs[n % 2][:], both, ACT.Exp, scale=scale))
                bank_read[2 * (n % 2)] = bank_read[2 * (n % 2) + 1] = e
                wait(dve, e, pv_done.get(n - 3))
                low_done[n] = DVE(dve.tensor_tensor(probs_low[n % 3][:], probs[n % 2][:],
                                                    probs_high[n % 3][:].bitcast(F32), ALU.subtract))

            def weigh(n):
                kv, s = steps[n]
                wait(pe, low_done[n])
                v_high, v_low = (v[:, s % 4, :] for v in held.pop(n))
                for half in range(2):
                    wait(pe, bank_read[4 + half])
                    o, cols = psum[:, 4 + half, :], slice(half * BANK, (half + 1) * BANK)
                    p_high, p_low = probs_high[n % 3][:, cols], probs_low[n % 3][:, cols]
                    pe.matmul(o, v_high, p_high, start=s == 0, stop=False)
                    pe.matmul(o, v_high, p_low, start=False, stop=False)
                    halves_done[half] = PE(pe.matmul(o, v_low, p_high, start=False, stop=s == NS0 - 1))
                pv_done[n] = halves_done[1]
                if s % 4 == 3 or s == NS0 - 1:
                    feed.release(pv_done[n])
                if s == NS0 - 1:
                    for half in range(2):
                        cols = slice(half * BANK, (half + 1) * BANK)
                        wait(act, halves_done[half], normalised[0])
                        e_raw = ACTE(act.activation(raw[:, cols], psum[0:HD0, 4 + half, :], ACT.Copy))
                        read, inverted = invert_row(psum[HD0:P, 4 + half, :], inverse[0:32, cols], sums[:, cols],
                                                    few[:, half * 16:(half + 1) * 16], e_raw)
                        bank_read[4 + half] = read
                    wait(dve, inverted)
                    for row in (32, 64):
                        e = DVE(dve.tensor_copy(inverse[row:row + 32, :], inverse[0:32, :]))
                    wait(dve, e)
                    e = DVE(dve.tensor_tensor(raw[:], raw[:], inverse[:], ALU.mult))
                    cols = slice(kv * G0 * T, (kv + 1) * G0 * T)
                    later.append((lambda cols=cols, e=e: halve(raw[:], q_high[0:HD0, cols], q_low[0:HD0, cols], [e])))

            normalised, halves_done, later = [None], [None, None], []
            splitter = None
            scores(0)
            scores(1)
            for n in range(len(steps)):
                if n + 2 < len(steps):
                    scores(n + 2)
                if later and steps[n][1] in (2, NS0 - 1):
                    _, normalised[0] = later.pop(0)()
                weigh(n)
                quantiser.step(n)
                if quantiser.finished() and not splitter:
                        q_all_spilled = [(s, s.value) for s in q_spilled]
                        quantiser_stack.close()
                        wait(act, *quantiser.turned_read, *quantiser.ints_read)
                        splitter = Splitter(split_tiles(split_stack, "panel_ab", 4), panels, 8 + 16)
            _, normalised[0] = later.pop(0)()
            attended = normalised[0]
            last_of_c = [attended, pv_done[len(steps) - 1]]

        heads = [slice(h * T, (h + 1) * T) for h in range(H0)]
        linear_split([(q_high[0:HD0, h], q_low[0:HD0, h]) for h in heads], [attended], splitter, 2, [0, 1, 2, 3],
                     add_to_x)
        attn0.close()
        done = [x_ready, *last_of_c, so_far(pe_done), so_far(act_done)]
        out_done = signal("out_done")

        def finish():
            wait(sp, x_ready)
            e = out_done.after(sp.dma_start(out.rearrange("a (t p) d -> p (a t) d", p=P), x[:]), 16)
            wait(sp, e)

        if stop <= 1:
            return finish()

        mask_b = sb(ctx, "mask_b", [P, 3 * P], BF16)

        class Causal:

            def __init__(self, name, heads, kv_heads, hd, scale, interleaved):
                self.name, self.heads, self.kv_heads, self.hd = name, heads, kv_heads, hd
                self.scale, self.interleaved = scale, interleaved

            def run(self, cos_dram, sin_dram, free, splitter):
                heads, kv_heads, hd = self.heads, self.kv_heads, self.hd
                per = P // hd
                KW = kv_heads * hd
                n_ = self.name
                with ExitStack() as phase:
                    xn = sb(phase, f"xn_{n_}", [P, TT, D])
                    xnT_high = sb(phase, f"xnT_high_{n_}", [P, KT, T], F32R)
                    xnT_low = sb(phase, f"xnT_low_{n_}", [P, KT, T], F32R)
                    q_rot = sb(phase, f"q_rot_{n_}", [P, TT, D])
                    k_rot = sb(phase, f"k_rot_{n_}", [P, TT, KW])
                    v = sb(phase, f"v_{n_}", [P, TT, KW])
                    qz = sb(phase, f"qz_{n_}", [P, heads, T])
                    kT = sb(phase, f"kT_{n_}", [P, KW // P, T])
                    cos = sb(phase, f"cos_{n_}", [P, TT, hd])
                    sin = sb(phase, f"sin_{n_}", [P, TT, hd])
                    mask = sb(phase, f"mask_{n_}", [P, 3 * P])
                    part = [sb(phase, f"part{i}_{n_}", [P, BANK]) for i in range(2)]
                    probs = [sb(phase, f"probs{i}_{n_}", [P, 3 * P]) for i in range(4)]
                    probsT = [sb(phase, f"probsT{i}_{n_}", [P, 3 * P]) for i in range(4)]
                    top = sb(phase, f"top_{n_}", [P, 2, 2, 2])
                    total = sb(phase, f"total_{n_}", [P, TT, heads])
                    inverse = sb(phase, f"inverse_{n_}", [P, TT, heads])
                    o = sb(phase, f"o_{n_}", [P, TT, D])
                    oT_high = sb(phase, f"oT_high_{n_}", [P, KT, T], F32R)
                    oT_low = sb(phase, f"oT_low_{n_}", [P, KT, T], F32R)
                    wait(sp, *free)
                    for dst, src in ((cos, cos_dram), (sin, sin_dram), (mask, a["mask"])):
                        tables_ready = const_in.after(sp.dma_start(dst[:], src), 16)
                    wait(pool, so_far(pool_done), *free)
                    zeroed = POOL(pool.memset(qz[:], 0.0))
                    normed = layernorm(xn, free)
                    turned = turn_split(xn, xnT_high, xnT_low, normed, [4, 5, 6, 7], free)
                    wait(act, tables_ready)
                    mask_ready = ACTE(act.activation(mask_b[:], mask[:], ACT.Copy))

                    def halves(ap):
                        if self.interleaved:
                            v4 = ap.rearrange("p b (i two) -> p b i two", two=2)
                            return v4[:, :, :, 0], v4[:, :, :, 1]
                        return ap[:, :, 0:hd // 2], ap[:, :, hd // 2:hd]

                    part_free = None

                    def rotate(dst, src, t, event):
                        nonlocal part_free
                        cols = src.shape[-1]
                        nb = cols // hd
                        blocks = lambda ap: ap.rearrange("p (b d) -> p b d", d=hd)
                        table = lambda z: z[:, t, :].unsqueeze(1).broadcast_to([P, nb, hd])
                        one, two = (blocks(z[:, 0:cols]) for z in part)
                        src, dst = blocks(src), blocks(dst)
                        wait(dve, event, tables_ready, part_free)
                        DVE(dve.tensor_tensor(one, src, table(cos), ALU.mult))
                        (s1, s2), (n1, n2), (t1, t2) = halves(src), halves(table(sin)), halves(two)
                        DVE(dve.tensor_tensor(t1, s2, n1, ALU.mult))
                        read = DVE(dve.tensor_tensor(t2, s1, n2, ALU.mult))
                        wait(dve, read)
                        (o1, o2), (d1, d2) = halves(one), halves(dst)
                        DVE(dve.tensor_tensor(d1, o1, t1, ALU.subtract))
                        part_free = DVE(dve.tensor_tensor(d2, o2, t2, ALU.add))
                        return read

                    xnT_k = [(xnT_high[:, k, :], xnT_low[:, k, :]) for k in range(KT)]

                    def take_q(n, t, product, event):
                        return rotate(q_rot[:, t, n * BANK:(n + 1) * BANK], product, t, event)

                    def take_k(n, t, product, event):
                        return rotate(k_rot[:, t, n * BANK:(n + 1) * BANK], product, t, event)

                    def take_v(n, t, product, event):
                        wait(act, event)
                        return ACTE(act.activation(v[:, t, n * BANK:(n + 1) * BANK], product, ACT.Copy))

                    def take_kv(n, t, product, event):
                        wait(act, event)
                        wait(dve, ACTE(act.activation(v[:, t, :], product[:, KW:2 * KW], ACT.Copy)))
                        return rotate(k_rot[:, t, :], product[:, 0:KW], t, event)

                    placed = {}

                    def place(i):
                        b = i % 4
                        wait(pe, q_ready, const_ready, bank_read[b])
                        for j in range(2):
                            for t in range(TT):
                                k = 2 * i + j
                                c = (j * TT + t) * P
                                e = PE(pe.transpose(psum[:, b, c:c + P], q_rot[:, t, k * P:k * P + P], ident[:]))
                        for j in range(2):
                            for g in range(per):
                                head = (2 * i + j) * per + g
                                row = head * kv_heads // heads * hd % P
                                dst = qz[row:row + hd, head, :]
                                src = psum[g * hd:(g + 1) * hd, b, j * T:(j + 1) * T]
                                if i % 2:
                                    wait(dve, e, zeroed)
                                    done = DVE(dve.tensor_copy(dst, src))
                                else:
                                    wait(act, e, zeroed)
                                    done = ACTE(act.activation(dst, src, ACT.Copy))
                        bank_read[b] = placed[i] = done

                    linear_split(xnT_k, turned, splitter, 2, [0, 1, 2, 3], take_q)
                    q_ready = part_free
                    two = [lambda: (place(0), place(1)), lambda: (place(2), place(3))]
                    if KW == D:
                        linear_split(xnT_k, turned, splitter, 2, [4, 5, 6, 7], take_k, [lambda: None, *two])
                        k_ready = part_free
                        linear_split(xnT_k, turned, splitter, 2, [0, 1, 2, 3], take_v)
                    else:
                        linear_split(xnT_k, turned, splitter, 1, [4, 5, 6, 7], take_kv, two)
                        k_ready = part_free
                    v_ready = so_far(act_done)
                    k_turned = turn(k_rot, kT, k_ready, [4, 5, 6, 7], KW)

                    scored, exps, turns, moved, weighed = {}, {}, {}, {}, {}
                    spans = (slice(0, P), slice(P, 3 * P))
                    PER = D // 4 // hd

                    def scores(h):
                        b = h % 4
                        block = h * kv_heads // heads * hd // P
                        wait(pe, bank_read[b], mask_ready, ident_ready, placed[h // per // 2], k_turned[block // 2])
                        pe.matmul(psum[:, b, 0:3 * P], ident_b[:], mask_b[:], start=True, stop=False,
                                  skip_group_check=True)
                        pe.matmul(psum[:, b, 0:P], qz[:, h, 0:P], kT[:, block, 0:P], start=False, stop=True,
                                  skip_group_check=True)
                        scored[h] = PE(pe.matmul(psum[:, b, P:3 * P], qz[:, h, P:T], kT[:, block, :],
                                                 start=False, stop=True, skip_group_check=True))

                    def soften(h):
                        b, turn_ = h % 4, h // 2 % 2
                        wait(dve, scored[h + 1], exps.get(h - 3))
                        for t in range(TT):
                            e = DVE(dve.tensor_reduce(top[:, turn_, :, t], psum[:, b:b + 2, spans[t]], AX_X, ALU.max))
                        wait(dve, e)
                        tops = top[:, turn_].rearrange("p h t -> p (h t)")
                        e = DVE(dve.tensor_scalar(tops, tops, -self.scale, None, ALU.mult))
                        for i in range(2):
                            wait(act, e, turns.get(h + i - 4))
                            for t in range(TT):
                                done = ACTE(act.activation(
                                    probs[(h + i) % 4][:, spans[t]], psum[:, b + i, spans[t]], ACT.Exp,
                                    scale=self.scale, bias=top[:, turn_, i, t:t + 1],
                                    accum_out=total[:, t, h + i:h + i + 1]))
                            exps[h + i] = bank_read[b + i] = done

                    def turn_probs(h):
                        b, s = 4 + h % 2, h % 4
                        wait(pe, exps[h], bank_read[b])
                        for i in range(3):
                            e = PE(pe.transpose(psum[:, b, i * P:(i + 1) * P], probs[s][:, i * P:(i + 1) * P],
                                                ident[:]))
                        turns[h] = e
                        if h % 2:
                            wait(dve, e, weighed.get(h - 4))
                            e = DVE(dve.tensor_copy(probsT[s][:], psum[:, b, 0:3 * P]))
                        else:
                            wait(act, e, weighed.get(h - 4))
                            e = ACTE(act.activation(probsT[s][:], psum[:, b, 0:3 * P], ACT.Copy))
                        bank_read[b] = moved[h] = e

                    def weigh(h):
                        s, quarter = h % 4, h // PER
                        b, col = 6 + quarter % 2, h % PER * hd
                        j = h * kv_heads // heads
                        wait(pe, moved[h], bank_read[b], v_ready)
                        value = [v[:, t, j * hd:(j + 1) * hd] for t in range(TT)]
                        pe.matmul(psum[:, b, col:col + hd], probsT[s][:, 0:P], value[0], start=True, stop=True)
                        out_1 = psum[:, b, T + col:T + col + hd]
                        pe.matmul(out_1, probsT[s][:, P:2 * P], value[0], start=True, stop=False)
                        weighed[h] = PE(pe.matmul(out_1, probsT[s][:, 2 * P:3 * P], value[1], start=False, stop=True))
                        if h % PER == PER - 1:
                            own = slice(quarter * PER, (quarter + 1) * PER)
                            wait(dve, exps[h])
                            e = DVE(dve.reciprocal(inverse[:, :, own], total[:, :, own]))
                            wait(dve, e, weighed[h])
                            for t in range(TT):
                                e = DVE(dve.tensor_tensor(
                                    o[:, t, quarter * T:(quarter + 1) * T].rearrange("p (h d) -> p h d", d=hd),
                                    psum[:, b, t * T:(t + 1) * T].rearrange("p (h d) -> p h d", d=hd),
                                    inverse[:, t, own].unsqueeze(2).broadcast_to([P, PER, hd]), ALU.mult))
                            bank_read[b] = e
                            quarters.append((quarter, e))

                    def turn_quarter(quarter, event):
                        b = 6 + quarter % 2
                        wait(pe, event)
                        for j in range(2):
                            for t in range(TT):
                                k, c = 2 * quarter + j, (j * TT + t) * P
                                e = PE(pe.transpose(psum[:, b, c:c + P], o[:, t, k * P:k * P + P], ident[:]))
                        ks = slice(2 * quarter, 2 * quarter + 2)
                        _, bank_read[b] = halve(psum[:, b, :].rearrange("p (j n) -> p j n", j=2),
                                                oT_high[:, ks, :], oT_low[:, ks, :], [e])
                        return bank_read[b]

                    quarters = []
                    for h in range(0, heads + 4, 2):
                        if h < heads:
                            scores(h)
                            scores(h + 1)
                            soften(h)
                        if quarters:
                            o_ready = turn_quarter(*quarters.pop(0))
                        for i in range(2):
                            if 0 <= h - 2 < heads:
                                turn_probs(h - 2 + i)
                            if h >= 4:
                                weigh(h - 4 + i)
                    o_ready = turn_quarter(*quarters.pop(0))
                    linear_split([(oT_high[:, k, :], oT_low[:, k, :]) for k in range(KT)],
                                 [o_ready], splitter, 2, [0, 1, 2, 3], add_to_x)
                return [x_ready, so_far(pe_done), so_far(act_done), so_far(dve_done)]

        attend_d = Causal("d", 16, 16, 64, 0.125, True)
        done = attend_d.run(a["cos_a"], a["sin_a"], done, splitter)
        split_stack.close()
        if stop <= 2:
            return finish()

        E_, R = 8, 16
        with ExitStack() as phase:
            xn = sb(phase, "xn_e", [P, TT, D])
            xnT = sb(phase, "xnT_e", [P, KT, T])
            rank = sb(phase, "rank", [P, E_])
            chosen = sb(phase, "chosen", [P, TT, 2, E_])
            best = sb(phase, "best", [P, TT, 2])
            hidden = sb(phase, "hidden_e", [P, TT, E_ * R])
            hiddenT = sb(phase, "hiddenT_e", [P, T])
            wait(sp, *done)
            rank_ready = const_in.after(sp.dma_start(rank[:], a["rank"]), 16)
            normed = layernorm(xn, done)
            turned = turn(xn, xnT, normed, [4, 5, 6, 7])
            routed = []

            def route(n, t, product, event):
                top, first = best[:, t, 0:1], best[:, t, 1:2]
                ranks, weights = chosen[:, t, 0, :], chosen[:, t, 1, :]
                wait(dve, event, rank_ready)
                wait(dve, DVE(dve.tensor_reduce(top, product[:, 0:E_], AX_X, ALU.max)))
                wait(dve, DVE(dve.scalar_tensor_tensor(out=ranks, in0=product[:, 0:E_], scalar=top, in1=rank[:],
                                                       op0=ALU.is_equal, op1=ALU.mult)))
                wait(dve, DVE(dve.tensor_reduce(first, ranks, AX_X, ALU.max)))
                wait(dve, DVE(dve.tensor_scalar(weights, ranks, first, top, ALU.is_equal, ALU.mult)))
                e = DVE(dve.tensor_tensor(hidden[:, t, :].rearrange("p (e r) -> p e r", r=R),
                                          product[:, E_:E_ + E_ * R].rearrange("p (e r) -> p e r", r=R),
                                          weights.unsqueeze(2).broadcast_to([P, E_, R]), ALU.mult))
                routed.append(e)
                return e

            linear([xnT[:, k, :] for k in range(KT)], turned, panels, 1, [0, 1], route, width=E_ + E_ * R)
            wait(pe, *routed, bank_read[2])
            for t in range(TT):
                e = PE(pe.transpose(psum[:, 2, t * P:(t + 1) * P], hidden[:, t, :], ident[:]))
            wait(act, e)
            bank_read[2] = ACTE(act.activation(hiddenT[:], psum[:, 2, 0:T], ACT.Copy))
            w, arrived = panels.take()
            wait(pe, bank_read[2], arrived)
            for n in range(2):
                for t in range(TT):
                    b = 4 + 2 * n + t
                    wait(pe, bank_read[b])
                    e = PE(pe.matmul(psum[:, b, :], hiddenT[:, t * P:(t + 1) * P], w.ap(n, BANK), start=True,
                                     stop=True))
                    bank_read[b] = add_to_x(n, t, psum[:, b, :], e)
            panels.release(e)
            done = [x_ready, so_far(pe_done), so_far(act_done)]
        if stop <= 3:
            return finish()

        H1 = KV1 * G1
        NS1 = CTX // P
        NC1 = CTX // BANK
        with ExitStack() as phase:
            q_rows = sb(phase, "q_rows", [3 * HD1 + 2, KV1, G1 * T], F32R)
            k_rows = [sb(phase, f"k_rows{i}", [3 * HD1 + 2, CTX], F32R) for i in range(2)]
            v_all = sb(phase, "v_all", [P, NS1, V1W])
            probs = [sb(phase, f"probs_f{i}", [P, G1 * T]) for i in range(4)]
            odd = sb(phase, "odd_f", [2 * HD1, G1 * T])
            inverse = sb(phase, "inverse_f", [2 * HD1, G1 * T])
            sums = sb(phase, "sums_f", [HD1, BANK])
            few = sb(phase, "few_f", [HD1, BANK // 32])
            top1 = sb(phase, "top1", [P, G1 * TT, NC1])
            neg_top1 = sb(phase, "neg_top1", [P, G1 * TT])
            t_high = sb(phase, "t_high", [G1 * TT, P], F32R)
            t_low = sb(phase, "t_low", [G1 * TT, P], F32R)
            oT_high = sb(phase, "oT_high_f", [P, KV1, T], F32R)
            oT_low = sb(phase, "oT_low_f", [P, KV1, T], F32R)
            k1_in = [signal(f"k1_in{i}") for i in range(2)]
            v1_in = signal("v1_in")
            top_in = signal("top_in")

            def k1_piece(kv):
                rows = slice(kv * HD1, (kv + 1) * HD1)
                return lambda k: [(k[0:HD1, :].bitcast(F32), k1_high[rows, :]),
                                  (k[HD1:2 * HD1, :].bitcast(F32), k1_high[rows, :]),
                                  (k[2 * HD1:3 * HD1, :].bitcast(F32), k1_low[rows, :])]

            wait(pool, *done)
            for k in k_rows:
                wait(pool, so_far(pool_done))
                ones_set = POOL(pool.memset(k[3 * HD1:3 * HD1 + 2, :].bitcast(F32), 1.0))
            keys = Feed(sp, wait, k_rows, k1_in, [k1_piece(kv) for kv in range(KV1)], first=[*done, *kv_spilled])
            v1_ready = v1_in.after(sp.dma_start(v_all[:], v1_dram), 16)

            xn_parts = [probs[0], probs[1]]
            wait(dve, stats_ready, *done)
            for t in range(TT):
                e = DVE(dve.bn_aggr(moments[:, t, :], stats[:, t].rearrange("p h s -> p (h s)")))
            r, e = inverse_root(moments[:, :, 1], 1e-5, e)
            wait(dve, e)
            for t in range(TT):
                e = DVE(dve.tensor_scalar(xn_parts[t][:], x[:, t, :], moments[:, t, 0:1], r[:, t:t + 1],
                                          ALU.subtract, ALU.mult))
            wait(pe, e)
            xnT_parts = [probs[2], probs[3]]
            turned = []
            for i in range(KT // 2):
                b = 4 + i
                wait(pe, bank_read[b])
                for j in range(2):
                    for t in range(TT):
                        c = (j * TT + t) * P
                        k = 2 * i + j
                        e = PE(pe.transpose(psum[:, b, c:c + P], xn_parts[t][:, k * P:(k + 1) * P], ident[:]))
                wait(act, e)
                bank_read[b] = ACTE(act.activation(xnT_parts[i // 2][:, i % 2 * 2 * T:(i % 2 + 1) * 2 * T],
                                                   psum[:, b, :], ACT.Copy))
            wait(pe, bank_read[7])
            max_jobs, q1_ready = {}, {}

            def maxima(kv, m):
                rows, chunk = divmod(m, NC1)
                k, arrived = max_jobs[kv]
                b = 6 + m % 2
                wait(pe, arrived, bank_read[b], q1_ready[kv])
                e = PE(pe.matmul(psum[:, b, :], q_rows[0:3 * HD1, kv, rows * P:(rows + 1) * P],
                                 k[0:3 * HD1, chunk * BANK:(chunk + 1) * BANK], start=True, stop=True))
                wait(dve, e)
                bank_read[b] = DVE(dve.tensor_reduce(top1[:, rows, chunk:chunk + 1], psum[:, b, :], AX_X, ALU.max))

            tops_read = {}

            def place_maxima(kv):
                wait(dve, bank_read[6], bank_read[7], tops_read.get("pe"))
                tops_read["dve"] = DVE(dve.tensor_reduce(neg_top1[:], top1[:], AX_X, ALU.max, negate=True))

            def place_rows(kv):
                wait(pe, tops_read["dve"], bank_read[6])
                e = PE(pe.transpose(psum[0:G1 * TT, 6, 0:P], neg_top1[:], ident[:]))
                tops_read["pe"] = e
                wait(act, e, tops_read.get("dma"))
                e = ACTE(act.activation(t_high[:], psum[0:G1 * TT, 6, 0:P], ACT.Copy))
                wait(dve, e, tops_read.get("dma"))
                bank_read[6] = DVE(dve.tensor_tensor(t_low[:], psum[0:G1 * TT, 6, 0:P], t_high[:].bitcast(F32),
                                                     ALU.subtract))
                wait(sp, e, bank_read[6])
                for r, top in ((0, t_high), (1, t_low)):
                    row = 3 * HD1 + r
                    e = top_in.after(sp.dma_start(
                        q_rows[row:row + 1, kv, :].bitcast(F32).rearrange("o (r n) -> o r n", n=P),
                        top[:].bitcast(F32)), 16)
                tops_read["dma"] = e
                return e

            max_jobs[0] = keys.take()
            beside = list(range(G1 * TT * NC1))
            for n in range(2):
                both = [panels.take() for _ in range(2)]
                wait(pe, *(arrived for _, arrived in both))
                for c in range(4):
                    b, kv = c, 4 * n + c
                    wait(pe, bank_read[b])
                    for k in range(KT):
                        if kv > 0 and beside:
                            maxima(0, beside.pop(0))
                        mm = pe.matmul(psum[:, b, 0:T], both[k // 4][0].ap(k % 4, BANK)[:, c * P:(c + 1) * P],
                                       xnT_parts[k // 4][:, k % 4 * T:(k % 4 + 1) * T], start=k == 0, stop=k == KT - 1)
                    e = PE(mm)
                    for g in range(G1):
                        src = psum[g * HD1:(g + 1) * HD1, b, 0:T]
                        cols = slice(g * T, (g + 1) * T)
                        wait(act, e)
                        high = q_rows[0:HD1, kv, cols]
                        ACTE(act.activation(high, src, ACT.Copy))
                        e_high = ACTE(act.activation(q_rows[2 * HD1:3 * HD1, kv, cols], src, ACT.Copy))
                        wait(dve, e_high)
                        bank_read[b] = DVE(dve.tensor_tensor(q_rows[HD1:2 * HD1, kv, cols], src,
                                                             high.bitcast(F32), ALU.subtract))
                    q1_ready[kv] = bank_read[b]
                for _ in both:
                    panels.release(e)
            q1_read = e

            scale = float(HD1 ** -0.5)
            for m in beside:
                maxima(0, m)
            place_maxima(0)
            placed = {0: place_rows(0)}
            exp_done, pv_done = {}, {}
            tiles = [(kv, s) for kv in range(KV1) for s in range(NS1)]

            def scores1(n):
                kv, s = tiles[n]
                k, arrived = max_jobs[kv]
                wait(pe, arrived, placed[kv], q1_ready[kv], ones_set)
                for half in range(2):
                    b = 2 * (n % 2) + half
                    wait(pe, bank_read[b])
                    e = PE(pe.matmul(psum[:, b, :], k[:, s * P:(s + 1) * P],
                                     q_rows[:, kv, half * BANK:(half + 1) * BANK], start=True, stop=True))
                wait(act, e, pv_done.get(n - 4), q1_read)
                exp_done[n] = ACTE(act.activation(
                    probs[n % 4][:], psum[:, 2 * (n % 2):2 * (n % 2) + 2, :].rearrange("p b n -> p (b n)"),
                    ACT.Exp, scale=scale))
                bank_read[2 * (n % 2)] = bank_read[2 * (n % 2) + 1] = exp_done[n]

            weighed_kv = [None, None]

            def weigh1(n, half):
                kv, s = tiles[n]
                wait(pe, exp_done[n], exp_done[n + 1], bank_read[4], bank_read[5], v1_ready, ones_set)
                for i in range(2):
                    col = kv // 2 * 3 * HD1 + kv % 2 * HD1
                    mm = pe.matmul(psum[i * 64:(i + 1) * 64, 4 + half, :], v_all[:, s + i, col:col + 2 * HD1],
                                   probs[(n + i) % 4][:, half * BANK:(half + 1) * BANK],
                                   start=s == 0, stop=s == NS1 - 2)
                pv_done[n] = pv_done[n + 1] = e = PE(mm)
                if s == NS1 - 2:
                    cols = slice(half * BANK, (half + 1) * BANK)
                    vr = slice(kv % 2 * HD1, kv % 2 * HD1 + HD1)
                    sr = slice(HD1 - kv % 2 * HD1, 2 * HD1 - kv % 2 * HD1)
                    wait(act, e, weighed_kv[half])
                    e = ACTE(act.activation(odd[:, cols], psum[64:128, 4 + half, :], ACT.Copy))
                    wait(dve, e)
                    e = DVE(dve.tensor_tensor(odd[:, cols], psum[0:64, 4 + half, :], odd[:, cols], ALU.add))
                    bank_read[4 + half] = e
                    later.append((kv, half, cols, vr, sr, e))

            later, unsplit, rounded_outputs = [], [], []

            def normalise1():
                kv, half, cols, vr, sr, e = later.pop(0)
                wait(dve, so_far(dve_done))
                _, e = invert_row(odd[sr, cols], inverse[vr, cols], sums[:], few[:], e)
                wait(dve, e)
                for g in (2 * half, 2 * half + 1):
                    c = slice(g * T, (g + 1) * T)
                    e = DVE(dve.tensor_tensor(inverse[vr, c], odd[vr, c], inverse[vr, c], ALU.mult))
                    unsplit.append((kv, half, g, vr, c, e))

            def split1():
                while rounded_outputs:
                    kv, half, rows, src, e = rounded_outputs.pop(0)
                    wait(dve, e)
                    weighed_kv[half] = DVE(dve.tensor_tensor(oT_low[rows, kv, :], src,
                                                             oT_high[rows, kv, :].bitcast(F32), ALU.subtract))
                while unsplit:
                    kv, half, g, vr, c, e = unsplit.pop(0)
                    rows = slice(g * HD1, (g + 1) * HD1)
                    wait(act, e)
                    e = ACTE(act.activation(oT_high[rows, kv, :], inverse[vr, c], ACT.Copy))
                    rounded_outputs.append((kv, half, rows, inverse[vr, c], e))

            splitter = Splitter(split_tiles(split_stack, "panel_fg", 2), panels, 4 + 10)
            scores1(0)
            scores1(1)
            jobs = G1 * TT * NC1
            first_pair, last_pair = 2, NS1 // 2 - 4
            count = last_pair - first_pair + 1
            for n in range(0, len(tiles), 2):
                kv, s = tiles[n]
                pair = s // 2
                ahead = kv + 1 < KV1
                if s == 0 and ahead:
                    max_jobs[kv + 1] = keys.take()
                beside = [m for m in range(jobs) if ahead and first_pair + m * count // jobs == pair]
                steps = [lambda n=n: scores1(n + 2), lambda n=n: scores1(n + 3)] if n + 2 < len(tiles) else []
                steps += [lambda n=n: weigh1(n, 0), lambda n=n: weigh1(n, 1)]
                for i, step in enumerate(steps):
                    for m in beside[i * len(beside) // 4:(i + 1) * len(beside) // 4]:
                        maxima(kv + 1, m)
                    step()
                    if i == 2 and ahead and pair == last_pair + 1:
                        placed[kv + 1] = place_rows(kv + 1)
                if ahead and pair == last_pair:
                    place_maxima(kv + 1)
                split1()
                if later and s != NS1 - 2:
                    normalise1()
                if s == NS1 - 2:
                    keys.release(pv_done[n])
            while later:
                normalise1()
                split1()
            split1()
            linear_split([(oT_high[:, kv, :], oT_low[:, kv, :]) for kv in range(KV1)], weighed_kv, splitter, 2,
                         [0, 1, 2, 3], add_to_x)
            done = [x_ready, so_far(pe_done), so_far(act_done), so_far(dve_done)]
        if stop <= 4:
            return finish()

        attend_g = Causal("g", 32, 8, 32, float(1.0 / np.sqrt(np.float32(32.0))), False)
        done = attend_g.run(a["cos_b"], a["sin_b"], done, splitter)
        split_stack.close()
        if stop <= 5:
            return finish()

        panel_stack.close()
        with ExitStack() as phase:
            xn = sb(phase, "xn_h", [P, TT, D])
            square = sb(phase, "square", [P, D])
            gain = sb(phase, "gain", [P, D])
            ints = sb(phase, "ints_h", [P, TT, D], BF16)
            intsT = sb(phase, "intsT_h", [P, KT, T], BF16)
            act_scale = sb(phase, "act_scale", [P, 8, TT])
            gate_up = [sb(phase, f"gate_up{i}", [P, 2, 4 * KT * P], BF16) for i in range(2)]
            down = sb(phase, "down", [P, KT, FT * P], BF16)
            ws_g = sb(phase, "ws_g", [P, FF])
            ws_u = sb(phase, "ws_u", [P, FF])
            ws_d = sb(phase, "ws_d", [P, D])
            ws_turned = sb(phase, "ws_turned", [NQ, P])
            g_part = [sb(phase, f"g_part{i}", [P, BANK]) for i in range(2)]
            s_part = [sb(phase, f"s_part{i}", [P, BANK]) for i in range(2)]
            u_part = [sb(phase, f"u_part{i}", [P, BANK]) for i in range(2)]
            hid = sb(phase, "hid", [P, TT, FF])
            gu_in = [signal(f"gu_in{i}") for i in range(2)]
            down_in, ws_sent, ws_in = signal("down_in"), signal("ws_sent"), signal("ws_in")
            wait(sp, *done)
            gain_ready = const_in.after(sp.dma_start(gain[:], a["rms_weight"].partition_broadcast(P)), 16)
            wait(pe, *done, bank_read[0])
            e = PE(pe.transpose(psum[0:NQ, 0, 0:P], w_scale[:], ident[:]))
            wait(act, e, *done)
            bank_read[0] = ACTE(act.activation(ws_turned[:], psum[0:NQ, 0, 0:P], ACT.Copy))
            wait(sp, bank_read[0])
            e = ws_sent.after(sp.dma_start(ws_dram, ws_turned[:]), 16)

            def chunk_piece(c):
                n = min(4, FT - 4 * c)

                def dmas(tile):
                    pairs = []
                    for which in range(2):
                        at = which * FT + 4 * c
                        whole = n if 4 * c + n < FT else n - 1
                        pairs.append((tile[:, which, 0:whole * KT * P].rearrange("p (i m) -> p i m", i=whole),
                                      q_dram[at:at + whole].rearrange("i p m -> p i m")))
                        if whole < n:
                            rest = FF % P
                            view = lambda z: z.rearrange("p (k n) -> p k n", n=P)[:, :, 0:rest]
                            pairs.append((view(tile[:, which, whole * KT * P:n * KT * P]), view(q_dram[at + whole])))
                    return pairs
                return dmas

            chunks = -(-FT // 4)
            order = [chunk_piece(c) for c in range(chunks)]
            ring = Feed(sp, wait, gate_up, gu_in, order, first=[*done, *q_all_spilled])
            wait(sp, e)
            flat = ws_dram.rearrange("r n -> (r n)")
            ws_in.after(sp.dma_start(ws_g[:], flat[0:FF].partition_broadcast(P)), 16)
            ws_in.after(sp.dma_start(ws_u[:], flat[FT * P:FT * P + FF].partition_broadcast(P)), 16)
            ws_ready = ws_in.after(sp.dma_start(ws_d[:], flat[2 * FT * P:NQ * P].partition_broadcast(P)), 16)
            whole = FF // P * P
            down_in.after(sp.dma_start(down[:, :, 0:whole], qd_dram[:, :, 0:whole].rearrange("k p m -> p k m")), 16)
            down_ready = down_in.after(sp.dma_start(
                down[0:FF - whole, :, whole:], qd_dram[:, 0:FF - whole, whole:].rearrange("k p m -> p k m")), 16)

            def quantise(values, result, t, slot, ready):
                top, sc, inv = (act_scale[:, slot + i, t:t + 1] for i in range(3))
                wait(dve, ready)
                wait(dve, DVE(dve.tensor_reduce(top, values, AX_X, ALU.max, apply_absolute_value=True)))
                wait(dve, DVE(dve.tensor_scalar(sc, top, 1.0 / QMAX, 1e-8, ALU.mult, ALU.max)))
                wait(dve, DVE(dve.reciprocal(inv, sc)))
                wait(dve, DVE(dve.tensor_scalar(values, values, inv, ROUND, ALU.mult, ALU.add)))
                return DVE(dve.tensor_scalar(result, values, ROUND, None, ALU.subtract))

            normed = layernorm(xn, done)
            mean_square = act_scale[:, 6, :]
            wait(act, normed)
            for t in range(TT):
                e = ACTE(act.activation(square[:], xn[:, t, :], ACT.Square, accum_out=mean_square[:, t:t + 1]))
                wait(act, e)
            wait(dve, e)
            e = DVE(dve.tensor_scalar(mean_square, mean_square, 1.0 / D, None, ALU.mult))
            r, e = inverse_root(mean_square, 1e-6, e)
            wait(dve, e, gain_ready)
            for t in range(TT):
                e = DVE(dve.scalar_tensor_tensor(out=xn[:, t, :], in0=xn[:, t, :], scalar=r[:, t:t + 1],
                                                 in1=gain[:], op0=ALU.mult, op1=ALU.mult))
                rounded = quantise(xn[:, t, :], ints[:, t, :], t, 0, e)
            wait(pe, rounded)
            for i in range(2):
                b = 1 + i
                wait(pe, bank_read[b])
                bank = psum[:, b, :].bitcast(BF16)
                for j in range(4):
                    for t in range(TT):
                        k = 4 * i + j
                        c = j * T + t * P
                        e = PE(pe.transpose(bank[:, c:c + P], ints[:, t, k * P:(k + 1) * P], ident_b[:]))
                wait(dve, e)
                bank_read[b] = DVE(dve.tensor_copy(intsT[:, 4 * i:4 * i + 4, :].rearrange("p k n -> p (k n)"), bank))
            ints_turned = [bank_read[1], bank_read[2]]

            job = 0
            silu_done, mixed = {}, {}
            for c in range(chunks):
                w, arrived = ring.take()
                n_tiles = min(4, FT - 4 * c)
                width = min(BANK, FF - c * BANK)
                wait(pe, arrived, *ints_turned)
                for t in range(TT):
                    bg, bu = 2 * (job % 4), 2 * (job % 4) + 1
                    wait(pe, bank_read[bg], bank_read[bu])
                    parts = [(0, width)] if width == BANK else [(i * P, min(P, width - i * P)) for i in range(n_tiles)]
                    for which, b in ((0, bg), (1, bu)):
                        grid = w[:, which, :].rearrange("p (i k n) -> p i k n", k=KT, n=P)
                        for first, count in parts:
                            for k in range(KT):
                                moving = grid[:, :, k, :] if width == BANK else grid[:, first // P, k, 0:count]
                                mm = pe.matmul(psum[:, b, first:first + count], intsT[:, k, t * P:(t + 1) * P],
                                               moving, start=k == 0, stop=k == KT - 1)
                    e = PE(mm)
                    at = slice(c * BANK, c * BANK + width)
                    i = job % 2
                    sc = act_scale[:, 1, t:t + 1]
                    wait(dve, e, ws_ready, mixed.get(job - 2))
                    e_g = DVE(dve.scalar_tensor_tensor(out=g_part[i][:, 0:width], in0=psum[:, bg, 0:width], scalar=sc,
                                                       in1=ws_g[:, at], op0=ALU.mult, op1=ALU.mult))
                    bank_read[bg] = e_g
                    wait(act, e_g, mixed.get(job - 2))
                    silu_done[job] = ACTE(act.activation(s_part[i][:, 0:width], g_part[i][:, 0:width], ACT.Silu))
                    e_u = DVE(dve.scalar_tensor_tensor(out=u_part[i][:, 0:width], in0=psum[:, bu, 0:width], scalar=sc,
                                                       in1=ws_u[:, at], op0=ALU.mult, op1=ALU.mult))
                    bank_read[bu] = e_u
                    wait(pool, silu_done[job], e_u, so_far(pool_done))
                    mixed[job] = POOL(pool.tensor_tensor(hid[:, t, at], s_part[i][:, 0:width], u_part[i][:, 0:width],
                                                         ALU.mult))
                    job += 1
                ring.release(e)
            chunks_read = e

            hid_i = [w[:, 0, 0:FF] for w in gate_up]
            out_T = [gate_up[t][:, 1, 0:FT * P] for t in range(TT)]
            for t in range(TT):
                wait(dve, chunks_read)
                rounded = quantise(hid[:, t, :], hid_i[t], t, 3, mixed[job - 1])
                wait(pe, rounded)
                for b0 in range(0, FT, 8):
                    b = b0 // 8 + 4 * t
                    some = range(b0, min(b0 + 8, FT))
                    bank = psum[:, b, :].bitcast(BF16).rearrange("p (k n) -> p k n", n=P)
                    wait(pe, bank_read[b])
                    for k in some:
                        rows = min(P, FF - k * P)
                        e = PE(pe.transpose(bank[0:rows, k - b0, :], hid_i[t][:, k * P:k * P + rows], ident_b[:]))
                    wait(act, e)
                    full = [k for k in some if FF - k * P >= P]
                    for height, k0, count in [(P, full[0], len(full))] + (
                            [(FF % P, some[-1], 1)] if len(full) < len(some) else []):
                        bank_read[b] = ACTE(act.activation(
                            out_T[t][0:height, k0 * P:(k0 + count) * P].rearrange("p (k n) -> p k n", n=P),
                            bank[0:height, k0 - b0:k0 - b0 + count, :], ACT.Copy))
                wait(pe, bank_read[b], down_ready)
                for n in range(2):
                    b = 3 + 4 * n
                    wait(pe, bank_read[b])
                    for k in range(FT):
                        rows = min(P, FF - k * P)
                        mm = pe.matmul(psum[:, b, :], out_T[t][0:rows, k * P:(k + 1) * P],
                                       down[0:rows, 4 * n:4 * n + 4, k * P:(k + 1) * P], start=k == 0, stop=k == FT - 1)
                    e = PE(mm)
                    wait(dve, e)
                    at = slice(n * BANK, (n + 1) * BANK)
                    e = DVE(dve.scalar_tensor_tensor(out=xn[:, t, at], in0=psum[:, b, :],
                                                     scalar=act_scale[:, 4, t:t + 1], in1=ws_d[:, at],
                                                     op0=ALU.mult, op1=ALU.mult))
                    bank_read[b] = e
                    wait(dve, e)
                    x_ready = DVE(dve.tensor_tensor(x[:, t, at], xn[:, t, at], x[:, t, at], ALU.add))
        return finish()


def program(nc, a, out, stop=99):
    build(nc, a, out, stop)


def layouts(i):
    c = np.ascontiguousarray
    P_, KT = 128, 8

    def tiled(w, width):
        k, n = w.shape
        return c(w.reshape(k // P_, P_, n // width, width).transpose(2, 1, 0, 3).reshape(n // width, P_, -1))

    a = {"x": i["x"], "ident": np.eye(P_, dtype=np.float32)}
    a["wq0"] = tiled(i["L0_xattn_Wq"].T, 96)
    k0, k1 = i["L0_xattn_Wk"].T.reshape(1024, 4, 96), i["L1_xattn_Wk"].reshape(1024, 8, 32)
    packed = np.concatenate([k0, k1[:, :4]], axis=2).reshape(1024, 512)
    wkv = np.concatenate([packed, k1[:, 4:].reshape(1024, 128), i["L0_xattn_Wv"].T, i["L1_xattn_Wv"]], axis=1)
    a["wkv"] = c(wkv.reshape(KT, P_, 1280))
    ctx = i["ctx_4096"][0].reshape(16, 256, KT, P_)
    a["ctxT"] = c(ctx.transpose(0, 3, 2, 1).reshape(16, P_, KT * 256))
    wo0 = i["L0_xattn_Wo"].T.reshape(16, 96, 2, 512)
    a["wo0"] = c(wo0.transpose(2, 1, 0, 3).reshape(2, 96, 16 * 512))
    for name, w in (("wq_a", i["L0_attn_w_q"].T), ("wk_a", i["L0_attn_w_k"].T), ("wv_a", i["L0_attn_w_v"].T),
                    ("wo_a", i["L0_attn_w_out"].T), ("wq1", i["L1_xattn_Wq"]), ("wo1", i["L1_xattn_Wo"]),
                    ("wq_b", i["L1_attn_Wq"]), ("wo_b", i["L1_attn_Wo"])):
        a[name] = tiled(w, 512)
    a["wkv_b"] = tiled(np.concatenate([i["L1_attn_Wk"], i["L1_attn_Wv"]], axis=1), 512)[0]
    a["route"] = tiled(np.concatenate([i["L0_ffn_route_w"], i["L0_ffn_A"].reshape(128, 1024)], axis=0).T, 136)[0]
    f = np.float32
    freq = f(1.0) / f(10000.0) ** (np.arange(0, 64, 2, dtype=f) / f(64))
    angles = np.repeat(np.arange(256, dtype=f)[:, None] * freq[None, :], 2, axis=1).reshape(2, P_, 64)
    a["cos_a"], a["sin_a"] = (c(g(angles).transpose(1, 0, 2)) for g in (np.cos, np.sin))
    a["cos_b"], a["sin_b"] = (c(i[n][:256].reshape(2, P_, 32).transpose(1, 0, 2))
                              for n in ("L1_attn_cos", "L1_attn_sin"))
    q = np.arange(P_)[:, None]
    keys = np.arange(2 * P_)[None, :]
    a["mask"] = np.where(np.concatenate([keys[:, :P_] <= q, keys <= q + P_], axis=1), f(0), f(-1e30)).astype(f)
    a["rank"] = np.tile(np.arange(8, 0, -1, dtype=f), (P_, 1))
    a["rms_weight"] = i["L1_ffn_rmsnorm_weight"]
    a["ffn_w0"], a["ffn_w1"], a["ffn_w2"] = i["L1_ffn_Wg"], i["L1_ffn_Wu"], i["L1_ffn_Wd"]
    a["lora_b"] = c(i["L0_ffn_Bw"].transpose(0, 2, 1).reshape(128, 1024))
    return a


def kernel(**inputs):
    from concourse import bacc
    from concourse.bass_utils import run_bass_kernel_spmd

    arrays = {f"in_{n}_dram": np.ascontiguousarray(v)
              for n, v in layouts({n: np.asarray(v) for n, v in inputs.items()}).items()}
    nc = bacc.Bacc("TRN2", target_bir_lowering=False, num_devices=1)
    a = {n[3:-5]: nc.dram_tensor(n, v.shape, mybir.dt.from_np(v.dtype), kind="ExternalInput").ap()
         for n, v in arrays.items()}
    out = nc.dram_tensor("out_0_dram", (1, 256, 1024), F32, kind="ExternalOutput").ap()
    program(nc, a, out)
    result = run_bass_kernel_spmd(nc, [arrays], core_ids=[0])
    return result.results[0]["out_0_dram"]
```

```python
from contextlib import ExitStack

import numpy as np

import concourse.bass as bass
from concourse import mybir

F32 = mybir.dt.float32
F32R = mybir.dt.float32r
BF16 = mybir.dt.bfloat16
ALU = mybir.AluOpType
ACT = mybir.ActivationFunctionType
AX_X = mybir.AxisListType.X

P = 128
BANK = 512
ROUND = 12582912.0
QMAX = 127.0


class Signal:

    def __init__(self, semaphore):
        self.semaphore, self.value = semaphore, 0

    def after(self, instruction, step=1):
        instruction.then_inc(self.semaphore, step)
        self.value += step
        return (self, self.value)


class Feed:

    def __init__(self, queue, wait, buffers, signals, pieces, first=()):
        self.queue, self.wait, self.buffers, self.signals = queue, wait, buffers, signals
        self.pieces, self.loaded, self.taken = pieces, [], 0
        for _ in range(min(len(buffers), len(pieces))):
            self.load(first)

    def load(self, events):
        n = len(self.loaded)
        if n == len(self.pieces):
            return
        slot = n % len(self.buffers)
        self.wait(self.queue, *events)
        for destination, source in self.pieces[n](self.buffers[slot]):
            event = self.signals[slot].after(self.queue.dma_start(destination, source), 16)
        self.loaded.append(event)

    def take(self):
        n = self.taken
        self.taken += 1
        return self.buffers[n % len(self.buffers)], self.loaded[n]

    def release(self, *events):
        self.load(events)


def build(nc, a, out, stop=99):
    T = 256
    D = 1024
    CTX = 4096
    TT, KT = T // P, D // P
    waited = {}

    with ExitStack() as ctx:
        def signal(name):
            return Signal(ctx.enter_context(nc.semaphore(name)))

        def wait(engine, *events):
            for event in events:
                if event is None:
                    continue
                s, value = event
                if waited.get((id(engine), id(s)), 0) < value:
                    engine.wait_ge(s.semaphore, value)
                    waited[(id(engine), id(s))] = value

        pe, act, dve, pool, sp = nc.tensor, nc.scalar, nc.vector, nc.gpsimd, nc.sync
        pe_done, act_done, dve_done, pool_done = (signal(f"{n}_done") for n in ("pe", "act", "dve", "pool"))
        PE, ACTE, DVE, POOL = pe_done.after, act_done.after, dve_done.after, pool_done.after

        def so_far(engine_done):
            return (engine_done, engine_done.value)

        def sb(stack, name, shape, dtype=F32):
            return stack.enter_context(nc.sbuf_tensor(name, shape, dtype))

        psum = ctx.enter_context(nc.psum_tensor("psum", [P, 8, BANK], F32))
        bank_read = [None] * 8
        const_in, x_in, small_dma = signal("const_in"), signal("x_in"), signal("small_dma")
        panel_in = [signal(f"panel_in{i}") for i in range(3)]

        x = sb(ctx, "x", [P, TT, D])
        ident = sb(ctx, "ident", [P, P])
        stats = sb(ctx, "stats", [P, TT, 2, 6])
        moments = sb(ctx, "moments", [P, TT, 2])
        tiny = sb(ctx, "tiny", [P, 8, TT])
        FF = 2752
        FT = -(-FF // P)
        NQ = 2 * FT + KT
        w_scale = sb(ctx, "w_scale", [P, NQ])
        w_inverse = sb(ctx, "w_inverse", [P, NQ])
        w_top = sb(ctx, "w_top", [P, NQ])
        ident_b = sb(ctx, "ident_b", [P, P], BF16)
        scales_set = POOL(pool.memset(w_scale[:], 1.0))
        x_in.after(sp.dma_start(x[:], a["x"].rearrange("a (t p) d -> p (a t) d", p=P)), 16)
        const_ready = const_in.after(sp.dma_start(ident[:], a["ident"]), 16)
        wait(act, const_ready)
        ident_ready = ACTE(act.activation(ident_b[:], ident[:], ACT.Copy))
        x_ready = (x_in, 16)
        stats_ready = None

        def inverse_root(variance, eps, ready, factor=1.0, meanwhile=None):
            v, sd, r, w = (tiny[:, i, :] for i in range(4))
            wait(dve, ready)
            e = DVE(dve.tensor_scalar(v, variance, factor, eps, ALU.mult, ALU.add))
            wait(act, e)
            e = ACTE(act.activation(sd, v, ACT.Sqrt))
            if meanwhile:
                meanwhile()
            wait(dve, e)
            wait(dve, DVE(dve.reciprocal(r, sd)))
            wait(dve, DVE(dve.tensor_tensor(w, v, r, ALU.mult)))
            wait(dve, DVE(dve.tensor_tensor(w, w, r, ALU.mult)))
            wait(dve, DVE(dve.tensor_scalar(w, w, -0.5, 1.5, ALU.mult, ALU.add)))
            return r, DVE(dve.tensor_tensor(r, r, w, ALU.mult))

        def take_stats(t, h):
            return DVE(dve.bn_stats(stats[:, t, h, :], x[:, t, h * BANK:(h + 1) * BANK]))

        def layernorm(xn, free=()):
            wait(dve, stats_ready, *free)
            for t in range(TT):
                e = DVE(dve.bn_aggr(moments[:, t, :], stats[:, t].rearrange("p h s -> p (h s)")))
            r, e = inverse_root(moments[:, :, 1], 1e-5, e)
            wait(dve, e)
            for t in range(TT):
                e = DVE(dve.tensor_scalar(xn[:, t, :], x[:, t, :], moments[:, t, 0:1], r[:, t:t + 1],
                                          ALU.subtract, ALU.mult))
            return e

        def turn(src, dst, ready, banks, cols=D, free=()):
            done = []
            wait(pe, ready, const_ready)
            for i in range(cols // P // 2):
                b = banks[i % len(banks)]
                wait(pe, bank_read[b])
                for j in range(2):
                    for t in range(TT):
                        k = 2 * i + j
                        c = (j * TT + t) * P
                        e = PE(pe.transpose(psum[:, b, c:c + P], src[:, t, k * P:k * P + P], ident[:]))
                copy = psum[:, b, :].rearrange("p (j n) -> p j n", j=2)
                if i % 2:
                    wait(dve, e, *free)
                    bank_read[b] = DVE(dve.tensor_copy(dst[:, 2 * i:2 * i + 2, :], copy))
                else:
                    wait(act, e, *free)
                    bank_read[b] = ACTE(act.activation(dst[:, 2 * i:2 * i + 2, :], copy, ACT.Copy))
                done.append(bank_read[b])
            return done

        def halve(src, high, low, ready, free=(), low_free=()):
            wait(act, *ready, *free)
            e_high = ACTE(act.activation(high, src, ACT.Copy))
            wait(dve, e_high, *free, *low_free)
            return e_high, DVE(dve.tensor_tensor(low, src, high.bitcast(F32), ALU.subtract))

        def turn_split(src, high, low, ready, banks, free=()):
            done = []
            wait(pe, ready, const_ready)
            for i in range(KT // 2):
                b = banks[i % len(banks)]
                wait(pe, bank_read[b])
                for j in range(2):
                    for t in range(TT):
                        k = 2 * i + j
                        c = (j * TT + t) * P
                        e = PE(pe.transpose(psum[:, b, c:c + P], src[:, t, k * P:k * P + P], ident[:]))
                bank = psum[:, b, :].rearrange("p (j n) -> p j n", j=2)
                _, bank_read[b] = halve(bank, high[:, 2 * i:2 * i + 2, :], low[:, 2 * i:2 * i + 2, :], [e], free)
                done.append(bank_read[b])
            return done

        class Panel:

            def __init__(self, tile, rows, k=P):
                self.tile, self.rows, self.k = tile, rows, k

            def ap(self, r, width):
                return self.tile[0:self.k, r * width:(r + 1) * width]

        class Panels:

            def __init__(self, feed, shapes):
                self.feed, self.shapes, self.n = feed, shapes, 0

            def take(self):
                tile, arrived = self.feed.take()
                rows, k = self.shapes[self.n]
                self.n += 1
                return Panel(tile, rows, k), arrived

            def release(self, *events):
                self.feed.release(*events)

        class Splitter:
            UNIT = 2

            def __init__(self, tiles, panels, count):
                self.panels, self.left = panels, count
                self.free = []
                self.ready, self.taken = [], []
                self.panel, self.row = None, 0
                self.grow(tiles)

            def grow(self, tiles):
                self.free += [(pair, None) for pair in tiles]

            def ahead(self):
                if self.free:
                    self.prepare()

            def prepare(self):
                if self.panel is None:
                    if not self.left:
                        return
                    self.left -= 1
                    (self.panel, self.arrived), self.row = self.panels.take(), 0
                k, at = self.panel.k, slice(self.row * BANK, (self.row + self.UNIT) * BANK)
                pair, read = self.free.pop(0)
                _, e = halve(self.panel.tile[0:k, at], pair[0][0:k, :], pair[1][0:k, :], [self.arrived], [read])
                self.ready.append((pair, k, e))
                self.row += self.UNIT
                if self.row == self.panel.rows:
                    self.panels.release(e)
                    self.panel = None

            def take(self):
                pair, k, event = self.ready.pop(0)
                self.taken.append(pair)
                return Panel(pair[0], self.UNIT, k), Panel(pair[1], self.UNIT, k), event

            def release(self, event):
                self.free.append((self.taken.pop(0), event))
                self.prepare()

        def linear_split(stationary, splitter, halves, banks, consume, beside=None):
            for n in range(halves):
                own = [banks[(TT * n + t) % len(banks)] for t in range(TT)]
                wait(pe, *(bank_read[b] for b in own))
                k = 0
                while k < len(stationary):
                    w_high, w_low, arrived = splitter.take()
                    wait(pe, arrived)
                    for r in range(w_high.rows):
                        high, low, ready = stationary[k]
                        wait(pe, ready)
                        for t in range(TT):
                            o, ts = psum[:, own[t], :], slice(t * P, (t + 1) * P)
                            pe.matmul(o, high[:, ts], w_high.ap(r, BANK), start=k == 0, stop=False)
                            pe.matmul(o, high[:, ts], w_low.ap(r, BANK), start=False, stop=False)
                            mm = pe.matmul(o, low[:, ts], w_high.ap(r, BANK), start=False,
                                           stop=k == len(stationary) - 1)
                        k += 1
                    e = PE(mm)
                    if k < len(stationary):
                        splitter.release(e)
                        if beside and k in (4, 8):
                            beside.pop(0)()
                last = consume is add_to_x
                if not last:
                    splitter.release(e)
                for t in range(TT):
                    bank_read[own[t]] = consume(n, t, psum[:, own[t], :], e)
                if last:
                    splitter.release(e)
                if beside and len(stationary) == 8:
                    beside.pop(0)()

        def linear(stationary, ready, panels, halves, banks, consume, width=BANK):
            wait(pe, *ready)
            for n in range(halves):
                own = [banks[(TT * n + t) % len(banks)] for t in range(TT)]
                wait(pe, *(bank_read[b] for b in own))
                k = 0
                while k < len(stationary):
                    w, arrived = panels.take()
                    wait(pe, arrived)
                    for r in range(w.rows):
                        for t in range(TT):
                            mm = pe.matmul(psum[:, own[t], 0:width], stationary[k][:, t * P:t * P + P],
                                           w.ap(r, width), start=k == 0, stop=k == len(stationary) - 1)
                        k += 1
                    e = PE(mm)
                    panels.release(e)
                for t in range(TT):
                    bank_read[own[t]] = consume(n, t, psum[:, own[t], 0:width], e)

        def add_to_x(n, t, product, event):
            nonlocal x_ready, stats_ready
            if n == 0 and t == 0:
                ACTE(act.activation(tiny[:, 7, 0:1], ident[:, 0:1], ACT.Sqrt))
            wait(dve, event)
            block = x[:, t, n * BANK:(n + 1) * BANK]
            x_ready = DVE(dve.tensor_tensor(block, product, block, ALU.add))
            read = x_ready
            wait(dve, x_ready)
            stats_ready = take_stats(t, n)
            return read

        def invert_row(rows, result, turned, few, ready):
            n = rows.shape[-1]
            wait(dve, ready)
            read = DVE(dve.transpose(turned, rows))
            wait(dve, read)
            wait(dve, DVE(dve.reciprocal(few, turned.rearrange("p (b j) -> p b j", j=32)[:, :, 0])))
            return read, DVE(dve.transpose(result, few.unsqueeze(2).broadcast_to([32, n // 32, 32])))

        H0, KV0, HD0 = 16, 4, 96
        G0 = H0 // KV0
        KV1, HD1 = 8, 32
        G1 = 4
        S0 = CTX + T
        CH = 256
        NCH = S0 // CH
        VW = P
        NS0 = S0 // P
        V1W = KV1 // 2 * 3 * HD1

        def scratch(name, shape, dtype):
            return nc.dram_tensor(name, shape, dtype, kind="Internal").ap()

        k0_high = scratch("k0_high", [KV0, HD0, S0], F32)
        k0_low = scratch("k0_low", [KV0, HD0, S0], F32)
        k1_high = scratch("k1_high", [KV1 * HD1, CTX], F32)
        k1_low = scratch("k1_low", [KV1 * HD1, CTX], F32)
        v0_high = scratch("v0_high", [KV0, P, NS0, VW], F32)
        v0_low = scratch("v0_low", [KV0, P, NS0, VW], F32)
        v1_dram = scratch("v1_dram", [P, CTX // P, V1W], F32)

        attn0 = ExitStack()
        q_high = sb(attn0, "q_high", [HD0 + 1, H0 * T], F32R)
        q_low = sb(attn0, "q_low", [HD0 + 1, H0 * T], F32R)
        top0 = sb(attn0, "top0", [P, KV0 * G0 * TT, NCH])
        neg_top0 = sb(attn0, "neg_top0", [P, KV0 * G0 * TT])
        top_high = sb(attn0, "top_high", [32, P], F32R)
        top_low = sb(attn0, "top_low", [32, P], F32R)

        kv_spilled = []
        with ExitStack() as phase:
            xnT = sb(phase, "xnT_ab", [P, KT, T])
            w_high = sb(phase, "w_high", [P, KT, 1280], F32R)
            w_low = sb(phase, "w_low", [P, KT, 1280], F32R)
            staged = [sb(phase, f"staged{i}", [P, 1280]) for i in range(4)]
            k_out = [[sb(phase, f"k_out{i}{p}", [P, 2, CH], F32R) for p in "hl"] for i in range(3)]
            v0_out = [[sb(phase, f"v0_out{i}{p}", [P, KV0, VW], F32R) for p in "hl"] for i in range(2)]
            v1_out = [sb(phase, f"v1_out{i}", [P, V1W]) for i in range(2)]
            stage_in = [signal(f"stage_in{i}") for i in range(4)]
            k_sent = [signal(f"k_sent{i}") for i in range(3)]
            v0_sent = [signal(f"v0_sent{i}") for i in range(2)]
            v1_sent = [signal(f"v1_sent{i}") for i in range(2)]

            for high, low in v0_out:
                POOL(pool.memset(high[:, :, HD0:VW].bitcast(F32), 1.0))
                POOL(pool.memset(low[:, :, HD0:VW].bitcast(F32), 0.0))
            for v in v1_out:
                ones_set = POOL(pool.memset(v[:], 1.0))

            def q_piece(h):
                return lambda s: [(s[:, 0:KT * HD0], a["wq0"][h])]

            def w_piece(k):
                return lambda s: [(s[:], a["wkv"][k])]

            def c_piece(c, half):
                return lambda s: [(s[:, 0:4 * CH], a["ctxT"][c, :, half * 4 * CH:(half + 1) * 4 * CH])]

            order = []
            for i in range(KT):
                order += [q_piece(2 * i), q_piece(2 * i + 1), w_piece(i)]
                if i == KT - 3:
                    order += [c_piece(0, 0), c_piece(0, 1)]
            for c in range(1, CTX // CH):
                order += [c_piece(c, 0), c_piece(c, 1)]
            stage = Feed(sp, wait, staged, stage_in, order)

            with ExitStack() as early:
                xn = sb(early, "xn_ab", [P, TT, D])
                wait(dve, x_ready)
                for t in range(TT):
                    for h in range(2):
                        stats_ready = take_stats(t, h)
                normed = layernorm(xn)
                turned = turn(xn, xnT, normed, [0, 1, 2, 3])
            c_high = [sb(phase, f"c_high{i}", [P, KT, CH], F32R) for i in range(2)]
            c_low = [sb(phase, f"c_low{i}", [P, KT, CH], F32R) for i in range(2)]
            chunk_read = [None] * NCH

            def split_chunk(c):
                high, low = c_high[c % 2], c_low[c % 2]
                free = chunk_read[c - 2] if c >= 2 else None
                for half in range(2):
                    ks = slice(4 * half, 4 * half + 4)
                    if c < CTX // CH:
                        s, arrived = stage.take()
                        src = s[:, 0:4 * CH].rearrange("p (k n) -> p k n", k=4)
                    else:
                        src, arrived = xnT[:, ks, :], None
                    wait(act, arrived, free)
                    e = ACTE(act.activation(high[:, ks, :], src, ACT.Copy))
                    wait(dve, e, free)
                    e = DVE(dve.tensor_tensor(low[:, ks, :], src, high[:, ks, :].bitcast(F32), ALU.subtract))
                    if c < CTX // CH:
                        stage.release(e)
                return e

            queries = []
            for h in range(H0):
                b = 4 + h % 4
                w, arrived = stage.take()
                wait(pe, arrived, bank_read[b], *turned)
                for k in range(KT):
                    mm = pe.matmul(psum[0:HD0, b, 0:T], w[:, k * HD0:(k + 1) * HD0], xnT[:, k, :],
                                   start=k == 0, stop=k == KT - 1)
                e = PE(mm)
                stage.release(e)
                cols = slice(h * T, (h + 1) * T)
                wait(act, e)
                e_high = ACTE(act.activation(q_high[0:HD0, cols], psum[0:HD0, b, 0:T], ACT.Copy))
                wait(dve, e_high)
                bank_read[b] = DVE(dve.tensor_tensor(q_low[0:HD0, cols], psum[0:HD0, b, 0:T],
                                                     q_high[0:HD0, cols].bitcast(F32), ALU.subtract))
                queries.append(bank_read[b])
                if h % 2:
                    i = h // 2
                    w, arrived = stage.take()
                    wait(act, arrived)
                    e = ACTE(act.activation(w_high[:, i, :], w[:], ACT.Copy))
                    wait(dve, e)
                    weights_split = DVE(dve.tensor_tensor(w_low[:, i, :], w[:],
                                                          w_high[:, i, :].bitcast(F32), ALU.subtract))
                    stage.release(weights_split)
                    if i == KT - 3:
                        split = [split_chunk(0)]

            bank_turn = 0

            def next_bank():
                nonlocal bank_turn
                bank_turn += 1
                return (bank_turn - 1) % 8

            k_slot = v_slot = 0
            k_slot_free = [()] * 3
            for c in range(NCH):
                latents = c == NCH - 1
                if not latents:
                    split.append(split_chunk(c + 1))
                high, low = c_high[c % 2], c_low[c % 2]
                at = slice(c * CH, (c + 1) * CH)
                wait(pe, split[c], weights_split)
                pending = []

                def take_maximum():
                    if not pending:
                        return
                    head, g, slot, e_high = pending.pop(0)
                    b = next_bank()
                    wait(pe, e_high, *queries, bank_read[b])
                    for i in range(2):
                        q0 = head * G0 * T + (g + i) * P
                        mm = pe.matmul(psum[:, b, i * CH:(i + 1) * CH], q_high[0:HD0, q0:q0 + P],
                                       k_out[slot][0][0:HD0, head % 2, :], start=True, stop=True)
                    e = PE(mm)
                    k_slot_free[slot] = k_slot_free[slot] + (e,)
                    wait(dve, e)
                    r0 = head * G0 * TT + g
                    bank_read[b] = DVE(dve.tensor_reduce(
                        top0[:, r0:r0 + 2, c], psum[:, b, :].rearrange("p (i n) -> p i n", i=2), AX_X, ALU.max))

                for pair in range(2 if latents else 3):
                    tiles = (0, 1) if pair < 2 else (0,)
                    m = HD0 if latents else P
                    b = next_bank()
                    wait(pe, bank_read[b])
                    for j in tiles:
                        col = (2 * pair + j) * P
                        for k in range(KT):
                            if k % (2 * len(tiles)) == 1:
                                take_maximum()
                            o = psum[0:m, b, j * CH:(j + 1) * CH]
                            pe.matmul(o, w_high[:, k, col:col + m], high[:, k, :], start=k == 0, stop=False)
                            pe.matmul(o, w_high[:, k, col:col + m], low[:, k, :], start=False, stop=False)
                            mm = pe.matmul(o, w_low[:, k, col:col + m], high[:, k, :], start=False,
                                           stop=k == KT - 1)
                    e = PE(mm)
                    slot = k_slot % 3
                    k_slot += 1
                    n = len(tiles)
                    src = psum[0:m, b, 0:n * CH].rearrange("p (j n) -> p j n", j=n)
                    kh, kl = (k_out[slot][i][0:m, 0:n, :] for i in range(2))
                    wait(act, e, *k_slot_free[slot])
                    e_high = ACTE(act.activation(kh, src, ACT.Copy))
                    wait(dve, e_high, *k_slot_free[slot])
                    bank_read[b] = DVE(dve.tensor_tensor(kl, src, kh.bitcast(F32), ALU.subtract))
                    wait(sp, bank_read[b])
                    for part, k0d, k1d in ((0, k0_high, k1_high), (1, k0_low, k1_low)):
                        o = k_out[slot][part][:].bitcast(F32)
                        if pair < 2:
                            e = k_sent[slot].after(sp.dma_start(
                                k0d[2 * pair:2 * pair + 2, :, at].rearrange("h d n -> d h n"), o[0:HD0, :, :]), 16)
                            if not latents:
                                e = k_sent[slot].after(sp.dma_start(
                                    k1d[2 * pair * HD1:(2 * pair + 2) * HD1, at].rearrange(
                                        "(h d) n -> d h n", d=HD1), o[HD0:P, :, :]), 16)
                        else:
                            e = k_sent[slot].after(sp.dma_start(k1d[P:2 * P, at], o[:, 0, :]), 16)
                    k_slot_free[slot] = (e,)
                    if pair < 2:
                        pending += [(2 * pair + j, g, slot, e_high) for j in range(2) for g in range(0, G0 * TT, 2)]

                for s in range(CH // P):
                    ts = slice(s * P, (s + 1) * P)
                    b0, b1 = next_bank(), next_bank()
                    wait(pe, bank_read[b0], bank_read[b1])
                    outs = [(psum[:, b0, 0:KV0 * HD0], slice(640, 1024))]
                    if not latents:
                        outs.append((psum[:, b1, 0:KV1 * HD1], slice(1024, 1280)))
                    for k in range(KT):
                        if k % 2:
                            take_maximum()
                        for tokens, weights in ((high, w_high), (high, w_low), (low, w_high)):
                            for o, cols in outs:
                                mm = pe.matmul(o, tokens[:, k, ts], weights[:, k, cols],
                                               start=k == 0 and tokens is high and weights is w_high,
                                               stop=k == KT - 1 and tokens is low)
                    e = PE(mm)
                    if s == CH // P - 1:
                        chunk_read[c] = e
                    slot = v_slot % 2
                    v_slot += 1
                    row = c * (CH // P) + s
                    _, bank_read[b0] = halve(
                        outs[0][0].rearrange("p (h d) -> p h d", h=KV0), v0_out[slot][0][:, :, 0:HD0],
                        v0_out[slot][1][:, :, 0:HD0], [e], [ones_set, so_far(v0_sent[slot])])
                    wait(sp, bank_read[b0])
                    for part, v0d in enumerate((v0_high, v0_low)):
                        v0_sent[slot].after(sp.dma_start(v0d[:, :, row, :].rearrange("h p d -> p h d"),
                                                         v0_out[slot][part][:].bitcast(F32)), 16)
                    if not latents:
                        wait(dve, e, ones_set, (v1_sent[slot], v1_sent[slot].value))
                        bank_read[b1] = DVE(dve.tensor_copy(
                            v1_out[slot][:].rearrange("p (q b d) -> p q b d", b=3, d=HD1)[:, :, 0:3:2, :],
                            outs[1][0].rearrange("p (q b d) -> p q b d", b=2, d=HD1)))
                        wait(sp, bank_read[b1])
                        v1_sent[slot].after(sp.dma_start(v1_dram[:, row, :], v1_out[slot][:]), 16)
                while pending:
                    take_maximum()
            kv_spilled = [(s, s.value) for s in (*k_sent, *v0_sent, *v1_sent)]

            wait(dve, bank_read[(bank_turn - 1) % 8], *bank_read)
            e = DVE(dve.tensor_reduce(neg_top0[:], top0[:], AX_X, ALU.max, negate=True))
            b = next_bank()
            wait(pe, e, bank_read[b])
            e = PE(pe.transpose(psum[0:32, b, 0:P], neg_top0[:], ident[:]))
            wait(act, e)
            e = ACTE(act.activation(top_high[:], psum[0:32, b, 0:P], ACT.Copy))
            wait(dve, e)
            bank_read[b] = DVE(dve.tensor_tensor(top_low[:], psum[0:32, b, 0:P], top_high[:].bitcast(F32),
                                                 ALU.subtract))
            wait(sp, bank_read[b], e)
            for q, top in ((q_high, top_high), (q_low, top_low)):
                tops_placed = small_dma.after(sp.dma_start(
                    q[HD0:HD0 + 1, :].bitcast(F32).rearrange("o (r n) -> o r n", n=P), top[:].bitcast(F32)), 16)
            last_of_b = [so_far(pe_done), so_far(act_done), so_far(dve_done), *kv_spilled]

        q_dram = scratch("q_dram", [2 * FT, P, KT * P], BF16)
        qd_dram = scratch("qd_dram", [KT, P, FT * P], BF16)
        ws_dram = scratch("ws_dram", [NQ, P], F32)
        q_spilled = [signal(f"q_spilled{i}") for i in range(2)]
        wf_in = [signal(f"wf_in{i}") for i in range(2)]

        class Quantiser:

            def __init__(self, stack, banks):
                self.rows = [sb(stack, f"wf_rows{i}", [P, FF]) for i in range(2)]
                self.ints = [sb(stack, f"wf_ints{i}", [P, FF], BF16) for i in range(2)]
                self.turned = [sb(stack, f"wf_turned{i}", [P, FT * P], BF16) for i in range(2)]
                self.top_first = sb(stack, "top_first", [P, 1])
                self.turned_read, self.ints_read = [None] * 2, [None] * 2
                self.banks, self.n, self.rounded, self.shifted = banks, 0, {}, {}

            def start(self, first):
                pieces = [self.piece(n) for n in range(NQ)]
                self.feed = Feed(sp, wait, self.rows, wf_in, pieces, first)

            def shape(self, n):
                if n < 2 * FT:
                    i = n % FT
                    return n // FT, i, min(P, FF - i * P), D
                return 2, n - 2 * FT, P, FF

            def piece(self, n):
                which, i, rows, cols = self.shape(n)
                return lambda tile: [(tile[0:rows, 0:cols], a[f"ffn_w{which}"][i * P:i * P + rows, :])]

            def reduce_first(self, n):
                _, _, rows, cols = self.shape(n)
                self.first_part = cols // 3 * 2
                w, arrived = self.feed.take()
                wait(dve, arrived)
                self.taken = w, DVE(dve.tensor_reduce(self.top_first[:], w[:, 0:self.first_part], AX_X, ALU.max,
                                                      apply_absolute_value=True))

            def quantise(self, n):
                which, _, rows, cols = self.shape(n)
                top, scale, inv = (z[0:rows, n:n + 1] for z in (w_top, w_scale, w_inverse))
                if which == 2:
                    w, e = self.taken
                    wait(dve, DVE(dve.tensor_reduce(top, w[:, self.first_part:cols], AX_X, ALU.max,
                                                    apply_absolute_value=True)), e)
                    wait(dve, DVE(dve.tensor_tensor(top, top, self.top_first[:], ALU.max)))
                    w = w[:, 0:cols]
                else:
                    w, arrived = self.feed.take()
                    w = w[0:rows, 0:cols]
                    wait(dve, arrived, scales_set)
                    wait(dve, DVE(dve.tensor_reduce(top, w, AX_X, ALU.max, apply_absolute_value=True)))
                wait(dve, DVE(dve.tensor_scalar(scale, top, 1.0 / QMAX, 1e-8, ALU.mult, ALU.max)))
                e = DVE(dve.reciprocal(inv, scale))
                wait(pool, e, so_far(pool_done))
                self.shifted[n] = (w, POOL(pool.tensor_scalar(w, w, inv, ROUND, ALU.mult, ALU.add)))

            def settle(self, n):
                _, _, rows, cols = self.shape(n)
                w, e = self.shifted.pop(n)
                wait(pool, e, self.ints_read[n % 2])
                self.rounded[n] = POOL(pool.tensor_scalar(self.ints[n % 2][0:rows, 0:cols], w, -ROUND, 1.0,
                                                          ALU.add, ALU.mult))
                self.feed.release(self.rounded[n])

            def turn(self, n, engine, blocks_from=0, blocks_to=None):
                which, i, rows, cols = self.shape(n)
                ints, out_tile = self.ints[n % 2], self.turned[n % 2]
                blocks = -(-cols // P)
                last = min(blocks, blocks_to or blocks)
                wait(pe, self.rounded[n], ident_ready, const_ready)
                for b0 in range(blocks_from, last, 8):
                    b = self.banks[(b0 // 8 + n) % 2]
                    some = range(b0, min(b0 + 8, blocks))
                    bank = psum[:, b, :].bitcast(BF16).rearrange("p (k n) -> p k n", n=P)
                    wait(pe, bank_read[b])
                    for k in some:
                        width = min(P, cols - k * P)
                        e = PE(pe.transpose(bank[0:width, k - b0, 0:rows], ints[0:rows, k * P:k * P + width],
                                            ident_b[0:rows, 0:rows]))
                    full = [k for k in some if cols - k * P >= P]
                    jobs = [(P, full[0], len(full))] if full else []
                    if len(full) < len(some):
                        jobs.append((cols % P, some[-1], 1))
                    for height, k0, count in jobs:
                        dst = out_tile[0:height, k0 * P:(k0 + count) * P].rearrange("p (k n) -> p k n", n=P)[:, :, 0:rows]
                        src = bank[0:height, k0 - b0:k0 - b0 + count, 0:rows]
                        if engine is act:
                            wait(act, e, self.turned_read[n % 2])
                            done = ACTE(act.activation(dst, src, ACT.Copy))
                        else:
                            wait(dve, e, self.turned_read[n % 2])
                            done = DVE(dve.tensor_copy(dst, src))
                    bank_read[b] = done
                if last < blocks:
                    return
                self.ints_read[n % 2] = e
                wait(sp, done)
                if which < 2:
                    pairs = [(q_dram[n], out_tile[:, 0:KT * P])] if rows == P else [
                        (q_dram[n].rearrange("p (k n) -> p k n", n=P)[:, :, 0:rows],
                         out_tile[:, 0:KT * P].rearrange("p (k n) -> p k n", n=P)[:, :, 0:rows])]
                else:
                    whole = FF // P * P
                    pairs = [(qd_dram[i, :, 0:whole], out_tile[:, 0:whole]),
                             (qd_dram[i, 0:FF - whole, whole:], out_tile[0:FF - whole, whole:])]
                for destination, source in pairs:
                    self.turned_read[n % 2] = q_spilled[n % 2].after(sp.dma_start(destination, source), 16)

            def turn_last(self):
                if 0 <= self.n - 2 < NQ:
                    self.turn(self.n - 2, dve)
                if 0 <= self.n - 1 < NQ:
                    self.settle(self.n - 1)

            def step(self, n):
                if self.finished():
                    return
                if self.n < 2 * FT:
                    if n % 2 == 1:
                        self.turn_last()
                        self.quantise(self.n)
                        self.n += 1
                elif n % 4 == 1:
                    if self.shape(self.n - 2)[0] < 2:
                        self.turn(self.n - 2, dve)
                    else:
                        self.turn(self.n - 2, dve, 0, 16)
                elif n % 4 == 2 and self.n < NQ:
                    self.reduce_first(self.n)
                elif n % 4 == 3:
                    if self.shape(self.n - 2)[0] == 2:
                        self.turn(self.n - 2, dve, 16)
                    if self.n - 1 < NQ:
                        self.settle(self.n - 1)
                    if self.n < NQ:
                        self.quantise(self.n)
                    self.n += 1

            def finished(self):
                return self.n > NQ + 1

        panel_stack = ExitStack()
        panel_tiles = [panel_stack.enter_context(nc.sbuf_tensor(f"panel{i}", [P, KT // 2 * BANK], F32, side="right"))
                       for i in range(3)]
        plan = []

        def panel(source, rows, width, k=P):
            plan.append((source, rows, width, k))

        def halved(name, rows=KT, k=P):
            for half in range(2):
                for first in range(0, rows, 4):
                    panel(a[name][half, :, first * BANK:(first + 4) * BANK], 4, BANK, k)

        halved("wo0", H0, HD0)
        for name in ("wq_a", "wk_a", "wv_a", "wo_a"):
            halved(name)
        panel(a["route"], KT, 136)
        panel(a["lora_b"], 2, BANK)
        for name in ("wq1", "wo1", "wq_b"):
            halved(name)
        for first in (0, 4):
            panel(a["wkv_b"][:, first * BANK:(first + 4) * BANK], 4, BANK)
        halved("wo_b")

        def panel_piece(source, rows, width, k):
            return lambda tile: [(tile[0:k, 0:rows * width], source)]

        def split_tiles(stack, name, slots):
            return [[stack.enter_context(nc.sbuf_tensor(f"{name}{i}{part}", [P, Splitter.UNIT * BANK], F32R,
                                                        side="right")) for part in "hl"] for i in range(slots)]

        split_stack = ExitStack()
        with ExitStack() as phase:
            SC = 512
            key_high = [sb(phase, f"key_high{i}", [HD0 + 1, SC], F32R) for i in range(4)]
            key_low = [sb(phase, f"key_low{i}", [HD0, SC], F32R) for i in range(4)]
            value_high = [sb(phase, f"value_high{i}", [P, SC // P, VW], F32R) for i in range(4)]
            value_low = [sb(phase, f"value_low{i}", [P, SC // P, VW], F32R) for i in range(4)]
            probs = [sb(phase, f"probs{i}", [P, G0 * T]) for i in range(2)]
            probs_high = [sb(phase, f"probs_high{i}", [P, G0 * T], F32R) for i in range(3)]
            probs_low = [sb(phase, f"probs_low{i}", [P, G0 * T], F32R) for i in range(3)]
            raw = sb(phase, "raw0", [HD0, G0 * T])
            sums = sb(phase, "sums0", [32, G0 * T])
            few = sb(phase, "few0", [32, G0 * T // 32])
            inverse = sb(phase, "inverse0", [HD0, G0 * T])
            kv_in = [signal(f"kv_in{i}") for i in range(4)]
            quantiser_stack = ExitStack()
            quantiser = Quantiser(quantiser_stack, (6, 7))
            wait(pool, *last_of_b)
            for k in key_high:
                wait(pool, so_far(pool_done))
                ones_set = POOL(pool.memset(k[HD0:HD0 + 1, :].bitcast(F32), 1.0))

            def kv_piece(kv, first):
                n = min(SC, S0 - first)

                def dmas(slot):
                    high, low, v_high, v_low = slot
                    return [(high[0:HD0, 0:n].bitcast(F32), k0_high[kv, :, first:first + n]),
                            (low[:, 0:n].bitcast(F32), k0_low[kv, :, first:first + n]),
                            (v_high[:, 0:n // P, :].bitcast(F32), v0_high[kv, :, first // P:(first + n) // P, :]),
                            (v_low[:, 0:n // P, :].bitcast(F32), v0_low[kv, :, first // P:(first + n) // P, :])]
                return dmas

            pieces = [kv_piece(kv, first) for kv in range(KV0) for first in range(0, S0, SC)]
            feed = Feed(sp, wait, list(zip(key_high, key_low, value_high, value_low)), kv_in, pieces,
                        first=last_of_b)
            quantiser.start(last_of_b)
            panels = Panels(Feed(sp, wait, panel_tiles, panel_in, [panel_piece(*p) for p in plan], first=last_of_b),
                            [(rows, k) for _, rows, _, k in plan])
            steps = [(kv, s) for kv in range(KV0) for s in range(NS0)]
            low_done, pv_done, held = {}, {}, {}
            scale = float(1.0 / np.sqrt(np.float32(HD0)))

            def scores(n):
                kv, s = steps[n]
                if s % (SC // P) == 0:
                    held["now"] = feed.take()
                (high, low, *held[n]), arrived = held["now"]
                wait(pe, arrived, tops_placed, ones_set)
                at = slice(s % 4 * P, s % 4 * P + P)
                for half in range(2):
                    b = 2 * (n % 2) + half
                    wait(pe, bank_read[b])
                    q = slice(kv * G0 * T + half * BANK, kv * G0 * T + (half + 1) * BANK)
                    pe.matmul(psum[:, b, :], high[:, at], q_high[:, q], start=True, stop=False)
                    pe.matmul(psum[:, b, :], high[:, at], q_low[:, q], start=False, stop=False)
                    mm = pe.matmul(psum[:, b, :], low[:, at], q_high[0:HD0, q], start=False, stop=True)
                e = PE(mm)
                both = psum[:, 2 * (n % 2):2 * (n % 2) + 2, :].rearrange("p b n -> p (b n)")
                wait(act, e, pv_done.get(n - 3), low_done.get(n - 2))
                ACTE(act.activation(probs_high[n % 3][:], both, ACT.Exp, scale=scale))
                e = ACTE(act.activation(probs[n % 2][:], both, ACT.Exp, scale=scale))
                bank_read[2 * (n % 2)] = bank_read[2 * (n % 2) + 1] = e
                wait(dve, e, pv_done.get(n - 3))
                low_done[n] = DVE(dve.tensor_tensor(probs_low[n % 3][:], probs[n % 2][:],
                                                    probs_high[n % 3][:].bitcast(F32), ALU.subtract))

            def weigh(n):
                kv, s = steps[n]
                wait(pe, low_done[n])
                v_high, v_low = (v[:, s % 4, :] for v in held.pop(n))
                for half in range(2):
                    wait(pe, bank_read[4 + half])
                    o, cols = psum[:, 4 + half, :], slice(half * BANK, (half + 1) * BANK)
                    p_high, p_low = probs_high[n % 3][:, cols], probs_low[n % 3][:, cols]
                    pe.matmul(o, v_high, p_high, start=s == 0, stop=False)
                    pe.matmul(o, v_high, p_low, start=False, stop=False)
                    halves_done[half] = PE(pe.matmul(o, v_low, p_high, start=False, stop=s == NS0 - 1))
                pv_done[n] = halves_done[1]
                if s % 4 == 3 or s == NS0 - 1:
                    feed.release(pv_done[n])
                if s == NS0 - 1:
                    for half in range(2):
                        cols = slice(half * BANK, (half + 1) * BANK)
                        wait(act, halves_done[half], normalised[0])
                        e_raw = ACTE(act.activation(raw[:, cols], psum[0:HD0, 4 + half, :], ACT.Copy))
                        read, inverted = invert_row(psum[HD0:P, 4 + half, :], inverse[0:32, cols], sums[:, cols],
                                                    few[:, half * 16:(half + 1) * 16], e_raw)
                        bank_read[4 + half] = read
                    wait(dve, inverted)
                    for row in (32, 64):
                        e = DVE(dve.tensor_copy(inverse[row:row + 32, :], inverse[0:32, :]))
                    wait(dve, e)
                    e = DVE(dve.tensor_tensor(raw[:], raw[:], inverse[:], ALU.mult))
                    cols = slice(kv * G0 * T, (kv + 1) * G0 * T)
                    later.append((lambda cols=cols, e=e: halve(raw[:], q_high[0:HD0, cols], q_low[0:HD0, cols], [e])))

            normalised, halves_done, later = [None], [None, None], []
            splitter, outputs_split = None, []
            scores(0)
            scores(1)
            for n in range(len(steps)):
                if n + 2 < len(steps):
                    scores(n + 2)
                if later and steps[n][1] in (2, NS0 - 1):
                    _, normalised[0] = later.pop(0)()
                    outputs_split.append(normalised[0])
                weigh(n)
                quantiser.step(n)
                if splitter:
                    splitter.ahead()
                if quantiser.finished() and not splitter:
                    q_all_spilled = [(s, s.value) for s in q_spilled]
                    quantiser_stack.close()
                    wait(act, *quantiser.turned_read, *quantiser.ints_read)
                    splitter = Splitter(split_tiles(split_stack, "panel_ab", 4), panels, 8 + 16)
            _, attended = later.pop(0)()
            outputs_split.append(attended)
            last_of_c = [attended, pv_done[len(steps) - 1]]

        heads = [slice(h * T, (h + 1) * T) for h in range(H0)]
        linear_split([(q_high[0:HD0, h], q_low[0:HD0, h], outputs_split[i // G0]) for i, h in enumerate(heads)],
                     splitter, 2, [0, 1, 2, 3], add_to_x)
        attn0.close()
        done = [x_ready, *last_of_c, so_far(pe_done), so_far(act_done)]
        out_done = signal("out_done")

        def finish():
            wait(sp, x_ready)
            e = out_done.after(sp.dma_start(out.rearrange("a (t p) d -> p (a t) d", p=P), x[:]), 16)
            wait(sp, e)

        if stop <= 1:
            return finish()

        mask_b = sb(ctx, "mask_b", [P, 3 * P], BF16)

        class Causal:

            def __init__(self, name, heads, kv_heads, hd, scale, interleaved):
                self.name, self.heads, self.kv_heads, self.hd = name, heads, kv_heads, hd
                self.scale, self.interleaved = scale, interleaved

            def run(self, cos_dram, sin_dram, free, splitter, load_ahead=None):
                heads, kv_heads, hd = self.heads, self.kv_heads, self.hd
                per = P // hd
                KW = kv_heads * hd
                n_ = self.name
                with ExitStack() as phase:
                    xn = sb(phase, f"xn_{n_}", [P, TT, D])
                    xnT_high = sb(phase, f"xnT_high_{n_}", [P, KT, T], F32R)
                    xnT_low = sb(phase, f"xnT_low_{n_}", [P, KT, T], F32R)
                    q_rot = sb(phase, f"q_rot_{n_}", [P, TT, D])
                    k_rot = sb(phase, f"k_rot_{n_}", [P, TT, KW])
                    v = sb(phase, f"v_{n_}", [P, TT, KW])
                    qz = sb(phase, f"qz_{n_}", [P, heads, T])
                    kT = sb(phase, f"kT_{n_}", [P, KW // P, T])
                    cos = sb(phase, f"cos_{n_}", [P, TT, hd])
                    sin = sb(phase, f"sin_{n_}", [P, TT, hd])
                    part = [sb(phase, f"part{i}_{n_}", [P, BANK]) for i in range(2)]
                    mask = part[0][:, 0:3 * P]
                    probs = [sb(phase, f"probs{i}_{n_}", [P, 3 * P]) for i in range(4)]
                    probsT = [sb(phase, f"probsT{i}_{n_}", [P, 3 * P]) for i in range(4)]
                    top = sb(phase, f"top_{n_}", [P, 2, 2, 2])
                    total = sb(phase, f"total_{n_}", [P, TT, heads])
                    inverse = sb(phase, f"inverse_{n_}", [P, TT, heads])
                    o, oT_high, oT_low = xn, xnT_high, xnT_low
                    wait(sp, *free)
                    for dst, src in ((cos, cos_dram), (sin, sin_dram), (mask, a["mask"])):
                        tables_ready = const_in.after(sp.dma_start(dst if dst is mask else dst[:], src), 16)
                    wait(pool, so_far(pool_done), *free)
                    zeroed = POOL(pool.memset(qz[:], 0.0))
                    normed = layernorm(xn, free)
                    turned = turn_split(xn, xnT_high, xnT_low, normed, [4, 5, 6, 7], free)
                    for _ in splitter.free[:]:
                        splitter.ahead()
                    wait(act, tables_ready)
                    mask_ready = ACTE(act.activation(mask_b[:], mask, ACT.Copy))

                    def halves(ap):
                        if self.interleaved:
                            v4 = ap.rearrange("p b (i two) -> p b i two", two=2)
                            return v4[:, :, :, 0], v4[:, :, :, 1]
                        return ap[:, :, 0:hd // 2], ap[:, :, hd // 2:hd]

                    part_free = None

                    def rotate(dst, src, t, event):
                        nonlocal part_free
                        cols = src.shape[-1]
                        nb = cols // hd
                        blocks = lambda ap: ap.rearrange("p (b d) -> p b d", d=hd)
                        table = lambda z: z[:, t, :].unsqueeze(1).broadcast_to([P, nb, hd])
                        one, two = (blocks(z[:, 0:cols]) for z in part)
                        src, dst = blocks(src), blocks(dst)
                        wait(dve, event, tables_ready, mask_ready, part_free)
                        DVE(dve.tensor_tensor(one, src, table(cos), ALU.mult))
                        (s1, s2), (n1, n2), (t1, t2) = halves(src), halves(table(sin)), halves(two)
                        DVE(dve.tensor_tensor(t1, s2, n1, ALU.mult))
                        read = DVE(dve.tensor_tensor(t2, s1, n2, ALU.mult))
                        wait(dve, read)
                        (o1, o2), (d1, d2) = halves(one), halves(dst)
                        DVE(dve.tensor_tensor(d1, o1, t1, ALU.subtract))
                        part_free = DVE(dve.tensor_tensor(d2, o2, t2, ALU.add))
                        return read

                    xnT_k = [(xnT_high[:, k, :], xnT_low[:, k, :], turned[k // 2]) for k in range(KT)]

                    def take_q(n, t, product, event):
                        return rotate(q_rot[:, t, n * BANK:(n + 1) * BANK], product, t, event)

                    def take_k(n, t, product, event):
                        return rotate(k_rot[:, t, n * BANK:(n + 1) * BANK], product, t, event)

                    def take_v(n, t, product, event):
                        wait(act, event)
                        return ACTE(act.activation(v[:, t, n * BANK:(n + 1) * BANK], product, ACT.Copy))

                    def take_kv(n, t, product, event):
                        wait(act, event)
                        wait(dve, ACTE(act.activation(v[:, t, :], product[:, KW:2 * KW], ACT.Copy)))
                        return rotate(k_rot[:, t, :], product[:, 0:KW], t, event)

                    placed = {}

                    def place(i):
                        b = i % 4
                        wait(pe, q_ready, const_ready, bank_read[b])
                        for j in range(2):
                            for t in range(TT):
                                k = 2 * i + j
                                c = (j * TT + t) * P
                                e = PE(pe.transpose(psum[:, b, c:c + P], q_rot[:, t, k * P:k * P + P], ident[:]))
                        for j in range(2):
                            for g in range(per):
                                head = (2 * i + j) * per + g
                                row = head * kv_heads // heads * hd % P
                                dst = qz[row:row + hd, head, :]
                                src = psum[g * hd:(g + 1) * hd, b, j * T:(j + 1) * T]
                                if i % 2:
                                    wait(dve, e, zeroed)
                                    done = DVE(dve.tensor_copy(dst, src))
                                else:
                                    wait(act, e, zeroed)
                                    done = ACTE(act.activation(dst, src, ACT.Copy))
                        bank_read[b] = placed[i] = done

                    linear_split(xnT_k, splitter, 2, [0, 1, 2, 3], take_q)
                    q_ready = part_free
                    two = [lambda: (place(0), place(1)), lambda: (place(2), place(3))]
                    if KW == D:
                        linear_split(xnT_k, splitter, 2, [4, 5, 6, 7], take_k,
                                     [lambda: None, *two])
                        k_ready = part_free
                        linear_split(xnT_k, splitter, 2, [0, 1, 2, 3], take_v)
                    else:
                        linear_split(xnT_k, splitter, 1, [4, 5, 6, 7], take_kv, two)
                        k_ready = part_free
                    v_ready = so_far(act_done)
                    k_turned = turn(k_rot, kT, k_ready, [4, 5, 6, 7], KW)
                    if load_ahead:
                        load_ahead(free)

                    scored, exps, turns, moved, weighed = {}, {}, {}, {}, {}
                    spans = (slice(0, P), slice(P, 3 * P))
                    PER = D // 4 // hd

                    def scores(h):
                        b = h % 4
                        block = h * kv_heads // heads * hd // P
                        wait(pe, bank_read[b], mask_ready, ident_ready, placed[h // per // 2], k_turned[block // 2])
                        pe.matmul(psum[:, b, 0:3 * P], ident_b[:], mask_b[:], start=True, stop=False,
                                  skip_group_check=True)
                        pe.matmul(psum[:, b, 0:P], qz[:, h, 0:P], kT[:, block, 0:P], start=False, stop=True,
                                  skip_group_check=True)
                        scored[h] = PE(pe.matmul(psum[:, b, P:3 * P], qz[:, h, P:T], kT[:, block, :],
                                                 start=False, stop=True, skip_group_check=True))

                    def soften(h):
                        b, turn_ = h % 4, h // 2 % 2
                        wait(dve, scored[h + 1], exps.get(h - 3))
                        for t in range(TT):
                            e = DVE(dve.tensor_reduce(top[:, turn_, :, t], psum[:, b:b + 2, spans[t]], AX_X, ALU.max))
                        wait(dve, e)
                        tops = top[:, turn_].rearrange("p h t -> p (h t)")
                        e = DVE(dve.tensor_scalar(tops, tops, -self.scale, None, ALU.mult))
                        for i in range(2):
                            wait(act, e, turns.get(h + i - 4))
                            for t in range(TT):
                                done = ACTE(act.activation(
                                    probs[(h + i) % 4][:, spans[t]], psum[:, b + i, spans[t]], ACT.Exp,
                                    scale=self.scale, bias=top[:, turn_, i, t:t + 1],
                                    accum_out=total[:, t, h + i:h + i + 1]))
                            exps[h + i] = bank_read[b + i] = done

                    def turn_probs(h):
                        b, s = 4 + h % 2, h % 4
                        wait(pe, exps[h], bank_read[b])
                        for i in range(3):
                            e = PE(pe.transpose(psum[:, b, i * P:(i + 1) * P], probs[s][:, i * P:(i + 1) * P],
                                                ident[:]))
                        turns[h] = e
                        if h % 2:
                            wait(dve, e, weighed.get(h - 4))
                            e = DVE(dve.tensor_copy(probsT[s][:], psum[:, b, 0:3 * P]))
                        else:
                            wait(act, e, weighed.get(h - 4))
                            e = ACTE(act.activation(probsT[s][:], psum[:, b, 0:3 * P], ACT.Copy))
                        bank_read[b] = moved[h] = e

                    def weigh(h):
                        s, quarter = h % 4, h // PER
                        b, col = 6 + quarter % 2, h % PER * hd
                        j = h * kv_heads // heads
                        wait(pe, moved[h], bank_read[b], v_ready)
                        value = [v[:, t, j * hd:(j + 1) * hd] for t in range(TT)]
                        pe.matmul(psum[:, b, col:col + hd], probsT[s][:, 0:P], value[0], start=True, stop=True)
                        out_1 = psum[:, b, T + col:T + col + hd]
                        pe.matmul(out_1, probsT[s][:, P:2 * P], value[0], start=True, stop=False)
                        weighed[h] = PE(pe.matmul(out_1, probsT[s][:, 2 * P:3 * P], value[1], start=False, stop=True))
                        if h % PER == PER - 1:
                            own = slice(quarter * PER, (quarter + 1) * PER)
                            wait(dve, exps[h])
                            e = DVE(dve.reciprocal(inverse[:, :, own], total[:, :, own]))
                            wait(dve, e, weighed[h])
                            for t in range(TT):
                                e = DVE(dve.tensor_tensor(
                                    o[:, t, quarter * T:(quarter + 1) * T].rearrange("p (h d) -> p h d", d=hd),
                                    psum[:, b, t * T:(t + 1) * T].rearrange("p (h d) -> p h d", d=hd),
                                    inverse[:, t, own].unsqueeze(2).broadcast_to([P, PER, hd]), ALU.mult))
                            bank_read[b] = e
                            quarters.append((quarter, e))

                    def turn_quarter(quarter, event):
                        b = 6 + quarter % 2
                        wait(pe, event)
                        for j in range(2):
                            for t in range(TT):
                                k, c = 2 * quarter + j, (j * TT + t) * P
                                e = PE(pe.transpose(psum[:, b, c:c + P], o[:, t, k * P:k * P + P], ident[:]))
                        ks = slice(2 * quarter, 2 * quarter + 2)
                        _, bank_read[b] = halve(psum[:, b, :].rearrange("p (j n) -> p j n", j=2),
                                                oT_high[:, ks, :], oT_low[:, ks, :], [e])
                        return bank_read[b]

                    quarters, o_ready = [], []
                    for h in range(0, heads + 4, 2):
                        if h < heads:
                            scores(h)
                            scores(h + 1)
                            soften(h)
                        if quarters:
                            o_ready.append(turn_quarter(*quarters.pop(0)))
                        for i in range(2):
                            if 0 <= h - 2 < heads:
                                turn_probs(h - 2 + i)
                            if h >= 4:
                                weigh(h - 4 + i)
                    o_ready.append(turn_quarter(*quarters.pop(0)))
                    linear_split([(oT_high[:, k, :], oT_low[:, k, :], o_ready[k // 2]) for k in range(KT)],
                                 splitter, 2, [0, 1, 2, 3], add_to_x)
                return [x_ready, so_far(pe_done), so_far(act_done), so_far(dve_done)]

        attend_d = Causal("d", 16, 16, 64, 0.125, True)
        done = attend_d.run(a["cos_a"], a["sin_a"], done, splitter)
        split_stack.close()
        if stop <= 2:
            return finish()

        E_, R = 8, 16
        with ExitStack() as phase:
            xn = sb(phase, "xn_e", [P, TT, D])
            xnT = sb(phase, "xnT_e", [P, KT, T])
            rank = sb(phase, "rank", [P, E_])
            chosen = sb(phase, "chosen", [P, TT, 2, E_])
            best = sb(phase, "best", [P, TT, 2])
            hidden = sb(phase, "hidden_e", [P, TT, E_ * R])
            hiddenT = sb(phase, "hiddenT_e", [P, T])
            wait(sp, *done)
            rank_ready = const_in.after(sp.dma_start(rank[:], a["rank"]), 16)
            normed = layernorm(xn, done)
            turned = turn(xn, xnT, normed, [4, 5, 6, 7])
            routed = []

            def route(n, t, product, event):
                top, first = best[:, t, 0:1], best[:, t, 1:2]
                ranks, weights = chosen[:, t, 0, :], chosen[:, t, 1, :]
                wait(dve, event, rank_ready)
                wait(dve, DVE(dve.tensor_reduce(top, product[:, 0:E_], AX_X, ALU.max)))
                wait(dve, DVE(dve.scalar_tensor_tensor(out=ranks, in0=product[:, 0:E_], scalar=top, in1=rank[:],
                                                       op0=ALU.is_equal, op1=ALU.mult)))
                wait(dve, DVE(dve.tensor_reduce(first, ranks, AX_X, ALU.max)))
                wait(dve, DVE(dve.tensor_scalar(weights, ranks, first, top, ALU.is_equal, ALU.mult)))
                e = DVE(dve.tensor_tensor(hidden[:, t, :].rearrange("p (e r) -> p e r", r=R),
                                          product[:, E_:E_ + E_ * R].rearrange("p (e r) -> p e r", r=R),
                                          weights.unsqueeze(2).broadcast_to([P, E_, R]), ALU.mult))
                routed.append(e)
                return e

            linear([xnT[:, k, :] for k in range(KT)], turned, panels, 1, [0, 1], route, width=E_ + E_ * R)
            wait(pe, *routed, bank_read[2])
            for t in range(TT):
                e = PE(pe.transpose(psum[:, 2, t * P:(t + 1) * P], hidden[:, t, :], ident[:]))
            wait(act, e)
            bank_read[2] = ACTE(act.activation(hiddenT[:], psum[:, 2, 0:T], ACT.Copy))
            w, arrived = panels.take()
            wait(pe, bank_read[2], arrived)
            for n in range(2):
                for t in range(TT):
                    b = 4 + 2 * n + t
                    wait(pe, bank_read[b])
                    e = PE(pe.matmul(psum[:, b, :], hiddenT[:, t * P:(t + 1) * P], w.ap(n, BANK), start=True,
                                     stop=True))
                    bank_read[b] = add_to_x(n, t, psum[:, b, :], e)
            panels.release(e)
            done = [x_ready, so_far(pe_done), so_far(act_done)]
        if stop <= 3:
            return finish()

        H1 = KV1 * G1
        NS1 = CTX // P
        NC1 = CTX // BANK
        with ExitStack() as phase:
            q_rows = sb(phase, "q_rows", [3 * HD1 + 2, KV1, G1 * T], F32R)
            k_rows = [sb(phase, f"k_rows{i}", [3 * HD1 + 2, CTX], F32R) for i in range(2)]
            v_all = sb(phase, "v_all", [P, NS1, V1W])
            probs = [sb(phase, f"probs_f{i}", [P, G1 * T]) for i in range(4)]
            odd = sb(phase, "odd_f", [2 * HD1, G1 * T])
            inverse = sb(phase, "inverse_f", [2 * HD1, G1 * T])
            sums = sb(phase, "sums_f", [HD1, BANK])
            few = sb(phase, "few_f", [HD1, BANK // 32])
            top1 = sb(phase, "top1", [P, G1 * TT, NC1])
            neg_top1 = sb(phase, "neg_top1", [P, G1 * TT])
            t_high = sb(phase, "t_high", [G1 * TT, P], F32R)
            t_low = sb(phase, "t_low", [G1 * TT, P], F32R)
            oT_high = sb(phase, "oT_high_f", [P, KV1, T], F32R)
            oT_low = sb(phase, "oT_low_f", [P, KV1, T], F32R)
            k1_in = [signal(f"k1_in{i}") for i in range(2)]
            v1_in = signal("v1_in")
            top_in = signal("top_in")

            def k1_piece(kv):
                rows = slice(kv * HD1, (kv + 1) * HD1)
                return lambda k: [(k[0:HD1, :].bitcast(F32), k1_high[rows, :]),
                                  (k[HD1:2 * HD1, :].bitcast(F32), k1_high[rows, :]),
                                  (k[2 * HD1:3 * HD1, :].bitcast(F32), k1_low[rows, :])]

            wait(pool, *done)
            for k in k_rows:
                wait(pool, so_far(pool_done))
                ones_set = POOL(pool.memset(k[3 * HD1:3 * HD1 + 2, :].bitcast(F32), 1.0))
            keys = Feed(sp, wait, k_rows, k1_in, [k1_piece(kv) for kv in range(KV1)], first=[*done, *kv_spilled])
            v1_ready = v1_in.after(sp.dma_start(v_all[:], v1_dram), 16)

            xn_parts = [probs[0], probs[1]]
            wait(dve, stats_ready, *done)
            for t in range(TT):
                e = DVE(dve.bn_aggr(moments[:, t, :], stats[:, t].rearrange("p h s -> p (h s)")))
            r, e = inverse_root(moments[:, :, 1], 1e-5, e)
            wait(dve, e)
            for t in range(TT):
                e = DVE(dve.tensor_scalar(xn_parts[t][:], x[:, t, :], moments[:, t, 0:1], r[:, t:t + 1],
                                          ALU.subtract, ALU.mult))
            wait(pe, e)
            xnT_parts = [probs[2], probs[3]]
            turned = []
            for i in range(KT // 2):
                b = 4 + i
                wait(pe, bank_read[b])
                for j in range(2):
                    for t in range(TT):
                        c = (j * TT + t) * P
                        k = 2 * i + j
                        e = PE(pe.transpose(psum[:, b, c:c + P], xn_parts[t][:, k * P:(k + 1) * P], ident[:]))
                wait(act, e)
                bank_read[b] = ACTE(act.activation(xnT_parts[i // 2][:, i % 2 * 2 * T:(i % 2 + 1) * 2 * T],
                                                   psum[:, b, :], ACT.Copy))
            wait(pe, bank_read[7])
            max_jobs, q1_ready = {}, {}

            def maxima(kv, m):
                rows, chunk = divmod(m, NC1)
                k, arrived = max_jobs[kv]
                b = 6 + m % 2
                wait(pe, arrived, bank_read[b], *q1_ready[kv])
                e = PE(pe.matmul(psum[:, b, :], q_rows[0:3 * HD1, kv, rows * P:(rows + 1) * P],
                                 k[0:3 * HD1, chunk * BANK:(chunk + 1) * BANK], start=True, stop=True))
                wait(dve, e)
                bank_read[b] = DVE(dve.tensor_reduce(top1[:, rows, chunk:chunk + 1], psum[:, b, :], AX_X, ALU.max))

            tops_read = {}

            def place_maxima(kv):
                wait(dve, bank_read[6], bank_read[7], tops_read.get("pe"))
                tops_read["dve"] = DVE(dve.tensor_reduce(neg_top1[:], top1[:], AX_X, ALU.max, negate=True))

            def place_rows(kv):
                wait(pe, tops_read["dve"], bank_read[6])
                e = PE(pe.transpose(psum[0:G1 * TT, 6, 0:P], neg_top1[:], ident[:]))
                tops_read["pe"] = e
                wait(act, e, tops_read.get("dma"))
                e = ACTE(act.activation(t_high[:], psum[0:G1 * TT, 6, 0:P], ACT.Copy))
                wait(dve, e, tops_read.get("dma"))
                bank_read[6] = DVE(dve.tensor_tensor(t_low[:], psum[0:G1 * TT, 6, 0:P], t_high[:].bitcast(F32),
                                                     ALU.subtract))
                wait(sp, e, bank_read[6])
                for r, top in ((0, t_high), (1, t_low)):
                    row = 3 * HD1 + r
                    e = top_in.after(sp.dma_start(
                        q_rows[row:row + 1, kv, :].bitcast(F32).rearrange("o (r n) -> o r n", n=P),
                        top[:].bitcast(F32)), 16)
                tops_read["dma"] = e
                return e

            max_jobs[0] = keys.take()
            beside = list(range(G1 * TT * NC1))
            for n in range(2):
                both = [panels.take() for _ in range(2)]
                wait(pe, *(arrived for _, arrived in both))
                for c in range(4):
                    b, kv = c, 4 * n + c
                    wait(pe, bank_read[b])
                    for k in range(KT):
                        if kv > 0 and beside:
                            maxima(0, beside.pop(0))
                        mm = pe.matmul(psum[:, b, 0:T], both[k // 4][0].ap(k % 4, BANK)[:, c * P:(c + 1) * P],
                                       xnT_parts[k // 4][:, k % 4 * T:(k % 4 + 1) * T], start=k == 0, stop=k == KT - 1)
                    e = PE(mm)
                    for g in range(G1):
                        src = psum[g * HD1:(g + 1) * HD1, b, 0:T]
                        cols = slice(g * T, (g + 1) * T)
                        wait(act, e)
                        high = q_rows[0:HD1, kv, cols]
                        e_high = ACTE(act.activation(high, src, ACT.Copy))
                        wait(dve, e_high)
                        bank_read[b] = DVE(dve.tensor_tensor(q_rows[HD1:2 * HD1, kv, cols], src,
                                                             high.bitcast(F32), ALU.subtract))
                    wait(pool, e_high, so_far(pool_done))
                    copied = POOL(pool.tensor_copy(q_rows[2 * HD1:3 * HD1, kv, :], q_rows[0:HD1, kv, :]))
                    q1_ready[kv] = (bank_read[b], copied)
                for _ in both:
                    panels.release(e)
            q1_read = e

            scale = float(HD1 ** -0.5)
            for m in beside:
                maxima(0, m)
            place_maxima(0)
            placed = {0: place_rows(0)}
            exp_done, pv_done = {}, {}
            tiles = [(kv, s) for kv in range(KV1) for s in range(NS1)]

            def scores1(n):
                kv, s = tiles[n]
                k, arrived = max_jobs[kv]
                wait(pe, arrived, placed[kv], *q1_ready[kv], ones_set)
                for half in range(2):
                    b = 2 * (n % 2) + half
                    wait(pe, bank_read[b])
                    e = PE(pe.matmul(psum[:, b, :], k[:, s * P:(s + 1) * P],
                                     q_rows[:, kv, half * BANK:(half + 1) * BANK], start=True, stop=True))
                wait(act, e, pv_done.get(n - 4), q1_read)
                exp_done[n] = ACTE(act.activation(
                    probs[n % 4][:], psum[:, 2 * (n % 2):2 * (n % 2) + 2, :].rearrange("p b n -> p (b n)"),
                    ACT.Exp, scale=scale))
                bank_read[2 * (n % 2)] = bank_read[2 * (n % 2) + 1] = exp_done[n]

            weighed_kv, outputs_split = [None, None], {}

            def weigh1(n, half):
                kv, s = tiles[n]
                wait(pe, exp_done[n], exp_done[n + 1], bank_read[4], bank_read[5], v1_ready, ones_set)
                for i in range(2):
                    col = kv // 2 * 3 * HD1 + kv % 2 * HD1
                    mm = pe.matmul(psum[i * 64:(i + 1) * 64, 4 + half, :], v_all[:, s + i, col:col + 2 * HD1],
                                   probs[(n + i) % 4][:, half * BANK:(half + 1) * BANK],
                                   start=s == 0, stop=s == NS1 - 2)
                pv_done[n] = pv_done[n + 1] = e = PE(mm)
                if s == NS1 - 2:
                    cols = slice(half * BANK, (half + 1) * BANK)
                    vr = slice(kv % 2 * HD1, kv % 2 * HD1 + HD1)
                    sr = slice(HD1 - kv % 2 * HD1, 2 * HD1 - kv % 2 * HD1)
                    wait(act, e, weighed_kv[half])
                    e = ACTE(act.activation(odd[:, cols], psum[64:128, 4 + half, :], ACT.Copy))
                    wait(dve, e)
                    e = DVE(dve.tensor_tensor(odd[:, cols], psum[0:64, 4 + half, :], odd[:, cols], ALU.add))
                    bank_read[4 + half] = e
                    later.append((kv, half, cols, vr, sr, e))

            later, unsplit, rounded_outputs = [], [], []

            def normalise1():
                kv, half, cols, vr, sr, e = later.pop(0)
                wait(dve, so_far(dve_done))
                _, e = invert_row(odd[sr, cols], inverse[vr, cols], sums[:], few[:], e)
                wait(dve, e)
                for g in (2 * half, 2 * half + 1):
                    c = slice(g * T, (g + 1) * T)
                    e = DVE(dve.tensor_tensor(inverse[vr, c], odd[vr, c], inverse[vr, c], ALU.mult))
                    unsplit.append((kv, half, g, vr, c, e))

            def split1():
                while rounded_outputs:
                    kv, half, rows, src, e = rounded_outputs.pop(0)
                    wait(dve, e)
                    weighed_kv[half] = outputs_split[kv] = DVE(dve.tensor_tensor(
                        oT_low[rows, kv, :], src, oT_high[rows, kv, :].bitcast(F32), ALU.subtract))
                while unsplit:
                    kv, half, g, vr, c, e = unsplit.pop(0)
                    rows = slice(g * HD1, (g + 1) * HD1)
                    wait(act, e)
                    e = ACTE(act.activation(oT_high[rows, kv, :], inverse[vr, c], ACT.Copy))
                    rounded_outputs.append((kv, half, rows, inverse[vr, c], e))

            splitter = Splitter(split_tiles(split_stack, "panel_fg", 2), panels, 4 + 10)
            ahead_from = len(tiles) - NS1 // 2
            scores1(0)
            scores1(1)
            jobs = G1 * TT * NC1
            first_pair, last_pair = 2, NS1 // 2 - 4
            count = last_pair - first_pair + 1
            for n in range(0, len(tiles), 2):
                kv, s = tiles[n]
                pair = s // 2
                ahead = kv + 1 < KV1
                if s == 0 and ahead:
                    max_jobs[kv + 1] = keys.take()
                beside = [m for m in range(jobs) if ahead and first_pair + m * count // jobs == pair]
                steps = [lambda n=n: scores1(n + 2), lambda n=n: scores1(n + 3)] if n + 2 < len(tiles) else []
                steps += [lambda n=n: weigh1(n, 0), lambda n=n: weigh1(n, 1)]
                for i, step in enumerate(steps):
                    for m in beside[i * len(beside) // 4:(i + 1) * len(beside) // 4]:
                        maxima(kv + 1, m)
                    step()
                    if i == 2 and ahead and pair == last_pair + 1:
                        placed[kv + 1] = place_rows(kv + 1)
                if ahead and pair == last_pair:
                    place_maxima(kv + 1)
                split1()
                if later and s != NS1 - 2:
                    normalise1()
                if n >= ahead_from:
                    splitter.ahead()
                if s == NS1 - 2:
                    keys.release(pv_done[n])
            while later:
                normalise1()
                split1()
            split1()
            linear_split([(oT_high[:, kv, :], oT_low[:, kv, :], outputs_split[kv]) for kv in range(KV1)],
                         splitter, 2, [0, 1, 2, 3], add_to_x)
            done = [x_ready, so_far(pe_done), so_far(act_done), so_far(dve_done)]
        if stop <= 4:
            return finish()

        gate_up = [sb(ctx, f"gate_up{i}", [P, 2, 4 * KT * P], BF16) for i in range(2)]
        gain = sb(ctx, "gain", [P, D])
        ws_g = sb(ctx, "ws_g", [P, FF])
        ws_u = sb(ctx, "ws_u", [P, FF])
        ws_d = sb(ctx, "ws_d", [P, D])
        ws_turned = sb(ctx, "ws_turned", [NQ, P])
        gu_in = [signal(f"gu_in{i}") for i in range(2)]
        down_in, ws_sent, ws_in = signal("down_in"), signal("ws_sent"), signal("ws_in")
        def chunk_piece(c):
            n = min(4, FT - 4 * c)

            def dmas(tile):
                pairs = []
                for which in range(2):
                    at = which * FT + 4 * c
                    whole = n if 4 * c + n < FT else n - 1
                    pairs.append((tile[:, which, 0:whole * KT * P].rearrange("p (i m) -> p i m", i=whole),
                                  q_dram[at:at + whole].rearrange("i p m -> p i m")))
                    if whole < n:
                        rest = FF % P
                        view = lambda z: z.rearrange("p (k n) -> p k n", n=P)[:, :, 0:rest]
                        pairs.append((view(tile[:, which, whole * KT * P:n * KT * P]), view(q_dram[at + whole])))
                return pairs
            return dmas

        chunks = -(-FT // 4)
        def load_ahead(done):
            nonlocal gain_ready, ring, ws_ready
            wait(sp, *done)
            gain_ready = const_in.after(sp.dma_start(gain[:], a["rms_weight"].partition_broadcast(P)), 16)
            wait(pe, *done, bank_read[7])
            e = PE(pe.transpose(psum[0:NQ, 7, 0:P], w_scale[:], ident[:]))
            wait(act, e, *done)
            bank_read[7] = ACTE(act.activation(ws_turned[:], psum[0:NQ, 7, 0:P], ACT.Copy))
            wait(sp, bank_read[7])
            scales_sent = ws_sent.after(sp.dma_start(ws_dram, ws_turned[:]), 16)

            ring = Feed(sp, wait, gate_up, gu_in, [chunk_piece(c) for c in range(chunks)], first=[*done, *q_all_spilled])
            wait(sp, scales_sent)
            flat = ws_dram.rearrange("r n -> (r n)")
            ws_in.after(sp.dma_start(ws_g[:], flat[0:FF].partition_broadcast(P)), 16)
            ws_in.after(sp.dma_start(ws_u[:], flat[FT * P:FT * P + FF].partition_broadcast(P)), 16)
            ws_ready = ws_in.after(sp.dma_start(ws_d[:], flat[2 * FT * P:NQ * P].partition_broadcast(P)), 16)

        gain_ready = ring = ws_ready = None
        attend_g = Causal("g", 32, 8, 32, float(1.0 / np.sqrt(np.float32(32.0))), False)
        splitter.grow(split_tiles(split_stack, "panel_g", 1))
        wait(act, *done)
        done = attend_g.run(a["cos_b"], a["sin_b"], done, splitter, load_ahead)
        split_stack.close()
        if stop <= 5:
            return finish()

        panel_stack.close()
        with ExitStack() as phase:
            xn = sb(phase, "xn_h", [P, TT, D])
            ints = sb(phase, "ints_h", [P, TT, D], BF16)
            intsT = sb(phase, "intsT_h", [P, KT, T], BF16)
            act_scale = sb(phase, "act_scale", [P, 8, TT])
            down = sb(phase, "down", [P, KT, FT * P], BF16)
            g_part = [sb(phase, f"g_part{i}", [P, BANK]) for i in range(2)]
            u_part = [sb(phase, f"u_part{i}", [P, BANK]) for i in range(2)]
            hid = sb(phase, "hid", [P, TT, FF])
            hid_top = sb(phase, "hid_top", [P, TT, chunks])
            hid_i = [sb(phase, f"hid_i{t}", [P, FF], BF16) for t in range(TT)]
            hid_T = [sb(phase, f"hid_T{t}", [P, FT * P], BF16) for t in range(TT)]
            whole = FF // P * P
            wait(sp, *done)
            down_in.after(sp.dma_start(down[:, :, 0:whole], qd_dram[:, :, 0:whole].rearrange("k p m -> p k m")), 16)
            down_ready = down_in.after(sp.dma_start(
                down[0:FF - whole, :, whole:], qd_dram[:, 0:FF - whole, whole:].rearrange("k p m -> p k m")), 16)

            wait(dve, stats_ready, *done)
            for t in range(TT):
                e = DVE(dve.bn_aggr(moments[:, t, :], stats[:, t].rearrange("p h s -> p (h s)")))
            largest = act_scale[:, 0, :]

            def centre():
                wait(dve, gain_ready)
                for t in range(TT):
                    e = DVE(dve.scalar_tensor_tensor(out=xn[:, t, :], in0=x[:, t, :], scalar=moments[:, t, 0:1],
                                                     in1=gain[:], op0=ALU.subtract, op1=ALU.mult))
                    wait(dve, e)
                    e = DVE(dve.tensor_reduce(largest[:, t:t + 1], xn[:, t, :], AX_X, ALU.max,
                                              apply_absolute_value=True))
                wait(dve, e)

            root, e = inverse_root(moments[:, :, 1], 1e-5 * 1e-6, e, 1.0 + 1e-6, centre)
            x_scale, x_factor, inverse = (act_scale[:, i, :] for i in (1, 2, 3))
            wait(dve, e)
            wait(dve, DVE(dve.tensor_tensor(largest, largest, root, ALU.mult)))
            wait(dve, DVE(dve.tensor_scalar(x_scale, largest, 1.0 / QMAX, 1e-8, ALU.mult, ALU.max)))
            wait(dve, DVE(dve.reciprocal(inverse, x_scale)))
            wait(dve, DVE(dve.tensor_tensor(x_factor, inverse, root, ALU.mult)))
            ints_turned = []
            for t in range(TT):
                e = DVE(dve.tensor_scalar(xn[:, t, :], xn[:, t, :], x_factor[:, t:t + 1], ROUND, ALU.mult, ALU.add))
                wait(act, e, *done)
                e = ACTE(act.activation(ints[:, t, :], xn[:, t, :], ACT.Copy, bias=-ROUND))
                b = 1 + t
                bank = psum[:, b, :].bitcast(BF16)
                wait(pe, e, bank_read[b])
                for k in range(KT):
                    e = PE(pe.transpose(bank[:, k * P:(k + 1) * P], ints[:, t, k * P:(k + 1) * P], ident_b[:]))
                wait(act, e)
                bank_read[b] = ACTE(act.activation(intsT[:, :, t * P:(t + 1) * P],
                                                   bank.rearrange("p (k n) -> p k n", n=P), ACT.Copy))
                ints_turned.append(bank_read[b])

            jobs = [(c, t) for c in range(chunks - 2) for t in range(TT)]
            jobs += [(c, t) for t in range(TT) for c in (chunks - 2, chunks - 1)]
            taken, mixed = {}, {}

            def gate_and_up(job):
                c, t = jobs[job]
                if c not in taken:
                    taken[c] = ring.take()
                w, arrived = taken[c]
                n_tiles = min(4, FT - 4 * c)
                width = min(BANK, FF - c * BANK)
                bg, bu = 2 * (job % 4), 2 * (job % 4) + 1
                wait(pe, arrived, ints_turned[t], bank_read[bg], bank_read[bu])
                parts = [(0, width)] if width == BANK else [(i * P, min(P, width - i * P)) for i in range(n_tiles)]
                for which, b in ((0, bg), (1, bu)):
                    grid = w[:, which, :].rearrange("p (i k n) -> p i k n", k=KT, n=P)
                    for first, count in parts:
                        for k in range(KT):
                            moving = grid[:, :, k, :] if width == BANK else grid[:, first // P, k, 0:count]
                            mm = pe.matmul(psum[:, b, first:first + count], intsT[:, k, t * P:(t + 1) * P],
                                           moving, start=k == 0, stop=k == KT - 1)
                    if which == 0:
                        gate_done = PE(mm)
                up_done = PE(mm)
                if t == TT - 1:
                    ring.release(up_done)
                at = slice(c * BANK, c * BANK + width)
                i = job % 2
                gate, up = g_part[i][:, 0:width], u_part[i][:, 0:width]
                sc = x_scale[:, t:t + 1]
                wait(dve, gate_done, ws_ready)
                e = DVE(dve.scalar_tensor_tensor(out=gate, in0=psum[:, bg, 0:width], scalar=sc, in1=ws_g[:, at],
                                                 op0=ALU.mult, op1=ALU.mult))
                bank_read[bg] = e
                wait(act, e)
                e = ACTE(act.activation(gate, gate, ACT.Silu))
                wait(dve, up_done)
                bank_read[bu] = DVE(dve.scalar_tensor_tensor(out=up, in0=psum[:, bu, 0:width], scalar=sc,
                                                             in1=ws_u[:, at], op0=ALU.mult, op1=ALU.mult))
                wait(dve, e, bank_read[bu])
                e = DVE(dve.tensor_tensor(hid[:, t, at], gate, up, ALU.mult))
                wait(dve, e)
                mixed[t] = DVE(dve.tensor_reduce(hid_top[:, t, c:c + 1], hid[:, t, at], AX_X, ALU.max,
                                                 apply_absolute_value=True))

            hid_ready = {}

            def quantise_hidden(t):
                top, sc, inv = (act_scale[:, i, t:t + 1] for i in (4, 5, 6))
                wait(dve, mixed[t])
                wait(dve, DVE(dve.tensor_reduce(top, hid_top[:, t, :], AX_X, ALU.max)))
                wait(dve, DVE(dve.tensor_scalar(sc, top, 1.0 / QMAX, 1e-8, ALU.mult, ALU.max)))
                wait(dve, DVE(dve.reciprocal(inv, sc)))
                for first in range(0, FT, 8):
                    at = slice(first * P, min(FF, (first + 8) * P))
                    e = DVE(dve.tensor_scalar(hid[:, t, at], hid[:, t, at], inv, ROUND, ALU.mult, ALU.add))
                    wait(act, e)
                    hid_ready[t, first] = ACTE(act.activation(hid_i[t][:, at], hid[:, t, at], ACT.Copy, bias=-ROUND))

            hid_turned, out_sent = {}, []

            def turn_hidden(t):
                for first in range(0, FT, 8):
                    b = first // 8 + 4 * t
                    some = range(first, min(first + 8, FT))
                    bank = psum[:, b, :].bitcast(BF16).rearrange("p (k n) -> p k n", n=P)
                    wait(pe, hid_ready[t, first], bank_read[b])
                    for k in some:
                        rows = min(P, FF - k * P)
                        e = PE(pe.transpose(bank[0:rows, k - first, :], hid_i[t][:, k * P:k * P + rows], ident_b[:]))
                    wait(dve, e)
                    full = [k for k in some if FF - k * P >= P]
                    for height, k0, count in [(P, full[0], len(full))] + (
                            [(FF % P, some[-1], 1)] if len(full) < len(some) else []):
                        bank_read[b] = hid_turned[t, first] = DVE(dve.tensor_copy(
                            hid_T[t][0:height, k0 * P:(k0 + count) * P].rearrange("p (k n) -> p k n", n=P),
                            bank[0:height, k0 - first:k0 - first + count, :]))

            def project(t):
                nonlocal x_ready
                wait(pe, down_ready)
                for n in range(2):
                    b = 3 + 4 * n
                    wait(pe, bank_read[b])
                    for k in range(FT):
                        wait(pe, hid_turned[t, k // 8 * 8])
                        rows = min(P, FF - k * P)
                        mm = pe.matmul(psum[:, b, :], hid_T[t][0:rows, k * P:(k + 1) * P],
                                       down[0:rows, 4 * n:4 * n + 4, k * P:(k + 1) * P], start=k == 0, stop=k == FT - 1)
                    e = PE(mm)
                    wait(dve, e)
                    at = slice(n * BANK, (n + 1) * BANK)
                    e = DVE(dve.scalar_tensor_tensor(out=xn[:, t, at], in0=psum[:, b, :],
                                                     scalar=act_scale[:, 5, t:t + 1], in1=ws_d[:, at],
                                                     op0=ALU.mult, op1=ALU.mult))
                    bank_read[b] = e
                    wait(dve, e)
                    x_ready = DVE(dve.tensor_tensor(x[:, t, at], xn[:, t, at], x[:, t, at], ALU.add))
                    wait(sp, x_ready)
                    out_sent.append(out_done.after(sp.dma_start(out[0, t * P:(t + 1) * P, at], x[:, t, at]), 16))

            for job, (c, t) in enumerate(jobs):
                gate_and_up(job)
                if c == chunks - 1 and t == 0:
                    quantise_hidden(0)
            turn_hidden(0)
            quantise_hidden(1)
            project(0)
            turn_hidden(1)
            project(1)
            wait(sp, out_sent[-1])


def program(nc, a, out, stop=99):
    build(nc, a, out, stop)


def layouts(i):
    c = np.ascontiguousarray
    P_, KT = 128, 8

    def tiled(w, width):
        k, n = w.shape
        return c(w.reshape(k // P_, P_, n // width, width).transpose(2, 1, 0, 3).reshape(n // width, P_, -1))

    a = {"x": i["x"], "ident": np.eye(P_, dtype=np.float32)}
    a["wq0"] = tiled(i["L0_xattn_Wq"].T, 96)
    k0, k1 = i["L0_xattn_Wk"].T.reshape(1024, 4, 96), i["L1_xattn_Wk"].reshape(1024, 8, 32)
    packed = np.concatenate([k0, k1[:, :4]], axis=2).reshape(1024, 512)
    wkv = np.concatenate([packed, k1[:, 4:].reshape(1024, 128), i["L0_xattn_Wv"].T, i["L1_xattn_Wv"]], axis=1)
    a["wkv"] = c(wkv.reshape(KT, P_, 1280))
    ctx = i["ctx_4096"][0].reshape(16, 256, KT, P_)
    a["ctxT"] = c(ctx.transpose(0, 3, 2, 1).reshape(16, P_, KT * 256))
    wo0 = i["L0_xattn_Wo"].T.reshape(16, 96, 2, 512)
    a["wo0"] = c(wo0.transpose(2, 1, 0, 3).reshape(2, 96, 16 * 512))
    for name, w in (("wq_a", i["L0_attn_w_q"].T), ("wk_a", i["L0_attn_w_k"].T), ("wv_a", i["L0_attn_w_v"].T),
                    ("wo_a", i["L0_attn_w_out"].T), ("wq1", i["L1_xattn_Wq"]), ("wo1", i["L1_xattn_Wo"]),
                    ("wq_b", i["L1_attn_Wq"]), ("wo_b", i["L1_attn_Wo"])):
        a[name] = tiled(w, 512)
    a["wkv_b"] = tiled(np.concatenate([i["L1_attn_Wk"], i["L1_attn_Wv"]], axis=1), 512)[0]
    a["route"] = tiled(np.concatenate([i["L0_ffn_route_w"], i["L0_ffn_A"].reshape(128, 1024)], axis=0).T, 136)[0]
    f = np.float32
    freq = f(1.0) / f(10000.0) ** (np.arange(0, 64, 2, dtype=f) / f(64))
    angles = np.repeat(np.arange(256, dtype=f)[:, None] * freq[None, :], 2, axis=1).reshape(2, P_, 64)
    a["cos_a"], a["sin_a"] = (c(g(angles).transpose(1, 0, 2)) for g in (np.cos, np.sin))
    a["cos_b"], a["sin_b"] = (c(i[n][:256].reshape(2, P_, 32).transpose(1, 0, 2))
                              for n in ("L1_attn_cos", "L1_attn_sin"))
    q = np.arange(P_)[:, None]
    keys = np.arange(2 * P_)[None, :]
    a["mask"] = np.where(np.concatenate([keys[:, :P_] <= q, keys <= q + P_], axis=1), f(0), f(-1e30)).astype(f)
    a["rank"] = np.tile(np.arange(8, 0, -1, dtype=f), (P_, 1))
    a["rms_weight"] = i["L1_ffn_rmsnorm_weight"]
    a["ffn_w0"], a["ffn_w1"], a["ffn_w2"] = i["L1_ffn_Wg"], i["L1_ffn_Wu"], i["L1_ffn_Wd"]
    a["lora_b"] = c(i["L0_ffn_Bw"].transpose(0, 2, 1).reshape(128, 1024))
    return a


def kernel(**inputs):
    from concourse import bacc
    from concourse.bass_utils import run_bass_kernel_spmd

    arrays = {f"in_{n}_dram": np.ascontiguousarray(v)
              for n, v in layouts({n: np.asarray(v) for n, v in inputs.items()}).items()}
    nc = bacc.Bacc("TRN2", target_bir_lowering=False, num_devices=1)
    a = {n[3:-5]: nc.dram_tensor(n, v.shape, mybir.dt.from_np(v.dtype), kind="ExternalInput").ap()
         for n, v in arrays.items()}
    out = nc.dram_tensor("out_0_dram", (1, 256, 1024), F32, kind="ExternalOutput").ap()
    program(nc, a, out)
    result = run_bass_kernel_spmd(nc, [arrays], core_ids=[0])
    return result.results[0]["out_0_dram"]
```
